# Optimizing a Trainium2 kernel written in Bass

```python
import numpy as np
import jax
import jax.numpy as jnp

def _softmax(x, axis=-1):
    return jax.nn.softmax(x, axis=axis)

def _gelu(x):
    return jax.nn.gelu(x, approximate=True)

def _silu(x):
    return jax.nn.silu(x)

def _sigmoid(x):
    return jax.nn.sigmoid(x)

def _layernorm(x, axis=-1, eps=1e-05):
    m = jnp.mean(x, axis=axis, keepdims=True)
    v = jnp.var(x, axis=axis, keepdims=True)
    return (x - m) / jnp.sqrt(v + eps)

def _scatter_add(tgt, idx, src, axis=0):
    return tgt.at[idx].add(src)

def _segment_sum(src, seg, n):
    return jax.ops.segment_sum(src, seg, n)
kernel_name = 'mk_adaln_d1_jaxref_r8_e79170'

def setup_inputs(seed: int=0):
    np.random.seed(seed)
    _w = jnp.asarray

    def _L0_attn_setup():
        import jax, jax.numpy as jnp
        import numpy as np
        from jax import lax
        NUM_LEVELS = 2
        NUM_HEADS = 16
        LN_EPS = 1e-05
        ATTN_EPS = 1e-06

        def dwconv(x, filt):
            C = x.shape[-1]
            return lax.conv_general_dilated(x, filt[:, None, :], window_strides=(1,), padding='SAME', dimension_numbers=('NWC', 'WIO', 'NWC'), feature_group_count=C)

        def linear_attention(x, num_heads):
            B, N, C = x.shape
            d = C // num_heads
            h = x.reshape(B, N, num_heads, d)
            q = jax.nn.elu(h) + 1.0
            k = q
            v = h
            kv = jnp.einsum('bnhd,bnhe->bhde', k, v)
            z = k.sum(axis=1)
            num = jnp.einsum('bnhd,bhde->bnhe', q, kv)
            den = jnp.einsum('bnhd,bhd->bnh', q, z)[..., None] + ATTN_EPS
            return (num / den).reshape(B, N, C)

        def layer_norm(x, gamma, beta):
            mu = jnp.mean(x, axis=-1, keepdims=True)
            var = jnp.mean(jnp.square(x - mu), axis=-1, keepdims=True)
            return (x - mu) * lax.rsqrt(var + LN_EPS) * gamma + beta
        key = jax.random.key(seed)
        ks = jax.random.split(key, 7)
        B, S, C, K = (8, 512, 128, 4)
        x = jax.random.normal(ks[0], (B, S, C), dtype=jnp.float32)
        scale = 1.0 / np.sqrt(K)
        h_filter = jax.random.normal(ks[1], (K, C), dtype=jnp.float32) * scale
        g_filter = jax.random.normal(ks[2], (K, C), dtype=jnp.float32) * scale
        h_synth = jax.random.normal(ks[3], (K, C), dtype=jnp.float32) * scale
        g_synth = jax.random.normal(ks[4], (K, C), dtype=jnp.float32) * scale
        norm_gamma = jnp.ones((C,), dtype=jnp.float32)
        norm_beta = jnp.zeros((C,), dtype=jnp.float32)
        return {'x': x, 'h_filter': h_filter, 'g_filter': g_filter, 'h_synth': h_synth, 'g_synth': g_synth, 'norm_gamma': norm_gamma, 'norm_beta': norm_beta}
    _L0_attn_in = _L0_attn_setup()

    def _L0_ffn_setup():
        import jax, jax.numpy as jnp
        import numpy as np
        L, H, NH, NKV, HD, FF, E, K = (4, 128, 16, 4, 64, 256, 8, 2)
        B, S = (2, 256)
        THETA, EPS = (10000.0, 1e-05)

        def _rms(x, w):
            return x * jax.lax.rsqrt(jnp.mean(x * x, axis=-1, keepdims=True) + EPS) * w

        def _rope_cos_sin(seq_len, head_dim, theta):
            inv = 1.0 / theta ** (jnp.arange(0, head_dim, 2, dtype=jnp.float32) / head_dim)
            f = jnp.arange(seq_len, dtype=jnp.float32)[:, None] * inv
            emb = jnp.concatenate([f, f], axis=-1)
            return (jnp.cos(emb), jnp.sin(emb))

        def _rot_half(x):
            h = x.shape[-1] // 2
            return jnp.concatenate([-x[..., h:], x[..., :h]], axis=-1)

        def _attention(x, wq, wk, wv, wo, cos, sin, causal_bias):
            b, s, _ = x.shape
            q = (x @ wq).reshape(b, s, NH, HD).transpose(0, 2, 1, 3)
            k = (x @ wk).reshape(b, s, NKV, HD).transpose(0, 2, 1, 3)
            v = (x @ wv).reshape(b, s, NKV, HD).transpose(0, 2, 1, 3)
            c = cos[None, None]
            sn = sin[None, None]
            q = q * c + _rot_half(q) * sn
            k = k * c + _rot_half(k) * sn
            rep = NH // NKV
            k = jnp.repeat(k, rep, axis=1)
            v = jnp.repeat(v, rep, axis=1)
            scores = jnp.einsum('bhqd,bhkd->bhqk', q, k) / jnp.sqrt(jnp.asarray(HD, x.dtype))
            scores = scores + causal_bias
            attn = jax.nn.softmax(scores, axis=-1)
            out = jnp.einsum('bhqk,bhkd->bhqd', attn, v)
            out = out.transpose(0, 2, 1, 3).reshape(b, s, NH * HD)
            return out @ wo

        def _moe(x, wr, wg, wu, wd):
            logits = x @ wr
            probs = jax.nn.softmax(logits, axis=-1)
            topv, topi = jax.lax.top_k(probs, K)
            topv = topv / jnp.sum(topv, axis=-1, keepdims=True)
            comb = jnp.sum(jax.nn.one_hot(topi, E, dtype=x.dtype) * topv[..., None], axis=-2)
            out = jnp.zeros_like(x)
            for e in range(E):
                h = jax.nn.silu(x @ wg[e]) * (x @ wu[e])
                out = out + comb[..., e:e + 1] * (h @ wd[e])
            return out
        key = jax.random.key(seed)
        ks = jax.random.split(key, 12)
        sc = 0.02
        inp = {'hidden_states': jax.random.normal(ks[0], (B, S, H), jnp.float32), 'ln1_w': jnp.ones((L, H), jnp.float32), 'ln2_w': jnp.ones((L, H), jnp.float32), 'wq': jax.random.normal(ks[1], (L, H, NH * HD), jnp.float32) * sc, 'wk': jax.random.normal(ks[2], (L, H, NKV * HD), jnp.float32) * sc, 'wv': jax.random.normal(ks[3], (L, H, NKV * HD), jnp.float32) * sc, 'wo': jax.random.normal(ks[4], (L, NH * HD, H), jnp.float32) * sc, 'wr': jax.random.normal(ks[5], (L, H, E), jnp.float32) * sc, 'wg': jax.random.normal(ks[6], (L, E, H, FF), jnp.float32) * sc, 'wu': jax.random.normal(ks[7], (L, E, H, FF), jnp.float32) * sc, 'wd': jax.random.normal(ks[8], (L, E, FF, H), jnp.float32) * sc}
        return inp
    _L0_ffn_in = _L0_ffn_setup()
    _L0_c = _w((lambda *s: np.random.randn(*s).astype(np.float32) * 0.05)(16, 128))
    _L0_wmod = _w((lambda *s: np.random.randn(*s).astype(np.float32) * 0.05)(128, 6 * 128) * 128 ** (-0.5))
    _d = {'L0_attn_x': _L0_attn_in['x'], 'L0_attn_h_filter': _L0_attn_in['h_filter'], 'L0_attn_g_filter': _L0_attn_in['g_filter'], 'L0_attn_h_synth': _L0_attn_in['h_synth'], 'L0_attn_g_synth': _L0_attn_in['g_synth'], 'L0_attn_norm_gamma': _L0_attn_in['norm_gamma'], 'L0_attn_norm_beta': _L0_attn_in['norm_beta'], 'L0_ffn_ln1_w': _L0_ffn_in['ln1_w'], 'L0_ffn_ln2_w': _L0_ffn_in['ln2_w'], 'L0_ffn_wq': _L0_ffn_in['wq'], 'L0_ffn_wk': _L0_ffn_in['wk'], 'L0_ffn_wv': _L0_ffn_in['wv'], 'L0_ffn_wo': _L0_ffn_in['wo'], 'L0_ffn_wr': _L0_ffn_in['wr'], 'L0_ffn_wg': _L0_ffn_in['wg'], 'L0_ffn_wu': _L0_ffn_in['wu'], 'L0_ffn_wd': _L0_ffn_in['wd'], 'L0_c': _L0_c, 'L0_wmod': _L0_wmod}
    _x0 = _d['L0_attn_x']
    _d['L0_attn_x'] = jax.random.normal(jax.random.fold_in(jax.random.key(seed), 1), (16, 256, 128), dtype=_x0.dtype)
    del _x0
    return _d

def reference(L0_attn_x, L0_attn_h_filter, L0_attn_g_filter, L0_attn_h_synth, L0_attn_g_synth, L0_attn_norm_gamma, L0_attn_norm_beta, L0_ffn_ln1_w, L0_ffn_ln2_w, L0_ffn_wq, L0_ffn_wk, L0_ffn_wv, L0_ffn_wo, L0_ffn_wr, L0_ffn_wg, L0_ffn_wu, L0_ffn_wd, L0_c, L0_wmod):

    def _L0_attn_ref(x, h_filter, g_filter, h_synth, g_synth, norm_gamma, norm_beta):
        import jax, jax.numpy as jnp
        import numpy as np
        from jax import lax
        NUM_LEVELS = 2
        NUM_HEADS = 16
        LN_EPS = 1e-05
        ATTN_EPS = 1e-06

        def dwconv(x, filt):
            C = x.shape[-1]
            return lax.conv_general_dilated(x, filt[:, None, :], window_strides=(1,), padding='SAME', dimension_numbers=('NWC', 'WIO', 'NWC'), feature_group_count=C)

        def linear_attention(x, num_heads):
            B, N, C = x.shape
            d = C // num_heads
            h = x.reshape(B, N, num_heads, d)
            q = jax.nn.elu(h) + 1.0
            k = q
            v = h
            kv = jnp.einsum('bnhd,bnhe->bhde', k, v)
            z = k.sum(axis=1)
            num = jnp.einsum('bnhd,bhde->bnhe', q, kv)
            den = jnp.einsum('bnhd,bhd->bnh', q, z)[..., None] + ATTN_EPS
            return (num / den).reshape(B, N, C)

        def layer_norm(x, gamma, beta):
            mu = jnp.mean(x, axis=-1, keepdims=True)
            var = jnp.mean(jnp.square(x - mu), axis=-1, keepdims=True)
            return (x - mu) * lax.rsqrt(var + LN_EPS) * gamma + beta
        low = x
        highs = []
        lens = []
        for _ in range(NUM_LEVELS):
            lens.append(low.shape[1])
            l = dwconv(low, h_filter)[:, ::2]
            h = dwconv(low, g_filter)[:, ::2]
            highs.append(h)
            low = l
        low = linear_attention(low, NUM_HEADS)
        for h, L in zip(reversed(highs), reversed(lens)):
            up_l = jnp.repeat(low, 2, axis=1)[:, :L]
            up_h = jnp.repeat(h, 2, axis=1)[:, :L]
            low = dwconv(up_l, h_synth) + dwconv(up_h, g_synth)
        return layer_norm(x + low, norm_gamma, norm_beta)

    def _L0_ffn_ref(hidden_states, ln1_w, ln2_w, wq, wk, wv, wo, wr, wg, wu, wd):
        import jax, jax.numpy as jnp
        import numpy as np
        L, H, NH, NKV, HD, FF, E, K = (4, 128, 16, 4, 64, 256, 8, 2)
        B, S = (2, 256)
        THETA, EPS = (10000.0, 1e-05)

        def _rms(x, w):
            return x * jax.lax.rsqrt(jnp.mean(x * x, axis=-1, keepdims=True) + EPS) * w

        def _rope_cos_sin(seq_len, head_dim, theta):
            inv = 1.0 / theta ** (jnp.arange(0, head_dim, 2, dtype=jnp.float32) / head_dim)
            f = jnp.arange(seq_len, dtype=jnp.float32)[:, None] * inv
            emb = jnp.concatenate([f, f], axis=-1)
            return (jnp.cos(emb), jnp.sin(emb))

        def _rot_half(x):
            h = x.shape[-1] // 2
            return jnp.concatenate([-x[..., h:], x[..., :h]], axis=-1)

        def _attention(x, wq, wk, wv, wo, cos, sin, causal_bias):
            b, s, _ = x.shape
            q = (x @ wq).reshape(b, s, NH, HD).transpose(0, 2, 1, 3)
            k = (x @ wk).reshape(b, s, NKV, HD).transpose(0, 2, 1, 3)
            v = (x @ wv).reshape(b, s, NKV, HD).transpose(0, 2, 1, 3)
            c = cos[None, None]
            sn = sin[None, None]
            q = q * c + _rot_half(q) * sn
            k = k * c + _rot_half(k) * sn
            rep = NH // NKV
            k = jnp.repeat(k, rep, axis=1)
            v = jnp.repeat(v, rep, axis=1)
            scores = jnp.einsum('bhqd,bhkd->bhqk', q, k) / jnp.sqrt(jnp.asarray(HD, x.dtype))
            scores = scores + causal_bias
            attn = jax.nn.softmax(scores, axis=-1)
            out = jnp.einsum('bhqk,bhkd->bhqd', attn, v)
            out = out.transpose(0, 2, 1, 3).reshape(b, s, NH * HD)
            return out @ wo

        def _moe(x, wr, wg, wu, wd):
            logits = x @ wr
            probs = jax.nn.softmax(logits, axis=-1)
            topv, topi = jax.lax.top_k(probs, K)
            topv = topv / jnp.sum(topv, axis=-1, keepdims=True)
            comb = jnp.sum(jax.nn.one_hot(topi, E, dtype=x.dtype) * topv[..., None], axis=-2)
            out = jnp.zeros_like(x)
            for e in range(E):
                h = jax.nn.silu(x @ wg[e]) * (x @ wu[e])
                out = out + comb[..., e:e + 1] * (h @ wd[e])
            return out
        s = hidden_states.shape[1]
        cos, sin = _rope_cos_sin(s, HD, THETA)
        causal_bias = jnp.where(jnp.tril(jnp.ones((s, s), bool))[None, None], 0.0, -1000000000.0).astype(hidden_states.dtype)
        x = hidden_states
        for l in range(L):
            res = x
            h = _rms(x, ln1_w[l])
            h = _attention(h, wq[l], wk[l], wv[l], wo[l], cos, sin, causal_bias)
            x = jnp.clip(res + h, -100.0, 100.0)
            res = x
            h = _rms(x, ln2_w[l])
            h = _moe(h, wr[l], wg[l], wu[l], wd[l])
            x = jnp.clip(res + h, -100.0, 100.0)
        return x
    x = L0_attn_x
    mod = (_silu(L0_c) @ L0_wmod).reshape(L0_c.shape[0], 6, 1, -1)
    sa, ca, ga, sb, cb, gb = (mod[:, 0], mod[:, 1], mod[:, 2], mod[:, 3], mod[:, 4], mod[:, 5])
    ga = (2 * (ga >= 0) - 1) * jnp.maximum(jnp.abs(ga), 0.25)
    gb = (2 * (gb >= 0) - 1) * jnp.maximum(jnp.abs(gb), 0.25)
    h = _layernorm(x, axis=-1) * (1 + ca) + sa
    x = x + ga * _L0_attn_ref(h, L0_attn_h_filter, L0_attn_g_filter, L0_attn_h_synth, L0_attn_g_synth, L0_attn_norm_gamma, L0_attn_norm_beta)
    h = _layernorm(x, axis=-1) * (1 + cb) + sb
    x = x + gb * _L0_ffn_ref(h, L0_ffn_ln1_w, L0_ffn_ln2_w, L0_ffn_wq, L0_ffn_wk, L0_ffn_wv, L0_ffn_wo, L0_ffn_wr, L0_ffn_wg, L0_ffn_wu, L0_ffn_wd)
    return x

_drawn_inputs = setup_inputs


def setup_inputs(seed=0):
    import zlib

    import numpy as np

    out = dict(_drawn_inputs(seed))
    spreads = {'L0_attn_norm_gamma': (1.0, 0.2),
     'L0_attn_norm_beta': (0.0, 0.332),
     'L0_ffn_ln1_w': (1.0, 0.6),
     'L0_ffn_ln2_w': (1.0, 0.6)}
    factors = {'L0_ffn_wq': 8.0,
     'L0_ffn_wk': 8.0,
     'L0_ffn_wv': 4.435,
     'L0_ffn_wo': 4.325,
     'L0_ffn_wr': 8.0,
     'L0_ffn_wg': 8.0,
     'L0_ffn_wu': 8.0,
     'L0_ffn_wd': 8.0}
    for name, (base, spread) in spreads.items():
        noise = np.random.default_rng([zlib.crc32(name.encode()), seed]).standard_normal(out[name].shape)
        drawn = base * np.exp(spread * noise) if base else spread * noise
        out[name] = jnp.asarray(drawn.astype(out[name].dtype))
    for name, factor in factors.items():
        out[name] = (out[name] * factor).astype(out[name].dtype)
    return out
```

```python
from contextlib import ExitStack

import numpy as np
import concourse.bass as bass
from concourse import mybir

F32 = mybir.dt.float32
BF16 = mybir.dt.bfloat16
U32 = mybir.dt.uint32
ALU = mybir.AluOpType
ACT = mybir.ActivationFunctionType
AX = mybir.AxisListType.X

P = 128
B, S, C = 16, 256, 128
NT = B * S // P
ST = S // P
L, NH, NKV, HD, FF, NE = 4, 16, 4, 64, 256, 8
TAPS = 4
LH = 8
EPS = 1e-5
ATTN_EPS = 1e-6
NEG = -8.0e9
SCALE = HD ** -0.5
PAIR = 2 * S
NP_ = B * S // PAIR

K_ID, K_MASK, K_COS, K_SIN, K_BD, K_IOTA, K_END = 0, 128, 384, 512, 640, 768, 776


def shape_constants():
    pos = np.arange(S, dtype=np.float32)
    inv = (1.0 / np.float32(10000.0) ** (np.arange(0, HD, 2, dtype=np.float32) / np.float32(HD))).astype(np.float32)
    ang = (pos[:, None] * inv).astype(np.float32)
    emb = np.concatenate([ang, ang], axis=-1)
    cos, sin = np.cos(emb).astype(np.float32), np.sin(emb).astype(np.float32)
    sin[:, :HD // 2] *= -1.0
    k = np.zeros((P, K_END), np.float32)
    k[:, K_ID:K_ID + P] = np.eye(P)
    k[:, K_MASK + P:K_MASK + 2 * P] = np.where(np.tril(np.ones((P, P))) > 0, 0.0, NEG)
    for t in range(ST):
        k[:, K_COS + t * HD:K_COS + (t + 1) * HD] = cos[t * P:(t + 1) * P]
        k[:, K_SIN + t * HD:K_SIN + (t + 1) * HD] = sin[t * P:(t + 1) * P]
    g = np.arange(P) // LH
    k[:, K_BD:K_BD + P] = g[:, None] == g[None, :]
    k[:, K_IOTA:K_IOTA + NE] = np.arange(NE)
    sel_seq = np.repeat(np.eye(B, dtype=np.float32), P, axis=1)
    sel_exp = np.repeat(np.tile(np.eye(NE, dtype=np.float32), (3, 1)), P, axis=1)
    return k, sel_seq, sel_exp


class Arena:

    def __init__(self, tensor, size):
        self.t, self.size, self.at = tensor, size, 0

    def take(self, *shape):
        n = int(np.prod(shape))
        ap = self.t[:, self.at:self.at + n]
        self.at += n
        assert self.at <= self.size, self.at
        if len(shape) == 2:
            ap = ap.rearrange("p (a b) -> p a b", a=shape[0])
        if len(shape) == 3:
            ap = ap.rearrange("p (a b c) -> p a b c", a=shape[0], b=shape[1])
        return ap


def bass_program(nc, I, out):
    ctx = ExitStack()
    with ctx:
        SIZE = 47000
        arena = Arena(ctx.enter_context(nc.sbuf_tensor("arena", [P, SIZE], F32)), SIZE)
        sel_exp = ctx.enter_context(nc.sbuf_tensor("sel_exp", [3 * NE, NE * P], BF16))
        comb_parts = ctx.enter_context(nc.sbuf_tensor("comb_parts", [P, 4, 3 * NE], BF16))
        combT = ctx.enter_context(nc.sbuf_tensor("combT", [3 * NE, PAIR], BF16))
        ident_bf = ctx.enter_context(nc.sbuf_tensor("ident_bf", [P, P], BF16))
        psum = ctx.enter_context(nc.psum_tensor("psum", [P, 8, 512], F32))
        sems = {}

        def sem(name):
            if name not in sems:
                sems[name] = ctx.enter_context(nc.semaphore(name))
            return sems[name]

        x = arena.take(NT, C)
        x1 = arena.take(NT, C)
        gb_rows = arena.take(B, C)
        consts = arena.take(K_END)
        ident = consts[:, K_ID:K_ID + P]
        mask = consts[:, K_MASK:K_MASK + 2 * P]
        blockdiag = consts[:, K_BD:K_BD + P]
        iota8 = consts[:, K_IOTA:K_IOTA + NE]
        lnw = arena.take(2, L)
        lnw_now = arena.take(2)
        minus_half = arena.take(NT)
        wq = arena.take(NH * HD)
        wk = arena.take(NKV * HD)
        wv = arena.take(NKV * HD)
        wo = arena.take(NH // 2, C)
        wr = arena.take(NE)
        done_flags = arena.take(16)
        before_moe_w = arena.at
        wg = arena.take(NE, FF)
        wu = arena.take(NE, FF)
        wd = arena.take(NE, 2, C)
        shared = arena.at

        arena.at = before_moe_w
        cT = arena.take(B)
        scT = arena.take(B)
        wmod = arena.take(6 * C)
        filt = arena.take(4, TAPS)
        fsum = arena.take(2, 3)
        modcol = arena.take(2, B)
        rows = arena.take(5, C)
        rtmp = arena.take(4, C)
        gamma_beta = arena.take(2, C)
        sel_seq = arena.take(B, P)
        row_bc = arena.take(B, 4 * C)
        mean = arena.take(NT)
        var = arena.take(NT)
        rstd0 = arena.take(NT)
        HPW = S + 4
        hp = arena.take(B, HPW)
        low1 = arena.take(B, S // 2 + 4)
        high1 = arena.take(B, S // 2 + 2)
        low2 = arena.take(B, S // 4 + 2)
        high2 = arena.take(B, S // 4 + 2)
        at_q = arena.at
        qf = arena.take(B, S // 4)
        q_tok = arena.take(8, P)
        v_tok = arena.take(8, P)
        kvm = arena.take(B, P)
        zmat = arena.take(B, P)
        zsum = arena.take(B)
        rden = arena.take(B, S // 4)
        syn_v = arena.take(B * S // 4)
        arena.at = at_q
        xc_a = arena.take(NT, C)
        arena.at = at_q
        syn = arena.take(B, S)
        arena.at = at_q
        sq2 = arena.take(NT, C)
        sq = x

        arena.at = shared
        xs = arena.take(ST, C)
        z = arena.take(ST, C)
        junk = arena.take(ST, C)
        ms = arena.take(ST)
        rstd = arena.take(ST)
        hT = arena.take(S)
        rope_a = arena.take(2, 512)
        rope_b = arena.take(2, 512)
        qr = arena.take(ST, NH * HD)
        kr = arena.take(ST, NKV * 2 * HD)
        QT = arena.take(NH // 2, S)
        KT = arena.take(NKV, S)
        v = arena.take(ST, NKV * HD)
        probs = arena.take(2, 4, 3 * P)
        rowmax = arena.take(2, 8)
        negmax = arena.take(2, 8)
        rowsum = arena.take(2, 8)
        rinv = arena.take(2, 8)
        probsT = arena.take(8, 3 * P)
        oT = arena.take(NH // 2, S)
        arena.at = shared
        xs2 = arena.take(4, C)
        z2 = arena.take(4, C)
        junk2 = arena.take(4, C)
        ms2 = arena.take(4)
        rstd2 = arena.take(4)
        h2T = arena.take(2, PAIR)
        logits = arena.take(4, NE)
        max8 = arena.take(4, NE)
        idx8 = arena.take(4, NE)
        idxf = arena.take(4, 2)
        gap = arena.take(4)
        th = arena.take(4)
        c12 = arena.take(2, 4)
        pick = arena.take(2, 4, NE)
        comb = arena.take(4, NE)
        rest = arena.take(4, NE)
        comb_bc = arena.take(2, NE, PAIR)
        silu_g = arena.take(3, PAIR)
        silu_c = arena.take(3, PAIR)
        hh = arena.take(3, PAIR)
        yT = arena.take(PAIR)

        block = ctx.enter_context(nc.Block())
        POOL_FROM_ONE = ("rope_done",)
        ACT_FROM_ONE = ("t_free", "yT_copied", "comb_bc_ready")
        DVE_FROM_ONE = ("s_free", "o_free", "x_updated", "z_ready", "y_added", "z2_ready")
        PH = 3

        def phase_done(eng, k):
            eng.wait_ge(sem("phase_end"), PH * (k + 1))

        @block.sync
        def _(sp):
            def load(dst, src, name):
                sp.dma_start(dst, src).then_inc(sem(name), 16)

            load(cT, I["cT"], "c_in")
            load(wmod, I["L0_wmod"], "wmod_in")
            load(consts, I["consts"], "consts_in")
            xv = I["L0_attn_x"].rearrange("b (t p) c -> p (b t) c", p=P)
            for q in range(4):
                load(x1[:, q * 8:(q + 1) * 8, :], xv[:, q * 8:(q + 1) * 8, :], "x_in")
            for q, n in enumerate(["h_filter", "g_filter", "h_synth", "g_synth"]):
                load(filt[:, q, :], I[n + "_T"], "filt_in")
            for q, n in enumerate(["L0_attn_norm_gamma", "L0_attn_norm_beta"]):
                load(gamma_beta[0:B, q, :], I[n].rearrange("(a c) -> a c", a=1).partition_broadcast(B), "rows_in")
            load(sel_seq[0:B].rearrange("p b m -> p (b m)"), I["sel_seq"], "rows_in")
            load(lnw[:, 0, :], I["ln1_T"], "small_in")
            load(lnw[:, 1, :], I["ln2_T"], "small_in")

            def attn_weights(l):
                d = bass.ds(l, 1) if not isinstance(l, int) else slice(l, l + 1)
                sp.dma_start(wq, I["L0_ffn_wq"][d].rearrange("l h n -> (l h) n")).then_inc(sem("wattn_in"), 16)
                sp.dma_start(wk, I["L0_ffn_wk"][d].rearrange("l h n -> (l h) n")).then_inc(sem("wattn_in"), 16)
                sp.dma_start(wv, I["L0_ffn_wv"][d].rearrange("l h n -> (l h) n")).then_inc(sem("wattn_in"), 16)
                sp.dma_start(wo, I["L0_ffn_wo"][d].rearrange("l (c p) n -> (l p) c n", p=P)).then_inc(sem("wattn_in"), 16)

            def moe_weights(l):
                d = bass.ds(l, 1) if not isinstance(l, int) else slice(l, l + 1)
                sp.dma_start(wg, I["L0_ffn_wg"][d].rearrange("l e h f -> (l h) e f")).then_inc(sem("wmoe_in"), 16)
                sp.dma_start(wu, I["L0_ffn_wu"][d].rearrange("l e h f -> (l h) e f")).then_inc(sem("wmoe_in"), 16)
                wdv = I["L0_ffn_wd"][d].rearrange("l e (f p) n -> (l p) e f n", p=P)
                for f in range(2):
                    sp.dma_start(wd[:, :, f, :], wdv[:, :, f, :]).then_inc(sem("wmoe_in"), 16)
                sp.dma_start(wr, I["L0_ffn_wr"][d].rearrange("l h n -> (l h) n")).then_inc(sem("wmoe_in"), 16)

            attn_weights(0)
            phase_done(sp, 0)
            moe_weights(0)
            with sp.Fori(0, L - 1) as l:
                phase_done(sp, 1 + 2 * l)
                attn_weights(l + 1)
                phase_done(sp, 2 + 2 * l)
                moe_weights(l + 1)
            ov = out.rearrange("b (t p) c -> p (b t) c", p=P)
            for q in range(4):
                sp.wait_ge(sem("out_ready"), q + 1)
                sp.dma_start(ov[:, q * 8:(q + 1) * 8, :], x1[:, q * 8:(q + 1) * 8, :]).then_inc(sem("out_written"), 16)
            sp.wait_ge(sem("out_written"), 64)

        N_ATTN_W, N_MOE_W = 4 * 16, 5 * 16

        S_BANK, T_BANK, O_BANK, W_BANK = 0, 4, 6, 7

        def s_bank(k):
            return S_BANK + (k % 4)

        S_PER, T_PER = 22, 23
        S_LAG = {k: 4 for k in range(22)}
        S_LAG.update({0: 2, 1: 2, 2: 6, 3: 6})

        def s_index(sg, k):
            return sg * S_PER + 6 + k

        def t_index(sg, k):
            return sg * T_PER + 7 + k

        @block.tensor
        def _(pe):
            T = nc.tensor
            pe.wait_ge(sem("silu_c"), 1)
            pe.wait_ge(sem("wmod_in"), 16)
            for j in range(2):
                T.matmul(psum[:, 0, j * B:(j + 1) * B], wmod[:, j * C:(j + 1) * C], scT, start=True, stop=True)
            T.matmul(psum[0:B, 1, :], scT, wmod[:, 2 * C:6 * C], start=True, stop=True).then_inc(sem("mod_mm"), 1)
            pe.wait_ge(sem("rows_ready"), 1)
            pe.wait_ge(sem("rows_in"), 48)
            for b in range(B):
                if b >= 4:
                    pe.wait_ge(sem("rowbc_copied"), b - 3)
                T.matmul(psum[:, 4 + b % 4, :], sel_seq[0:B, b, :], rows[0:B, 0:4, :].rearrange("p a c -> p (a c)"),
                         start=True, stop=True).then_inc(sem("rowbc_mm"), 1)
            for q in range(4):
                pe.wait_ge(sem("rowbc_copied"), B - 3 + q)
                for j in range(4):
                    mm = T.matmul(psum[:, 4 + q, j * C:(j + 1) * C], sel_seq[0:B, 4 * q + j, :], rows[0:B, 4, :],
                                  start=True, stop=True)
                mm.then_inc(sem("rowbc_mm"), 1)
            pe.wait_ge(sem("consts_in"), 16)
            pe.wait_ge(sem("xc_ready"), 1)
            for b in range(B):
                if b < 2:
                    pe.wait_ge(sem("mod_copied"), 1)
                if b >= 2:
                    pe.wait_ge(sem("hp_ready"), b - 1)
                for t in range(ST):
                    mm = T.transpose(psum[:, b % 2, t * P:(t + 1) * P], xc_a[:, b * ST + t, :], ident)
                mm.then_inc(sem("xcT_mm"), 1)
            pe.wait_ge(sem("qf_ready"), 1)
            for g in range(8):
                T.transpose(psum[:, 2 + g // 4, (g % 4) * P:(g % 4 + 1) * P],
                            qf[:, 2 * g:2 * g + 2, :].rearrange("p b n -> p (b n)"), ident)
            pe.wait_ge(sem("rowbc_copied"), B + 4)
            pe.wait_ge(sem("lowc_ready"), 1)
            for g in range(8):
                mm = T.transpose(psum[:, 4 + g // 4, (g % 4) * P:(g % 4 + 1) * P],
                                 syn_v[:, g * P:(g + 1) * P], ident)
            mm.then_inc(sem("qv_tok_mm"), 1)
            pe.wait_ge(sem("qv_tok_ready"), 1)
            for b in range(B):
                r = slice(64 * (b % 2), 64 * (b % 2) + 64)
                bank = [6, 7][b // 8] if b % 2 == 0 else [0, 1][b // 8]
                mm = T.matmul(psum[:, bank, (b // 2 % 4) * P:(b // 2 % 4 + 1) * P], q_tok[r, b // 2, :], v_tok[r, b // 2, :],
                              start=True, stop=True)
            mm.then_inc(sem("kv_mm"), 1)
            pe.wait_ge(sem("kvz_ready"), 1)
            for b in range(B):
                T.matmul(psum[:, 2 + b // 8, (b % 8) * 64:(b % 8 + 1) * 64], kvm[:, b, :], qf[:, b, :],
                         start=True, stop=True)
            for b in range(B):
                mm = T.matmul(psum[:, 4 + b // 8, (b % 8) * 64:(b % 8 + 1) * 64], zmat[:, b, :], qf[:, b, :],
                              start=True, stop=True)
            mm.then_inc(sem("numden_mm"), 1)
            for b in range(B):
                pe.wait_ge(sem("syn_ready"), 1)
                if b >= 4:
                    pe.wait_ge(sem("yt_copied"), b - 3)
                bank = [0, 1, 6, 7][b % 4]
                for t in range(ST):
                    mm = T.transpose(psum[:, bank, t * P:(t + 1) * P], syn[:, b, t * P:(t + 1) * P], ident)
                mm.then_inc(sem("yt_mm"), 1)

            def scores(sg, q):
                for i in range(4):
                    k = 4 * q + i
                    if i == 0 and q == 0:
                        pe.wait_ge(sem("t_free"), 1 + t_index(sg, 0))
                    pe.wait_ge(sem("s_free"), 1 + s_index(sg, k) - S_LAG[k] + 1)
                    r = slice(64 * (i % 2), 64 * (i % 2) + 64)
                    c = (4 * q + i) // 2
                    bank = s_bank(k)
                    T.matmul(psum[:, bank, 0:P], QT[r, c, 0:P], KT[r, q, 0:P], start=True, stop=True)
                    T.matmul(psum[:, bank, P:3 * P], QT[r, c, P:2 * P], KT[r, q, :],
                             start=True, stop=True).then_inc(sem("s_full"), 1)

            def turn_probs(sg, q, k0):
                pe.wait_ge(sem("probs_ready"), 4 * sg + q + 1)
                for i in range(4):
                    k = k0 + i
                    pe.wait_ge(sem("t_free"), 1 + t_index(sg, k) - (1 if k else 0))
                    for j in range(3):
                        mm = T.transpose(psum[:, T_BANK + k % 2, j * P:(j + 1) * P],
                                         probs[:, q % 2, i, j * P:(j + 1) * P], ident)
                    mm.then_inc(sem("t_full"), 1)

            def weigh_values(sg, q, k0):
                pe.wait_ge(sem("o_free"), 1 + 4 * sg + q)
                for i in range(4):
                    pe.wait_ge(sem("t_free"), 1 + t_index(sg, k0 + i) + 1)
                    r = slice(64 * (i % 2), 64 * (i % 2) + 64)
                    c0 = 256 * (i // 2)
                    pt = probsT[:, 4 * (q % 2) + i, :]
                    T.matmul(psum[r, O_BANK, c0:c0 + S], v[:, 0, q * HD:(q + 1) * HD], pt[:, 0:S],
                             start=True, stop=False, skip_group_check=True)
                    mm = T.matmul(psum[r, O_BANK, c0 + P:c0 + S], v[:, 1, q * HD:(q + 1) * HD], pt[:, S:S + P],
                                  start=False, stop=True, skip_group_check=True)
                mm.then_inc(sem("o_full"), 1)

            def turn_h(sg, n, k, first):
                pe.wait_ge(sem("z_ready"), 1 + sg + 1)
                if not first:
                    pe.wait_ge(sem("t_free"), 1 + n - 1)
                for t in range(ST):
                    mm = T.transpose(psum[:, T_BANK + k % 2, t * P:(t + 1) * P], z[:, t, :], ident)
                mm.then_inc(sem("t_full"), 1)

            def project_qk(sg, hT_n, n, first):
                pe.wait_ge(sem("t_free"), 1 + hT_n + 1)
                for u in range(5):
                    if not (first and u < 4):
                        pe.wait_ge(sem("s_free"), 1 + n + u - 3)
                    bank = s_bank(u)
                    if u < 4:
                        t, half = u // 2, u % 2
                        mm = T.matmul(psum[:, bank, :], hT[:, t * P:(t + 1) * P], wq[:, half * 512:(half + 1) * 512],
                                      start=True, stop=True)
                    else:
                        for t in range(ST):
                            mm = T.matmul(psum[:, bank, t * 256:(t + 1) * 256], hT[:, t * P:(t + 1) * P], wk,
                                          start=True, stop=True)
                    mm.then_inc(sem("s_full"), 1)

            def project_v(n):
                pe.wait_ge(sem("s_free"), 1 + n - 3)
                for t in range(ST):
                    mm = T.matmul(psum[:, s_bank(5), t * 256:(t + 1) * 256], hT[:, t * P:(t + 1) * P], wv,
                                  start=True, stop=True)
                mm.then_inc(sem("s_full"), 1)

            def turn_qk(sg, n, k0):
                for u in range(6):
                    if u == 0:
                        pe.wait_ge(sem("rope_done"), 1 + 5 * sg + 4)
                    if u == 4:
                        pe.wait_ge(sem("rope_done"), 1 + 5 * sg + 5)
                    pe.wait_ge(sem("t_free"), 1 + n + u - 1)
                    for i in range(2):
                        for t in range(ST):
                            if u < 4:
                                src = qr[:, t, (2 * u + i) * P:(2 * u + i + 1) * P]
                            else:
                                src = kr[:, t, (2 * (u - 4) + i) * P:(2 * (u - 4) + i + 1) * P]
                            mm = T.transpose(psum[:, T_BANK + (k0 + u) % 2, (2 * i + t) * P:(2 * i + t + 1) * P],
                                             src, ident)
                    mm.then_inc(sem("t_full"), 1)

            def project_out(sg):
                pe.wait_ge(sem("o_free"), 1 + 4 * sg + 4)
                pe.wait_ge(sem("x_updated"), 1 + sg)
                for t in range(ST):
                    for c in range(NH // 2):
                        mm = T.matmul(psum[:, W_BANK, t * P:(t + 1) * P], oT[:, c, t * P:(t + 1) * P], wo[:, c, :],
                                      start=(c == 0), stop=(c == NH // 2 - 1))
                mm.then_inc(sem("w_full"), 1)

            def sequence(sg, head):
                scores(sg, 0)
                scores(sg, 1)
                turn_probs(sg, 0, 0)
                weigh_values(sg, 0, 0)
                scores(sg, 2)
                turn_probs(sg, 1, 4)
                weigh_values(sg, 1, 4)
                if head:
                    turn_h(sg + 1, t_index(sg, 8), 8, False)
                scores(sg, 3)
                turn_probs(sg, 2, 8 + head)
                weigh_values(sg, 2, 8 + head)
                if head:
                    project_qk(sg + 1, t_index(sg, 8), s_index(sg, 16), False)
                turn_probs(sg, 3, 12 + head)
                weigh_values(sg, 3, 12 + head)
                if head:
                    project_v(s_index(sg, 21))
                project_out(sg)
                if head:
                    turn_qk(sg + 1, t_index(sg, 17), 17)

            PREP_AT_PE = {2: 0, 4: 1, 8: 2, 9: 3, 10: 4, 11: 5, 12: 6, 13: 7, 14: 8, 15: 9}

            def prepare(pg, step, par):
                if step == 0:
                    pe.wait_ge(sem("z2_ready"), 1 + pg + 1)
                    pe.wait_ge(sem("comb_bc_ready"), 1 + NE * pg)
                    for t in range(4):
                        mm = T.transpose(psum[:, 5, t * P:(t + 1) * P], z2[:, t, :], ident)
                    mm.then_inc(sem("h2T_mm"), 1)
                if step == 1:
                    pe.wait_ge(sem("h2T_ready"), pg + 1)
                    for t in range(4):
                        mm = T.matmul(psum[:, 6, t * NE:(t + 1) * NE], h2T[:, par, t * P:(t + 1) * P], wr,
                                      start=True, stop=True)
                    mm.then_inc(sem("logits_mm"), 1)
                if step == 2:
                    pe.wait_ge(sem("comb_ready"), pg + 1)
                    for t in range(4):
                        mm = T.transpose(psum[0:3 * NE, 6, t * 64:(t + 1) * 64].bitcast(BF16), comb_parts[:, t, :],
                                         ident_bf[:, :])
                    mm.then_inc(sem("combT_mm"), 1)
                if step >= 3:
                    e = step - 3
                    if e == 0:
                        pe.wait_ge(sem("combT_ready"), pg + 1)
                    else:
                        pe.wait_ge(sem("comb_bc_ready"), 1 + NE * pg + e - 1)
                    T.matmul(psum[:, 5 + e % 2, :], sel_exp[:, e * P:(e + 1) * P], combT[:, :],
                             start=True, stop=True).then_inc(sem("comb_bc_mm"), 1)

            def experts(pg, par, prep):
                NU = 2 * NE

                def down(n):
                    e, f = n // 2, n % 2
                    pe.wait_ge(sem("hh_ready"), NU * pg + n + 1)
                    mm = T.matmul(psum[:, 4, :], wd[:, e, f, :], hh[:, n % 3, :], start=(n == 0), stop=(n == NU - 1),
                                  skip_group_check=True)
                    if n == NU - 1:
                        mm.then_inc(sem("y_mm"), 1)
                    else:
                        mm.then_inc(sem("down_mm"), 1)

                pe.wait_ge(sem("yT_copied"), 1 + pg)
                for n in range(NU):
                    e, f = n // 2, n % 2
                    if n >= 2:
                        pe.wait_ge(sem("hh_ready"), NU * pg + n - 1)
                    T.matmul(psum[:, 2 * (n % 2), :], wg[:, e, f * P:(f + 1) * P], h2T[:, par, :],
                             start=True, stop=True).then_inc(sem("gate_mm"), 1)
                    T.matmul(psum[:, 2 * (n % 2) + 1, :], wu[:, e, f * P:(f + 1) * P], h2T[:, par, :],
                             start=True, stop=True).then_inc(sem("up_mm"), 1)
                    if n >= 1:
                        down(n - 1)
                    if prep and n in PREP_AT_PE:
                        prepare(pg + 1, PREP_AT_PE[n], 1 - par)
                if prep:
                    prepare(pg + 1, 2 + NE, 1 - par)
                down(NU - 1)
                pe.wait_ge(sem("yT_copied"), 1 + pg + 1)
                pe.wait_ge(sem("y_added"), 1 + pg)
                for t in range(4):
                    mm = T.transpose(psum[:, 7, t * P:(t + 1) * P], yT[:, t * P:(t + 1) * P], ident)
                mm.then_inc(sem("y_tok_mm"), 1)

            with pe.Fori(0, L) as l:
                phase_done(pe, 2 * l)
                pe.wait_ge(sem("wattn_in"), N_ATTN_W * (l + 1))
                s0 = l * B
                turn_h(s0, s0 * T_PER, 0, True)
                project_qk(s0, s0 * T_PER, s0 * S_PER, True)
                project_v(s0 * S_PER + 5)
                turn_qk(s0, s0 * T_PER + 1, 1)
                with pe.Fori(0, B - 1) as s:
                    sequence(l * B + s, 1)
                sequence(l * B + B - 1, 0)
                phase_done(pe, 1 + 2 * l)
                pe.wait_ge(sem("wmoe_in"), N_MOE_W * (l + 1))
                for step in range(11):
                    prepare(l * NP_, step, 0)
                with pe.Fori(0, NP_ // 2 - 1) as i:
                    experts(l * NP_ + 2 * i, 0, True)
                    experts(l * NP_ + 2 * i + 1, 1, True)
                experts(l * NP_ + NP_ - 2, 0, True)
                experts(l * NP_ + NP_ - 1, 1, False)

        @block.scalar
        def _(act):
            A = nc.scalar
            act.wait_ge(sem("pool_const"), 2)
            for name in ACT_FROM_ONE:
                A.copy(done_flags[:, 0:1], done_flags[:, 5:6]).then_inc(sem(name), 1)
                act.wait_ge(sem(name), 1)
            act.wait_ge(sem("c_in"), 16)
            A.activation(scT, cT, ACT.Silu).then_inc(sem("silu_c"), 1)
            for b in range(B):
                act.wait_ge(sem("rowbc_mm"), b + 1)
                A.copy(row_bc[:, b, :], psum[:, 4 + b % 4, :]).then_inc(sem("rowbc_copied"), 1)
            for q in range(4):
                act.wait_ge(sem("rowbc_mm"), B + q + 1)
                A.copy(gb_rows[:, 4 * q:4 * q + 4, :].rearrange("p b c -> p (b c)"), psum[:, 4 + q, :]) \
                    .then_inc(sem("rowbc_copied"), 1)
            act.wait_ge(sem("centred"), 1)
            A.activation(sq, xc_a, ACT.Square).then_inc(sem("squared"), 1)
            act.wait_ge(sem("hp_zeroed"), 1)
            for b in range(B):
                act.wait_ge(sem("xcT_mm"), b + 1)
                A.activation(hp[:, b, 1:S + 1], psum[:, b % 2, 0:S], ACT.Identity, bias=modcol[:, 0, b:b + 1],
                             scale=modcol[:, 1, b:b + 1]).then_inc(sem("hp_ready"), 1)
            act.wait_ge(sem("qmin_ready"), 1)
            A.activation(rden, rden, ACT.Exp).then_inc(sem("qexp_ready"), 1)
            act.wait_ge(sem("qv_tok_mm"), 1)
            for h in range(2):
                A.copy(v_tok[:, 4 * h:4 * h + 4, :].rearrange("p a b -> p (a b)"), psum[:, 4 + h, :]) \
                    .then_inc(sem("v_tok_ready"), 1)
            for b in range(B):
                act.wait_ge(sem("yt_mm"), b + 1)
                A.copy(x[:, ST * b:ST * b + ST, :].rearrange("p a b -> p (a b)"),
                       psum[:, [0, 1, 6, 7][b % 4], 0:S]).then_inc(sem("yt_copied"), 1)
            act.wait_ge(sem("centred"), 2)
            A.activation(sq2, x, ACT.Square).then_inc(sem("squared"), 1)
            act.wait_ge(sem("centred"), 3)
            A.activation(sq2, x, ACT.Square).then_inc(sem("squared"), 1)
            A.copy(done_flags[:, 0:1], done_flags[:, 5:6]).then_inc(sem("phase_end"), 1)

            def exps(sg, q):
                act.wait_ge(sem("negmax_ready"), 4 * sg + q + 1)
                for k in range(8):
                    i, t = k // 2, k % 2
                    a = probs[:, q % 2, i, 0:P] if t == 0 else probs[:, q % 2, i, P:3 * P]
                    ins = A.activation(a, a, ACT.Exp, bias=negmax[:, q % 2, k:k + 1],
                                       accum_out=rowsum[:, q % 2, k:k + 1])
                ins.then_inc(sem("exp_done"), 1)

            def copy_probs(sg, q, k0):
                for i in range(4):
                    act.wait_ge(sem("t_full"), t_index(sg, k0 + i) + 1)
                    A.copy(probsT[:, 4 * (q % 2) + i, :], psum[:, T_BANK + (k0 + i) % 2, 0:3 * P]) \
                        .then_inc(sem("t_free"), 1)

            def copy_h(n, k):
                act.wait_ge(sem("t_full"), n + 1)
                A.mul(hT, psum[:, T_BANK + k % 2, 0:S], lnw_now[:, 0:1]).then_inc(sem("t_free"), 1)

            def copy_qk(n, k0):
                for u in range(6):
                    act.wait_ge(sem("t_full"), n + u + 1)
                    dst = QT[:, 2 * u:2 * u + 2, :] if u < 4 else KT[:, 2 * (u - 4):2 * (u - 4) + 2, :]
                    A.copy(dst.rearrange("p a b -> p (a b)"), psum[:, T_BANK + (k0 + u) % 2, :]) \
                        .then_inc(sem("t_free"), 1)

            def sequence(sg, head):
                exps(sg, 0)
                exps(sg, 1)
                copy_probs(sg, 0, 0)
                exps(sg, 2)
                copy_probs(sg, 1, 4)
                if head:
                    copy_h(t_index(sg, 8), 8)
                exps(sg, 3)
                copy_probs(sg, 2, 8 + head)
                copy_probs(sg, 3, 12 + head)
                if head:
                    copy_qk(t_index(sg, 17), 17)

            PREP_AT_ACT = {3: 0, 6: 1, 10: 3, 11: 4, 12: 5, 13: 6, 14: 7, 15: 8}

            def prepare(pg, step, par):
                if step == 0:
                    act.wait_ge(sem("h2T_mm"), pg + 1)
                    A.mul(h2T[:, par, :], psum[:, 5, :], lnw_now[:, 1:2]).then_inc(sem("h2T_ready"), 1)
                if step == 1:
                    act.wait_ge(sem("gap_ready"), pg + 1)
                    A.activation(th, gap, ACT.Tanh, scale=0.5).then_inc(sem("tanh_ready"), 1)
                if step >= 3:
                    e = step - 3
                    act.wait_ge(sem("comb_bc_mm"), NE * pg + e + 1)
                    A.copy(comb_bc[:, par, e, :], psum[:, 5 + e % 2, :]).then_inc(sem("comb_bc_ready"), 1)

            def experts(pg, par, prep):
                NU = 2 * NE
                for n in range(NU):
                    act.wait_ge(sem("gate_mm"), NU * pg + n + 1)
                    if n >= 3:
                        act.wait_ge(sem("silu_c_ready"), NU * pg + n - 2)
                    A.activation(silu_g[:, n % 3, :], psum[:, 2 * (n % 2), :], ACT.Silu).then_inc(sem("silu_ready"), 1)
                    if prep and n in PREP_AT_ACT:
                        prepare(pg + 1, PREP_AT_ACT[n], 1 - par)
                if prep:
                    prepare(pg + 1, 3 + NE - 2, 1 - par)
                    prepare(pg + 1, 3 + NE - 1, 1 - par)
                act.wait_ge(sem("y_mm"), pg + 1)
                act.wait_ge(sem("y_added"), 1 + pg)
                A.copy(yT, psum[:, 4, :]).then_inc(sem("yT_copied"), 1)

            with act.Fori(0, L) as l:
                phase_done(act, 2 * l)
                copy_h(l * B * T_PER, 0)
                copy_qk(l * B * T_PER + 1, 1)
                with act.Fori(0, B - 1) as s:
                    sequence(l * B + s, 1)
                sequence(l * B + B - 1, 0)
                A.copy(done_flags[:, 0:1], done_flags[:, 5:6]).then_inc(sem("phase_end"), 1)
                phase_done(act, 1 + 2 * l)
                for step in range(11):
                    prepare(l * NP_, step, 0)
                with act.Fori(0, NP_ // 2 - 1) as i:
                    experts(l * NP_ + 2 * i, 0, True)
                    experts(l * NP_ + 2 * i + 1, 1, True)
                experts(l * NP_ + NP_ - 2, 0, True)
                experts(l * NP_ + NP_ - 1, 1, False)
                A.copy(done_flags[:, 0:1], done_flags[:, 5:6]).then_inc(sem("phase_end"), 1)

        @block.gpsimd
        def _(pool):
            G = nc.gpsimd
            G.dma_start(sel_exp[:, :], I["sel_exp"]).then_inc(sem("sel_exp_in"), 16)
            G.memset(minus_half, -0.5).then_inc(sem("pool_const"), 1)
            G.memset(done_flags[:, 5:8], 0.0).then_inc(sem("pool_const"), 1)
            pool.wait_ge(sem("pool_const"), 2)
            for name in POOL_FROM_ONE:
                G.memset(done_flags[:, 1:2], 0.0).then_inc(sem(name), 1)
                pool.wait_ge(sem(name), 1)
            for n in range(3):
                pool.wait_ge(sem("var_ready"), n + 1)
                G.tensor_tensor(rstd0, var, minus_half, ALU.pow).then_inc(sem("rstd0_ready"), 1)
            pool.wait_ge(sem("sel_exp_in"), 16)
            G.memset(done_flags[:, 1:2], 0.0).then_inc(sem("phase_end"), 1)

            def load_x(sg, s):
                pool.wait_ge(sem("z_ready"), 1 + sg)
                G.tensor_tensor(done_flags[:, 6:7], done_flags[:, 7:8], done_flags[:, 7:8], ALU.add)
                G.tensor_copy(xs, x[:, bass.ds(s * ST, ST), :]).then_inc(sem("xs_ready"), 1)

            def root(sg):
                pool.wait_ge(sem("ms_ready"), sg + 1)
                G.tensor_tensor(rstd, ms, minus_half[:, 0:ST], ALU.pow).then_inc(sem("rstd_ready"), 1)

            def normalise(sg, q):
                pool.wait_ge(sem("rinv_ready"), 4 * sg + q + 1)
                r = rinv[:, q % 2, :].rearrange("p (i t) -> p i t", t=2)
                for t in range(2):
                    a = probs[:, q % 2, :, 0:P] if t == 0 else probs[:, q % 2, :, P:3 * P]
                    ins = G.tensor_tensor(a, a, r[:, :, t:t + 1].broadcast_to([P, 4, P * (t + 1)]), ALU.mult)
                ins.then_inc(sem("probs_ready"), 1)

            def rope_adds(sg):
                for u in range(5):
                    pool.wait_ge(sem("rope_parts"), 5 * sg + u + 1)
                    a, b = rope_a[:, u % 2, :], rope_b[:, u % 2, :]
                    if u < 4:
                        G.tensor_tensor(qr[:, u // 2, (u % 2) * 512:(u % 2 + 1) * 512], a, b, ALU.add) \
                            .then_inc(sem("rope_done"), 1)
                    else:
                        for t in range(ST):
                            for d in range(2):
                                dst = kr[:, t, :].rearrange("p (j d e) -> p j d e", j=NKV, d=2)[:, :, d, :]
                                ins = G.tensor_tensor(
                                    dst, a[:, t * 256:(t + 1) * 256].rearrange("p (j e) -> p j e", j=NKV),
                                    b[:, t * 256:(t + 1) * 256].rearrange("p (j e) -> p j e", j=NKV), ALU.add)
                        ins.then_inc(sem("rope_done"), 1)

            def sequence(sg, s, head):
                if head:
                    load_x(sg + 1, s + 1)
                normalise(sg, 0)
                if head:
                    root(sg + 1)
                normalise(sg, 1)
                normalise(sg, 2)
                normalise(sg, 3)
                if head:
                    rope_adds(sg + 1)

            def prepare(pg, p, step):
                if step == 0:
                    pool.wait_ge(sem("z2_ready"), 1 + pg)
                    G.tensor_tensor(done_flags[:, 6:7], done_flags[:, 7:8], done_flags[:, 7:8], ALU.add)
                    G.tensor_copy(xs2, x[:, bass.ds(p * 4, 4), :]).then_inc(sem("xs2_ready"), 1)
                if step == 1:
                    pool.wait_ge(sem("ms2_ready"), pg + 1)
                    G.tensor_tensor(rstd2, ms2, minus_half[:, 0:4], ALU.pow).then_inc(sem("rstd2_ready"), 1)

            def experts(pg, p, par, prep):
                NU = 2 * NE
                for n in range(NU):
                    if prep and n == 0:
                        prepare(pg + 1, p + 1, 0)
                    if n == 0:
                        pool.wait_ge(sem("comb_bc_ready"), 1 + NE * (pg + 1))
                    pool.wait_ge(sem("silu_ready"), NU * pg + n + 1)
                    if n >= 3:
                        pool.wait_ge(sem("hh_ready"), NU * pg + n - 2)
                    G.tensor_tensor(silu_c[:, n % 3, :], silu_g[:, n % 3, :], comb_bc[:, par, n // 2, :], ALU.mult) \
                        .then_inc(sem("silu_c_ready"), 1)
                    if prep and n == 0:
                        prepare(pg + 1, p + 1, 1)

            with pool.Fori(0, L) as l:
                phase_done(pool, 2 * l)
                pool.wait_ge(sem("small_in"), 32)
                for j in range(2):
                    ins = G.tensor_copy(lnw_now[:, j:j + 1], lnw[:, j, bass.ds(l, 1)])
                load_x(l * B, 0)
                root(l * B)
                rope_adds(l * B)
                with pool.Fori(0, B - 1) as s:
                    sequence(l * B + s, s, 1)
                sequence(l * B + B - 1, None, 0)
                G.memset(done_flags[:, 1:2], 0.0).then_inc(sem("phase_end"), 1)
                phase_done(pool, 1 + 2 * l)
                prepare(l * NP_, 0, 0)
                prepare(l * NP_, 0, 1)
                with pool.Fori(0, NP_ // 2 - 1) as i:
                    experts(l * NP_ + 2 * i, 2 * i, 0, True)
                    experts(l * NP_ + 2 * i + 1, 2 * i + 1, 1, True)
                experts(l * NP_ + NP_ - 2, NP_ - 2, 0, True)
                experts(l * NP_ + NP_ - 1, NP_ - 1, 1, False)
                G.memset(done_flags[:, 1:2], 0.0).then_inc(sem("phase_end"), 1)

        @block.vector
        def _(dve):
            V = nc.vector

            class Steps:

                def __init__(self, base):
                    self.base, self.n = base, 0

                def __call__(self, ins):
                    ins.then_inc(sem("dve_step"), 1)
                    self.n += 1
                    dve.wait_ge(sem("dve_step"), self.base + self.n)

            step = Steps(0)
            D = S // 4
            for name in DVE_FROM_ONE:
                V.memset(done_flags[:, 2:3], 0.0).then_inc(sem(name), 1)
                dve.wait_ge(sem(name), 1)
            step(V.memset(hp, 0.0))
            step(V.memset(low1, 0.0))
            step(V.memset(high1, 0.0))
            step(V.memset(high2, 0.0))
            V.memset(low2, 0.0).then_inc(sem("hp_zeroed"), 1)
            dve.wait_ge(sem("hp_zeroed"), 1)
            dve.wait_ge(sem("consts_in"), 16)
            step(V.tensor_copy(ident_bf[:, :], ident))
            dve.wait_ge(sem("mod_mm"), 1)
            dve.wait_ge(sem("rows_in"), 48)
            step(V.tensor_copy(modcol[:, 0, :], psum[:, 0, 0:B]))
            step(V.tensor_scalar(modcol[:, 1, :], psum[:, 0, B:2 * B], 1.0, None, ALU.add))
            rt = rtmp[0:B]
            rw = rows[0:B]
            for src, dst in ((0, rt[:, 2, :]), (3, rw[:, 4, :])):
                g = psum[0:B, 1, src * C:(src + 1) * C]
                step(V.tensor_copy(rt[:, 3, :], g))
                step(V.scalar_tensor_tensor(rt[:, 0, :], rt[:, 3, :], -1.0, rt[:, 3, :], ALU.mult, ALU.max))
                step(V.tensor_scalar(rt[:, 0, :], rt[:, 0, :], 0.25, None, ALU.max))
                step(V.tensor_scalar(rt[:, 1, :], rt[:, 3, :], 0.0, 2.0, ALU.is_ge, ALU.mult))
                step(V.scalar_tensor_tensor(dst, rt[:, 1, :], -1.0, rt[:, 0, :], ALU.add, ALU.mult))
            step(V.tensor_tensor(rw[:, 0, :], rt[:, 2, :], gamma_beta[0:B, 0, :], ALU.mult))
            step(V.tensor_tensor(rw[:, 1, :], rt[:, 2, :], gamma_beta[0:B, 1, :], ALU.mult))
            step(V.tensor_scalar(rw[:, 2, :], psum[0:B, 1, 2 * C:3 * C], 1.0, None, ALU.add))
            V.tensor_copy(rw[:, 3, :], psum[0:B, 1, C:2 * C]).then_inc(sem("rows_ready"), 1)
            V.memset(done_flags[:, 3:4], 0.0).then_inc(sem("mod_copied"), 1)
            dve.wait_ge(sem("mod_copied"), 1)
            dve.wait_ge(sem("rows_ready"), 1)

            def per_row(a):
                return a.rearrange("p (t a) -> p t a", a=1).broadcast_to([P, NT, C])

            def layer_norm(src, dst, squares, n, wait_src):
                wait_src()
                step(V.tensor_reduce(mean, src, AX, ALU.add))
                step(V.tensor_scalar(mean, mean, 1.0 / C, None, ALU.mult))
                V.tensor_tensor(dst, src, per_row(mean), ALU.subtract).then_inc(sem("centred"), 1)
                dve.wait_ge(sem("squared"), n + 1)
                step(V.tensor_reduce(var, squares, AX, ALU.add))
                V.tensor_scalar(var, var, 1.0 / C, EPS, ALU.mult, ALU.add).then_inc(sem("var_ready"), 1)
                dve.wait_ge(sem("rstd0_ready"), n + 1)

            layer_norm(x1, xc_a, sq, 0, lambda: dve.wait_ge(sem("x_in"), 64))
            V.tensor_tensor(xc_a, xc_a, per_row(rstd0), ALU.mult).then_inc(sem("xc_ready"), 1)
            dve.wait_ge(sem("filt_in"), 64)
            dve.wait_ge(sem("hp_ready"), B)

            def analyse(src, dst, f, n):
                for k in range(TAPS):
                    a = src[:, :, k:k + 2 * n - 1:2]
                    tap = filt[:, f, k:k + 1]
                    if k == 0:
                        step(V.tensor_scalar(dst, a, tap, None, ALU.mult))
                    else:
                        step(V.scalar_tensor_tensor(dst, a, tap, dst, ALU.mult, ALU.add))

            analyse(hp, low1[:, :, 1:1 + S // 2], 0, S // 2)
            analyse(hp, high1[:, :, 1:1 + S // 2], 1, S // 2)
            analyse(low1, low2[:, :, 1:1 + D], 0, D)
            analyse(low1, high2[:, :, 1:1 + D], 1, D)
            lc = low2[:, :, 1:1 + D]
            step(V.tensor_copy(syn_v.rearrange("p (b n) -> p b n", b=B), lc))
            V.tensor_scalar(rden, lc, 0.0, None, ALU.min).then_inc(sem("qmin_ready"), 1)
            dve.wait_ge(sem("qexp_ready"), 1)
            V.scalar_tensor_tensor(qf, lc, 0.0, rden, ALU.max, ALU.add).then_inc(sem("qf_ready"), 1)
            V.memset(done_flags[:, 3:4], 0.0).then_inc(sem("lowc_ready"), 1)
            dve.wait_ge(sem("qf_ready"), 1)
            step(V.tensor_reduce(zsum, qf, AX, ALU.add))
            dve.wait_ge(sem("qv_tok_mm"), 1)
            for h in range(2):
                step(V.tensor_copy(q_tok[:, 4 * h:4 * h + 4, :].rearrange("p a b -> p (a b)"), psum[:, 2 + h, :]))
            dve.wait_ge(sem("v_tok_ready"), 2)
            V.memset(done_flags[:, 3:4], 0.0).then_inc(sem("qv_tok_ready"), 1)
            bd4 = blockdiag.rearrange("p (a c) -> p a c", a=1).broadcast_to([P, 4, P])
            for g in range(4):
                zs = zsum[:, 4 * g:4 * g + 4].rearrange("p (b a) -> p b a", a=1).broadcast_to([P, 4, P])
                step(V.tensor_tensor(zmat[:, 4 * g:4 * g + 4, :], bd4, zs, ALU.mult))
            dve.wait_ge(sem("kv_mm"), 1)
            for g in range(4):
                bank, odd, b0 = [6, 7, 0, 1][g], g // 2, 8 * (g % 2)
                ins = V.tensor_tensor(kvm[:, b0 + odd:b0 + odd + 7:2, :],
                                      psum[:, bank, :].rearrange("p (a c) -> p a c", a=4), bd4, ALU.mult)
            ins.then_inc(sem("kvz_ready"), 1)
            dve.wait_ge(sem("numden_mm"), 1)
            for h in range(2):
                den = psum[:, 4 + h, :].rearrange("p (b n) -> p b n", b=8)
                num = psum[:, 2 + h, :].rearrange("p (b n) -> p b n", b=8)
                rd = rden[:, 8 * h:8 * h + 8, :]
                step(V.tensor_scalar(rd, den, ATTN_EPS, None, ALU.add))
                step(V.reciprocal(rd, rd))
                step(V.tensor_tensor(low2[:, 8 * h:8 * h + 8, 1:1 + D], num, rd, ALU.mult))
            for f in range(2):
                for j, (a, b) in enumerate(((1, 2), (0, 1), (2, 3))):
                    step(V.tensor_tensor(fsum[:, f, j:j + 1], filt[:, 2 + f, a:a + 1], filt[:, 2 + f, b:b + 1],
                                         ALU.add))

            def synthesise(low, high, dst, n, start):
                even, odd = dst[:, :, 0:2 * n - 1:2], dst[:, :, 1:2 * n:2]
                for f, src in enumerate((low, high)):
                    before, at, after = src[:, :, 0:n], src[:, :, 1:n + 1], src[:, :, 2:n + 2]
                    terms = (((before, filt[:, 2 + f, 0:1]), (at, fsum[:, f, 0:1]), (after, filt[:, 2 + f, 3:4])),
                             ((at, fsum[:, f, 1:2]), (after, fsum[:, f, 2:3])))
                    for o, ts in zip((even, odd), terms):
                        for k, (a, tap) in enumerate(ts):
                            if f == 0 and k == 0 and start is None:
                                step(V.tensor_scalar(o, a, tap, None, ALU.mult))
                            elif f == 0 and k == 0:
                                base = start[:, :, 0:2 * n - 1:2] if o is even else start[:, :, 1:2 * n:2]
                                step(V.scalar_tensor_tensor(o, a, tap, base, ALU.mult, ALU.add))
                            else:
                                step(V.scalar_tensor_tensor(o, a, tap, o, ALU.mult, ALU.add))

            synthesise(low2, high2, low1[:, :, 1:1 + S // 2], D, None)
            step(V.memset(low1[:, :, 0:1], 0.0))
            step(V.memset(low1[:, :, 1 + S // 2:4 + S // 2], 0.0))
            synthesise(low1, high1, syn, S // 2, hp[:, :, 1:S + 1])
            V.memset(done_flags[:, 3:4], 0.0).then_inc(sem("syn_ready"), 1)
            rb = row_bc.rearrange("p b (k c) -> p b k c", k=4)

            def by_row(k):
                return rb[:, :, k:k + 1, :].broadcast_to([P, B, ST, C])

            def seqs(a):
                return a.rearrange("p (b t) c -> p b t c", t=ST)

            layer_norm(x, x, sq2, 1, lambda: dve.wait_ge(sem("yt_copied"), B))
            step(V.tensor_tensor(x, x, per_row(rstd0), ALU.mult))
            step(V.tensor_tensor(seqs(x), seqs(x), by_row(0), ALU.mult))
            step(V.tensor_tensor(seqs(x), seqs(x), by_row(1), ALU.add))
            step(V.tensor_tensor(x1, x1, x, ALU.add))
            layer_norm(x1, x, sq2, 2, lambda: None)
            step(V.tensor_tensor(x, x, per_row(rstd0), ALU.mult))
            step(V.tensor_tensor(seqs(x), seqs(x), by_row(2), ALU.mult))
            step(V.tensor_tensor(seqs(x), seqs(x), by_row(3), ALU.add))
            V.memset(done_flags[:, 2:3], 0.0).then_inc(sem("phase_end"), 1)
            STEPS0 = step.n

            def mean_square(sg):
                dve.wait_ge(sem("xs_ready"), sg + 1)
                for t in range(ST):
                    ins = V.tensor_tensor_reduce(junk[:, t, :], xs[:, t, :], xs[:, t, :], 1.0 / C, EPS, ALU.mult, ALU.add,
                                                 ms[:, t:t + 1])
                ins.then_inc(sem("ms_ready"), 1)

            def scale_rows(sg):
                dve.wait_ge(sem("rstd_ready"), sg + 1)
                for t in range(ST):
                    ins = V.tensor_scalar(z[:, t, :], xs[:, t, :], rstd[:, t:t + 1], None, ALU.mult)
                ins.then_inc(sem("z_ready"), 1)

            def rope(sg, n):
                for u in range(5):
                    dve.wait_ge(sem("s_full"), n + u + 1)
                    dve.wait_ge(sem("rope_done"), 1 + 5 * sg + max(u - 1, 0))
                    bank = psum[:, s_bank(u), :]
                    a, b = rope_a[:, u % 2, :], rope_b[:, u % 2, :]
                    if u < 4:
                        parts = [(slice(0, 512), u // 2, 8)]
                    else:
                        parts = [(slice(0, 256), 0, 4), (slice(256, 512), 1, 4)]
                    for sl, t, nh in parts:
                        src = bank[:, sl].rearrange("p (h d) -> p h d", h=nh)
                        aa = a[:, sl].rearrange("p (h d) -> p h d", h=nh)
                        bb = b[:, sl].rearrange("p (h d) -> p h d", h=nh)
                        cos = consts[:, K_COS + t * HD:K_COS + (t + 1) * HD].rearrange("p (a d) -> p a d", a=1)
                        sin = consts[:, K_SIN + t * HD:K_SIN + (t + 1) * HD].rearrange("p (a d) -> p a d", a=1)
                        hf = HD // 2
                        V.tensor_tensor(aa, src, cos.broadcast_to([P, nh, HD]), ALU.mult)
                        V.tensor_tensor(bb[:, :, 0:hf], src[:, :, hf:HD], sin[:, :, 0:hf].broadcast_to([P, nh, hf]),
                                        ALU.mult)
                        ins = V.tensor_tensor(bb[:, :, hf:HD], src[:, :, 0:hf],
                                              sin[:, :, hf:HD].broadcast_to([P, nh, hf]), ALU.mult)
                    ins.then_inc(sem("rope_parts"), 1)
                    dve.wait_ge(sem("rope_parts"), 5 * sg + u + 1)
                    V.memset(done_flags[:, 3:4], 0.0).then_inc(sem("s_free"), 1)

            def copy_v(n):
                dve.wait_ge(sem("s_full"), n + 1)
                V.tensor_copy(v.rearrange("p t c -> p (t c)"), psum[:, s_bank(5), :]).then_inc(sem("s_free"), 1)

            def mask_and_max(sg, q):
                for i in range(4):
                    k = 4 * q + i
                    dve.wait_ge(sem("s_full"), s_index(sg, k) + 1)
                    V.memset(done_flags[:, 8 + i:9 + i], 0.0)
                    V.tensor_tensor_reduce(probs[:, q % 2, i, 0:P], psum[:, s_bank(k), 0:P], mask[:, P:2 * P],
                                           SCALE, -3.0e38, ALU.add, ALU.max, rowmax[:, q % 2, 2 * i:2 * i + 1])
                    V.tensor_tensor_reduce(probs[:, q % 2, i, P:3 * P], psum[:, s_bank(k), P:3 * P], mask,
                                           SCALE, -3.0e38, ALU.add, ALU.max,
                                           rowmax[:, q % 2, 2 * i + 1:2 * i + 2]).then_inc(sem("s_free"), 1)
                dve.wait_ge(sem("s_free"), 1 + s_index(sg, 4 * q + 3) + 1)
                V.tensor_scalar(negmax[:, q % 2, :], rowmax[:, q % 2, :], -1.0, None, ALU.mult) \
                    .then_inc(sem("negmax_ready"), 1)

            def invert(sg, q):
                dve.wait_ge(sem("exp_done"), 4 * sg + q + 1)
                V.reciprocal(rinv[:, q % 2, :], rowsum[:, q % 2, :]).then_inc(sem("rinv_ready"), 1)

            def copy_o(sg, q):
                dve.wait_ge(sem("o_full"), 4 * sg + q + 1)
                V.tensor_copy(oT[:, 2 * q:2 * q + 2, :].rearrange("p a b -> p (a b)"), psum[:, O_BANK, :]) \
                    .then_inc(sem("o_free"), 1)

            def update_x(sg, s):
                dve.wait_ge(sem("w_full"), sg + 1)
                xv = x[:, bass.ds(s * ST, ST), :]
                V.tensor_tensor(xv, xv, psum[:, W_BANK, 0:S].rearrange("p (t c) -> p t c", t=ST), ALU.add) \
                    .then_inc(sem("x_added"), 1)
                dve.wait_ge(sem("x_added"), sg + 1)
                V.tensor_scalar(xv, xv, 100.0, -100.0, ALU.min, ALU.max).then_inc(sem("x_updated"), 1)

            def sequence(sg, s, head):
                mask_and_max(sg, 0)
                mask_and_max(sg, 1)
                invert(sg, 0)
                if head:
                    mean_square(sg + 1)
                mask_and_max(sg, 2)
                invert(sg, 1)
                if head:
                    scale_rows(sg + 1)
                copy_o(sg, 0)
                mask_and_max(sg, 3)
                invert(sg, 2)
                copy_o(sg, 1)
                invert(sg, 3)
                copy_o(sg, 2)
                if head:
                    rope(sg + 1, s_index(sg, 16))
                copy_o(sg, 3)
                if head:
                    copy_v(s_index(sg, 21))
                update_x(sg, s)

            PREP_STEPS = 15

            def prepare(pg, part, par):
                st = Steps(STEPS0 + pg * PREP_STEPS)
                if part == 0:
                    dve.wait_ge(sem("xs2_ready"), pg + 1)
                    for t in range(4):
                        ins = V.tensor_tensor_reduce(junk2[:, t, :], xs2[:, t, :], xs2[:, t, :], 1.0 / C, EPS,
                                                     ALU.mult, ALU.add, ms2[:, t:t + 1])
                    ins.then_inc(sem("ms2_ready"), 1)
                    return
                if part == 1:
                    dve.wait_ge(sem("rstd2_ready"), pg + 1)
                    for t in range(4):
                        ins = V.tensor_scalar(z2[:, t, :], xs2[:, t, :], rstd2[:, t:t + 1], None, ALU.mult)
                    ins.then_inc(sem("z2_ready"), 1)
                    return
                if part == 2:
                    dve.wait_ge(sem("logits_mm"), pg + 1)
                    st(V.tensor_copy(logits.rearrange("p a b -> p (a b)"), psum[:, 6, 0:4 * NE]))
                    V.memset(done_flags[:, 4:5], 0.0)
                    for t in range(4):
                        ins = V.max(max8[:, t, :], logits[:, t, :])
                    st(ins)
                    V.tensor_tensor(gap.rearrange("p (t a) -> p t a", a=1), max8[:, :, 0:1], max8[:, :, 1:2],
                                    ALU.subtract).then_inc(sem("gap_ready"), 1)
                    for t in range(4):
                        ins = V.max_index(idx8[:, t, :].bitcast(U32), max8[:, t, :], logits[:, t, :])
                    st(ins)
                    st(V.tensor_copy(idxf, idx8[:, :, 0:2].bitcast(U32)))
                    io = iota8.rearrange("p (a e) -> p a e", a=1).broadcast_to([P, 4, NE])
                    for j in range(2):
                        st(V.tensor_tensor(pick[:, j], io, idxf[:, :, j:j + 1].broadcast_to([P, 4, NE]), ALU.is_equal))
                    return
                if part == 4:
                    dve.wait_ge(sem("combT_mm"), pg + 1)
                    V.tensor_copy(combT[:, :], psum[0:3 * NE, 6, 0:256].bitcast(BF16)).then_inc(sem("combT_ready"), 1)
                    return
                st.n = 6
                dve.wait_ge(sem("tanh_ready"), pg + 1)
                st(V.tensor_scalar(c12[:, 0, :], th, 0.5, 0.5, ALU.mult, ALU.add))
                st(V.tensor_scalar(c12[:, 1, :], th, -0.5, 0.5, ALU.mult, ALU.add))
                for j in range(2):
                    cj = c12[:, j, :].rearrange("p (t a) -> p t a", a=1).broadcast_to([P, 4, NE])
                    st(V.tensor_tensor(pick[:, j], pick[:, j], cj, ALU.mult))
                st(V.tensor_tensor(comb, pick[:, 0], pick[:, 1], ALU.add))
                st(V.tensor_copy(comb_parts[:, :, 0:NE], comb))
                st(V.tensor_tensor(rest, comb, comb_parts[:, :, 0:NE], ALU.subtract))
                st(V.tensor_copy(comb_parts[:, :, NE:2 * NE], rest))
                st(V.tensor_tensor(rest, rest, comb_parts[:, :, NE:2 * NE], ALU.subtract))
                V.tensor_copy(comb_parts[:, :, 2 * NE:3 * NE], rest).then_inc(sem("comb_ready"), 1)
                assert st.n == PREP_STEPS, st.n

            def experts(pg, p, par, prep):
                NU = 2 * NE
                for n in range(NU):
                    dve.wait_ge(sem("silu_c_ready"), NU * pg + n + 1)
                    dve.wait_ge(sem("up_mm"), NU * pg + n + 1)
                    V.tensor_tensor(hh[:, n % 3, :], silu_c[:, n % 3, :], psum[:, 2 * (n % 2) + 1, :], ALU.mult) \
                        .then_inc(sem("hh_ready"), 1)
                    if prep and n == 0:
                        prepare(pg + 1, 0, 1 - par)
                    if prep and n == 1:
                        prepare(pg + 1, 1, 1 - par)
                    if prep and n == 5:
                        prepare(pg + 1, 2, 1 - par)
                    if prep and n == 6:
                        prepare(pg + 1, 3, 1 - par)
                    if prep and n == 9:
                        prepare(pg + 1, 4, 1 - par)
                dve.wait_ge(sem("y_tok_mm"), pg + 1)
                xv = x[:, bass.ds(p * 4, 4), :]
                V.tensor_tensor(xv, xv, psum[:, 7, :].rearrange("p (t c) -> p t c", t=4), ALU.add) \
                    .then_inc(sem("y_added"), 1)
                dve.wait_ge(sem("y_added"), 1 + pg + 1)
                V.tensor_scalar(xv, xv, 100.0, -100.0, ALU.min, ALU.max).then_inc(sem("x2_updated"), 1)

            with dve.Fori(0, L) as l:
                phase_done(dve, 2 * l)
                s0 = l * B
                mean_square(s0)
                scale_rows(s0)
                rope(s0, s0 * S_PER)
                copy_v(s0 * S_PER + 5)
                with dve.Fori(0, B - 1) as s:
                    sequence(l * B + s, s, 1)
                sequence(l * B + B - 1, B - 1, 0)
                V.memset(done_flags[:, 2:3], 0.0).then_inc(sem("phase_end"), 1)
                phase_done(dve, 1 + 2 * l)
                for part in range(5):
                    prepare(l * NP_, part, 0)
                with dve.Fori(0, NP_ // 2 - 1) as i:
                    experts(l * NP_ + 2 * i, 2 * i, 0, True)
                    experts(l * NP_ + 2 * i + 1, 2 * i + 1, 1, True)
                experts(l * NP_ + NP_ - 2, NP_ - 2, 0, True)
                experts(l * NP_ + NP_ - 1, NP_ - 1, 1, False)
                V.memset(done_flags[:, 2:3], 0.0).then_inc(sem("phase_end"), 1)
            dve.wait_ge(sem("x2_updated"), L * NP_)
            NQ = B // 4
            for q in range(4):
                xq = seqs(x)[:, q * NQ:(q + 1) * NQ]
                gq = gb_rows[:, q * NQ:(q + 1) * NQ, :].rearrange("p b (a c) -> p b a c", a=1)
                V.tensor_tensor(xq, xq, gq.broadcast_to([P, NQ, ST, C]), ALU.mult).then_inc(sem("gated"), 1)
                dve.wait_ge(sem("gated"), q + 1)
                V.tensor_tensor(seqs(x1)[:, q * NQ:(q + 1) * NQ], seqs(x1)[:, q * NQ:(q + 1) * NQ], xq, ALU.add) \
                    .then_inc(sem("out_ready"), 1)


def kernel(**inputs):
    import concourse.bacc as _bacc
    from concourse.bass_utils import run_bass_kernel_spmd as _run

    nc = _bacc.Bacc("TRN2", target_bir_lowering=False, num_devices=1)
    k, sel_seq, sel_exp = shape_constants()
    given = {n: inputs[n] for n in ("L0_attn_x", "L0_wmod", "L0_attn_norm_gamma", "L0_attn_norm_beta", "L0_ffn_wq",
                                    "L0_ffn_wk", "L0_ffn_wv", "L0_ffn_wo", "L0_ffn_wr", "L0_ffn_wg", "L0_ffn_wu",
                                    "L0_ffn_wd")}
    given["cT"] = np.asarray(inputs["L0_c"]).T
    for n in ("h_filter", "g_filter", "h_synth", "g_synth"):
        given[n + "_T"] = np.asarray(inputs["L0_attn_" + n]).T
    given["ln1_T"] = np.asarray(inputs["L0_ffn_ln1_w"]).T
    given["ln2_T"] = np.asarray(inputs["L0_ffn_ln2_w"]).T
    given.update(consts=k, sel_seq=sel_seq, sel_exp=sel_exp)
    arrays, aps = {}, {}
    for n, a in given.items():
        a = np.ascontiguousarray(a)
        arrays["in_" + n] = a
        aps[n] = nc.dram_tensor("in_" + n, a.shape, mybir.dt.from_np(a.dtype), kind="ExternalInput").ap()
    out = nc.dram_tensor("out_0", (B, S, C), F32, kind="ExternalOutput").ap()
    bass_program(nc, aps, out)
    r = _run(nc, [arrays], core_ids=[0])
    return r.results[0]["out_0"]
```

```python
from contextlib import ExitStack

import numpy as np
import concourse.bass as bass
from concourse import mybir

F32 = mybir.dt.float32
BF16 = mybir.dt.bfloat16
U32 = mybir.dt.uint32
ALU = mybir.AluOpType
ACT = mybir.ActivationFunctionType
AX = mybir.AxisListType.X

P = 128
B, S, C = 16, 256, 128
NT = B * S // P
ST = S // P
L, NH, NKV, HD, FF, NE = 4, 16, 4, 64, 256, 8
TAPS = 4
LH = 8
EPS = 1e-5
ATTN_EPS = 1e-6
NEG = -8.0e9
SCALE = HD ** -0.5
PAIR = 2 * S
NP_ = B * S // PAIR

K_ID, K_MASK, K_COS, K_SIN, K_BD, K_IOTA, K_END = 0, 128, 384, 512, 640, 768, 776


def shape_constants():
    pos = np.arange(S, dtype=np.float32)
    inv = (1.0 / np.float32(10000.0) ** (np.arange(0, HD, 2, dtype=np.float32) / np.float32(HD))).astype(np.float32)
    ang = (pos[:, None] * inv).astype(np.float32)
    emb = np.concatenate([ang, ang], axis=-1)
    cos, sin = np.cos(emb).astype(np.float32), np.sin(emb).astype(np.float32)
    sin[:, :HD // 2] *= -1.0
    k = np.zeros((P, K_END), np.float32)
    k[:, K_ID:K_ID + P] = np.eye(P)
    k[:, K_MASK + P:K_MASK + 2 * P] = np.where(np.tril(np.ones((P, P))) > 0, 0.0, NEG)
    for t in range(ST):
        k[:, K_COS + t * HD:K_COS + (t + 1) * HD] = cos[t * P:(t + 1) * P]
        k[:, K_SIN + t * HD:K_SIN + (t + 1) * HD] = sin[t * P:(t + 1) * P]
    g = np.arange(P) // LH
    k[:, K_BD:K_BD + P] = g[:, None] == g[None, :]
    k[:, K_IOTA:K_IOTA + NE] = np.arange(NE)
    sel_seq = np.repeat(np.eye(B, dtype=np.float32), P, axis=1)
    sel_exp = np.repeat(np.tile(np.eye(NE, dtype=np.float32), (3, 1)), P, axis=1)
    return k, sel_seq, sel_exp


class Arena:

    def __init__(self, tensor, size):
        self.t, self.size, self.at = tensor, size, 0

    def take(self, *shape):
        n = int(np.prod(shape))
        ap = self.t[:, self.at:self.at + n]
        self.at += n
        assert self.at <= self.size, self.at
        if len(shape) == 2:
            ap = ap.rearrange("p (a b) -> p a b", a=shape[0])
        if len(shape) == 3:
            ap = ap.rearrange("p (a b c) -> p a b c", a=shape[0], b=shape[1])
        return ap


def bass_program(nc, I, out):
    ctx = ExitStack()
    with ctx:
        SIZE = 46400
        arena = Arena(ctx.enter_context(nc.sbuf_tensor("arena", [P, SIZE], F32)), SIZE)
        sel_exp = ctx.enter_context(nc.sbuf_tensor("sel_exp", [3 * NE, NE * P], BF16))
        comb_parts = ctx.enter_context(nc.sbuf_tensor("comb_parts", [P, 4, 3 * NE], BF16))
        combT = ctx.enter_context(nc.sbuf_tensor("combT", [3 * NE, PAIR], BF16))
        ident_bf = ctx.enter_context(nc.sbuf_tensor("ident_bf", [P, P], BF16))
        psum = ctx.enter_context(nc.psum_tensor("psum", [P, 8, 512], F32))
        sems = {}

        def sem(name):
            if name not in sems:
                sems[name] = ctx.enter_context(nc.semaphore(name))
            return sems[name]

        x = arena.take(NT, C)
        x1 = arena.take(NT, C)
        gb_rows = arena.take(B, C)
        consts = arena.take(K_END)
        ident = consts[:, K_ID:K_ID + P]
        mask = consts[:, K_MASK:K_MASK + 2 * P]
        blockdiag = consts[:, K_BD:K_BD + P]
        iota8 = consts[:, K_IOTA:K_IOTA + NE]
        lnw = arena.take(2, L)
        lnw_now = arena.take(2)
        minus_half = arena.take(NT)
        wq = arena.take(NH * HD)
        wk = arena.take(NKV * HD)
        wv = arena.take(NKV * HD)
        wo = arena.take(NH // 2, C)
        wr = arena.take(NE)
        done_flags = arena.take(16)
        before_moe_w = arena.at
        wg = arena.take(NE, FF)
        wu = arena.take(NE, FF)
        wd = arena.take(NE, 2, C)
        shared = arena.at

        arena.at = before_moe_w
        cT = arena.take(B)
        scT = arena.take(B)
        wmod = arena.take(6 * C)
        filt = arena.take(4, TAPS)
        fsum = arena.take(2, 3)
        modcol = arena.take(2, B)
        rows = arena.take(5, C)
        rtmp = arena.take(4, C)
        gamma_beta = arena.take(2, C)
        sel_seq = arena.take(B, P)
        row_bc = arena.take(B, 4 * C)
        mean = arena.take(NT)
        var = arena.take(NT)
        rstd0 = arena.take(NT)
        HPW = S + 4
        hp = arena.take(B, HPW)
        low1 = arena.take(B, S // 2 + 4)
        high1 = arena.take(B, S // 2 + 2)
        low2 = arena.take(B, S // 4 + 2)
        high2 = arena.take(B, S // 4 + 2)
        at_q = arena.at
        qf = arena.take(B, S // 4)
        q_tok = arena.take(8, P)
        v_tok = arena.take(8, P)
        kvm = arena.take(B, P)
        zmat = arena.take(B, P)
        zsum = arena.take(B)
        rden = arena.take(B, S // 4)
        syn_v = arena.take(B * S // 4)
        arena.at = at_q
        xc_a = arena.take(NT, C)
        arena.at = at_q
        syn = arena.take(B, S)
        arena.at = at_q
        sq2 = arena.take(NT, C)
        sq = x

        arena.at = shared
        xs = arena.take(ST, C)
        z = arena.take(ST, C)
        junk = arena.take(ST, C)
        ms = arena.take(ST)
        rstd = arena.take(ST)
        hT = arena.take(S)
        rope_a = arena.take(2, 512)
        rope_b = arena.take(2, 512)
        qr = arena.take(ST, NH * HD)
        kr = arena.take(ST, NKV * 2 * HD)
        QT = arena.take(NH // 2, S)
        KT = arena.take(2, NKV, S)
        v = arena.take(ST, NKV * HD)
        probs = arena.take(4, 4, 3 * P)
        rowmax = arena.take(4, 8)
        negmax = arena.take(4, 8)
        rowsum = arena.take(4, 8)
        rinv = arena.take(4, 8)
        probsT = arena.take(8, 3 * P)
        oT = arena.take(NH // 2, S)
        arena.at = shared
        xs2 = arena.take(4, C)
        z2 = arena.take(4, C)
        junk2 = arena.take(4, C)
        ms2 = arena.take(4)
        rstd2 = arena.take(4)
        h2T = arena.take(2, PAIR)
        logits = arena.take(4, NE)
        max8 = arena.take(4, NE)
        idx8 = arena.take(4, NE)
        idxf = arena.take(4, 2)
        gap = arena.take(4)
        th = arena.take(4)
        c12 = arena.take(2, 4)
        pick = arena.take(2, 4, NE)
        comb = arena.take(4, NE)
        rest = arena.take(4, NE)
        comb_bc = arena.take(2, NE, PAIR)
        silu_g = arena.take(3, PAIR)
        silu_c = arena.take(3, PAIR)
        hh = arena.take(3, PAIR)
        yT = arena.take(PAIR)

        block = ctx.enter_context(nc.Block())
        POOL_FROM_ONE = ("rope_done",)
        ACT_FROM_ONE = ("t_free", "yT_copied", "comb_bc_ready")
        DVE_FROM_ONE = ("s_free", "o_free", "z_ready", "y_added", "z2_ready")
        PH = 3

        def phase_done(eng, k):
            eng.wait_ge(sem("phase_end"), PH * (k + 1))

        @block.sync
        def _(sp):
            def load(dst, src, name):
                sp.dma_start(dst, src).then_inc(sem(name), 16)

            load(cT, I["cT"], "c_in")
            load(wmod, I["L0_wmod"], "wmod_in")
            load(consts, I["consts"], "consts_in")
            xv = I["L0_attn_x"].rearrange("b (t p) c -> p (b t) c", p=P)
            for q in range(4):
                load(x1[:, q * 8:(q + 1) * 8, :], xv[:, q * 8:(q + 1) * 8, :], "x_in")
            for q, n in enumerate(["h_filter", "g_filter", "h_synth", "g_synth"]):
                load(filt[:, q, :], I[n + "_T"], "filt_in")
            for q, n in enumerate(["L0_attn_norm_gamma", "L0_attn_norm_beta"]):
                load(gamma_beta[0:B, q, :], I[n].rearrange("(a c) -> a c", a=1).partition_broadcast(B), "rows_in")
            load(sel_seq[0:B].rearrange("p b m -> p (b m)"), I["sel_seq"], "rows_in")
            load(lnw[:, 0, :], I["ln1_T"], "small_in")
            load(lnw[:, 1, :], I["ln2_T"], "small_in")

            def attn_weights(l):
                d = bass.ds(l, 1) if not isinstance(l, int) else slice(l, l + 1)
                sp.dma_start(wq, I["L0_ffn_wq"][d].rearrange("l h n -> (l h) n")).then_inc(sem("wattn_in"), 16)
                sp.dma_start(wk, I["L0_ffn_wk"][d].rearrange("l h n -> (l h) n")).then_inc(sem("wattn_in"), 16)
                sp.dma_start(wv, I["L0_ffn_wv"][d].rearrange("l h n -> (l h) n")).then_inc(sem("wattn_in"), 16)
                sp.dma_start(wo, I["L0_ffn_wo"][d].rearrange("l (c p) n -> (l p) c n", p=P)).then_inc(sem("wattn_in"), 16)

            def moe_weights(l):
                d = bass.ds(l, 1) if not isinstance(l, int) else slice(l, l + 1)
                sp.dma_start(wg, I["L0_ffn_wg"][d].rearrange("l e h f -> (l h) e f")).then_inc(sem("wmoe_in"), 16)
                sp.dma_start(wu, I["L0_ffn_wu"][d].rearrange("l e h f -> (l h) e f")).then_inc(sem("wmoe_in"), 16)
                wdv = I["L0_ffn_wd"][d].rearrange("l e (f p) n -> (l p) e f n", p=P)
                for f in range(2):
                    sp.dma_start(wd[:, :, f, :], wdv[:, :, f, :]).then_inc(sem("wmoe_in"), 16)
                sp.dma_start(wr, I["L0_ffn_wr"][d].rearrange("l h n -> (l h) n")).then_inc(sem("wmoe_in"), 16)

            attn_weights(0)
            phase_done(sp, 0)
            moe_weights(0)
            with sp.Fori(0, L - 1) as l:
                phase_done(sp, 1 + 2 * l)
                attn_weights(l + 1)
                phase_done(sp, 2 + 2 * l)
                moe_weights(l + 1)
            ov = out.rearrange("b (t p) c -> p (b t) c", p=P)
            for q in range(4):
                sp.wait_ge(sem("out_ready"), q + 1)
                sp.dma_start(ov[:, q * 8:(q + 1) * 8, :], x1[:, q * 8:(q + 1) * 8, :]).then_inc(sem("out_written"), 16)
            sp.wait_ge(sem("out_written"), 64)

        N_ATTN_W, N_MOE_W = 4 * 16, 5 * 16

        S_BANK, T_BANK, O_BANK = 0, 4, 7

        S_PER, T_PER = NH + 7, NH + 7
        S_HEAD = {0: 0, 1: 4, 2: 10, 3: 19}
        S_V, S_OUT, S_QK, S_END = 8, 9, 14, 23
        T_OLD, T_H, T_NEW, T_QK = {2: 0, 3: 4}, 8, {0: 9, 1: 13}, 17
        T_LAST = {0: 8, 1: 12, 2: 16, 3: 20}

        S_FIRST = S_END - 5

        def s_place(k, last):
            return k - 5 if last and k >= S_QK else k

        def s_bank(k):
            return S_BANK + k % 4

        def s_index(sg, k, first=False):
            return sg * S_PER + (5 if first and k < S_OUT else 4) + k

        def s_waited(sg, k, first=False, last=False):
            lag = 3 if k < 3 or (first and k > S_OUT) else 4
            return s_index(sg, k, first) - lag + 1

        def t_index(sg, k):
            return sg * T_PER - 1 + k

        def t_waited(n, k):
            return n - (1 if k < 2 else 2)

        def t_turned(sg, first):
            return sg * T_PER + 7 if first else t_index(sg, 0)

        def t_bank(k):
            return T_BANK + k % 3

        @block.tensor
        def _(pe):
            T = nc.tensor
            pe.wait_ge(sem("silu_c"), 1)
            pe.wait_ge(sem("wmod_in"), 16)
            for j in range(2):
                T.matmul(psum[:, 0, j * B:(j + 1) * B], wmod[:, j * C:(j + 1) * C], scT, start=True, stop=True)
            T.matmul(psum[0:B, 1, :], scT, wmod[:, 2 * C:6 * C], start=True, stop=True).then_inc(sem("mod_mm"), 1)
            pe.wait_ge(sem("rows_ready"), 1)
            pe.wait_ge(sem("rows_in"), 48)
            for b in range(B):
                if b >= 4:
                    pe.wait_ge(sem("rowbc_copied"), b - 3)
                T.matmul(psum[:, 4 + b % 4, :], sel_seq[0:B, b, :], rows[0:B, 0:4, :].rearrange("p a c -> p (a c)"),
                         start=True, stop=True).then_inc(sem("rowbc_mm"), 1)
            for q in range(4):
                pe.wait_ge(sem("rowbc_copied"), B - 3 + q)
                for j in range(4):
                    mm = T.matmul(psum[:, 4 + q, j * C:(j + 1) * C], sel_seq[0:B, 4 * q + j, :], rows[0:B, 4, :],
                                  start=True, stop=True)
                mm.then_inc(sem("rowbc_mm"), 1)
            pe.wait_ge(sem("consts_in"), 16)
            pe.wait_ge(sem("xc_ready"), 1)
            for b in range(B):
                if b < 2:
                    pe.wait_ge(sem("mod_copied"), 1)
                if b >= 2:
                    pe.wait_ge(sem("hp_ready"), b - 1)
                for t in range(ST):
                    mm = T.transpose(psum[:, b % 2, t * P:(t + 1) * P], xc_a[:, b * ST + t, :], ident)
                mm.then_inc(sem("xcT_mm"), 1)
            pe.wait_ge(sem("qf_ready"), 1)
            for g in range(8):
                T.transpose(psum[:, 2 + g // 4, (g % 4) * P:(g % 4 + 1) * P],
                            qf[:, 2 * g:2 * g + 2, :].rearrange("p b n -> p (b n)"), ident)
            pe.wait_ge(sem("rowbc_copied"), B + 4)
            pe.wait_ge(sem("lowc_ready"), 1)
            for g in range(8):
                mm = T.transpose(psum[:, 4 + g // 4, (g % 4) * P:(g % 4 + 1) * P],
                                 syn_v[:, g * P:(g + 1) * P], ident)
            mm.then_inc(sem("qv_tok_mm"), 1)
            pe.wait_ge(sem("qv_tok_ready"), 1)
            for b in range(B):
                r = slice(64 * (b % 2), 64 * (b % 2) + 64)
                bank = [6, 7][b // 8] if b % 2 == 0 else [0, 1][b // 8]
                mm = T.matmul(psum[:, bank, (b // 2 % 4) * P:(b // 2 % 4 + 1) * P], q_tok[r, b // 2, :], v_tok[r, b // 2, :],
                              start=True, stop=True)
            mm.then_inc(sem("kv_mm"), 1)
            pe.wait_ge(sem("kvz_ready"), 1)
            for b in range(B):
                T.matmul(psum[:, 2 + b // 8, (b % 8) * 64:(b % 8 + 1) * 64], kvm[:, b, :], qf[:, b, :],
                         start=True, stop=True)
            for b in range(B):
                mm = T.matmul(psum[:, 4 + b // 8, (b % 8) * 64:(b % 8 + 1) * 64], zmat[:, b, :], qf[:, b, :],
                              start=True, stop=True)
            mm.then_inc(sem("numden_mm"), 1)
            for b in range(B):
                pe.wait_ge(sem("syn_ready"), 1)
                if b >= 4:
                    pe.wait_ge(sem("yt_copied"), b - 3)
                bank = [0, 1, 6, 7][b % 4]
                for t in range(ST):
                    mm = T.transpose(psum[:, bank, t * P:(t + 1) * P], syn[:, b, t * P:(t + 1) * P], ident)
                mm.then_inc(sem("yt_mm"), 1)

            def scores(sg, q, first, last):
                if q == 0:
                    pe.wait_ge(sem("t_free"), 1 + t_turned(sg, first))
                for i in range(4):
                    k = s_place(S_HEAD[q] + i, last)
                    pe.wait_ge(sem("s_free"), 1 + s_waited(sg, k, first))
                    c, bank = (4 * q + i) // 2, s_bank(k)
                    T.matmul(psum[:, bank, 0:P], QT[:, c, 0:P], KT[:, i % 2, q, 0:P], start=True, stop=True)
                    T.matmul(psum[:, bank, P:3 * P], QT[:, c, P:2 * P], KT[:, i % 2, q, :],
                             start=True, stop=True).then_inc(sem("s_full"), 1)

            def attend(qg, q, n, k, first=False):
                pe.wait_ge(sem("probs_ready"), qg + 1)
                pe.wait_ge(sem("o_free"), 1 + qg)
                for i in range(4):
                    pe.wait_ge(sem("t_free"), 1 + t_waited(n + i, k + i))
                    for j in range(3):
                        mm = T.transpose(psum[:, t_bank(k + i), j * P:(j + 1) * P],
                                         probs[:, q, i, j * P:(j + 1) * P], ident)
                    mm.then_inc(sem("t_full"), 1)
                    if i >= 2:
                        weigh(q, i - 2, n)
                weigh(q, 2, n)
                weigh(q, 3, n).then_inc(sem("o_full"), 1)

            def weigh(q, i, n):
                pe.wait_ge(sem("t_free"), 1 + n + i + 1)
                r = slice(64 * (i % 2), 64 * (i % 2) + 64)
                c0 = 256 * (i // 2)
                pt = probsT[:, 4 * (q % 2) + i, :]
                T.matmul(psum[r, O_BANK, c0:c0 + S], v[:, 0, q * HD:(q + 1) * HD], pt[:, 0:S],
                         start=True, stop=False, skip_group_check=True)
                return T.matmul(psum[r, O_BANK, c0 + P:c0 + S], v[:, 1, q * HD:(q + 1) * HD], pt[:, S:S + P],
                                start=False, stop=True, skip_group_check=True)

            def turn_h(sg, n, k, started):
                pe.wait_ge(sem("z_ready"), 1 + sg + 1)
                if started:
                    pe.wait_ge(sem("t_free"), 1 + t_waited(n, k))
                for t in range(ST):
                    mm = T.transpose(psum[:, t_bank(k), t * P:(t + 1) * P], z[:, t, :], ident)
                mm.then_inc(sem("t_full"), 1)

            def project_qk(h_n, n, k0, first):
                pe.wait_ge(sem("t_free"), 1 + h_n + 1)
                for u in range(5):
                    if not (first and u < 4):
                        pe.wait_ge(sem("s_free"), 1 + n + u - 3)
                    bank = s_bank(k0 + u)
                    if u < 4:
                        t, half = u // 2, u % 2
                        mm = T.matmul(psum[:, bank, :], hT[:, t * P:(t + 1) * P], wq[:, half * 512:(half + 1) * 512],
                                      start=True, stop=True)
                    else:
                        for t in range(ST):
                            mm = T.matmul(psum[:, bank, t * 256:(t + 1) * 256], hT[:, t * P:(t + 1) * P], wk,
                                          start=True, stop=True)
                    mm.then_inc(sem("s_full"), 1)

            def project_v(sg, first):
                pe.wait_ge(sem("s_free"), 1 + s_waited(sg, S_V, first))
                for t in range(ST):
                    mm = T.matmul(psum[:, s_bank(S_V), t * 256:(t + 1) * 256], hT[:, t * P:(t + 1) * P], wv,
                                  start=True, stop=True)
                mm.then_inc(sem("s_full"), 1)

            def turn_qk(sg, n, k0, first=False):
                for u in range(6):
                    if u == 0:
                        pe.wait_ge(sem("rope_done"), 1 + 5 * sg + 4)
                    if u == 4:
                        pe.wait_ge(sem("rope_done"), 1 + 5 * sg + 5)
                    if u >= 2 or not first:
                        pe.wait_ge(sem("t_free"), 1 + n + u - 2)
                    for i in range(2):
                        for t in range(ST):
                            if u < 4:
                                src = qr[:, t, (2 * u + i) * P:(2 * u + i + 1) * P]
                            else:
                                src = kr[:, t, (2 * (u - 4) + i) * P:(2 * (u - 4) + i + 1) * P]
                            mm = T.transpose(psum[:, t_bank(k0 + u), (2 * i + t) * P:(2 * i + t + 1) * P],
                                             src, ident)
                    mm.then_inc(sem("t_full"), 1)

            def project_out(sg, k, waited):
                pe.wait_ge(sem("o_free"), 1 + 4 * sg + 4)
                pe.wait_ge(sem("s_free"), 1 + waited)
                for t in range(ST):
                    for c in range(NH // 2):
                        mm = T.matmul(psum[:, s_bank(k), t * P:(t + 1) * P], oT[:, c, t * P:(t + 1) * P], wo[:, c, :],
                                      start=(c == 0), stop=(c == NH // 2 - 1))
                mm.then_inc(sem("s_full"), 1)

            def sequence(sg, first, last):
                n = t_index(sg, 0)
                new = T_LAST if last else T_NEW
                scores(sg, 0, first, last)
                if not first:
                    attend(4 * sg - 2, 2, n + T_OLD[2], T_OLD[2])
                scores(sg, 1, first, last)
                if not first:
                    attend(4 * sg - 1, 3, n + T_OLD[3], T_OLD[3])
                project_v(sg, first)
                if not first:
                    project_out(sg - 1, S_OUT, s_waited(sg, S_OUT))
                if not last:
                    turn_h(sg + 1, n + T_H, T_H, True)
                scores(sg, 2, first, last)
                if not last:
                    project_qk(n + T_H, s_index(sg, S_QK), S_QK, False)
                attend(4 * sg, 0, n + new[0], new[0])
                scores(sg, 3, first, last)
                attend(4 * sg + 1, 1, n + new[1], new[1])
                if not last:
                    turn_qk(sg + 1, n + T_QK, T_QK)
                else:
                    for q in (2, 3):
                        attend(4 * sg + q, q, n + T_LAST[q], T_LAST[q])
                    k = s_place(S_END, True)
                    project_out(sg, k, s_waited(sg, k))

            PREP_AT_PE = {2: 0, 4: 1, 8: 2, 9: 3, 10: 4, 11: 5, 12: 6, 13: 7, 14: 8, 15: 9}

            def prepare(pg, step, par):
                if step == 0:
                    pe.wait_ge(sem("z2_ready"), 1 + pg + 1)
                    pe.wait_ge(sem("comb_bc_ready"), 1 + NE * pg)
                    for t in range(4):
                        mm = T.transpose(psum[:, 5, t * P:(t + 1) * P], z2[:, t, :], ident)
                    mm.then_inc(sem("h2T_mm"), 1)
                if step == 1:
                    pe.wait_ge(sem("h2T_ready"), pg + 1)
                    for t in range(4):
                        mm = T.matmul(psum[:, 6, t * NE:(t + 1) * NE], h2T[:, par, t * P:(t + 1) * P], wr,
                                      start=True, stop=True)
                    mm.then_inc(sem("logits_mm"), 1)
                if step == 2:
                    pe.wait_ge(sem("comb_ready"), pg + 1)
                    for t in range(4):
                        mm = T.transpose(psum[0:3 * NE, 6, t * 64:(t + 1) * 64].bitcast(BF16), comb_parts[:, t, :],
                                         ident_bf[:, :])
                    mm.then_inc(sem("combT_mm"), 1)
                if step >= 3:
                    e = step - 3
                    if e == 0:
                        pe.wait_ge(sem("combT_ready"), pg + 1)
                    else:
                        pe.wait_ge(sem("comb_bc_ready"), 1 + NE * pg + e - 1)
                    T.matmul(psum[:, 5 + e % 2, :], sel_exp[:, e * P:(e + 1) * P], combT[:, :],
                             start=True, stop=True).then_inc(sem("comb_bc_mm"), 1)

            def experts(pg, par, prep):
                NU = 2 * NE

                def down(n):
                    e, f = n // 2, n % 2
                    pe.wait_ge(sem("hh_ready"), NU * pg + n + 1)
                    mm = T.matmul(psum[:, 4, :], wd[:, e, f, :], hh[:, n % 3, :], start=(n == 0), stop=(n == NU - 1),
                                  skip_group_check=True)
                    if n == NU - 1:
                        mm.then_inc(sem("y_mm"), 1)
                    else:
                        mm.then_inc(sem("down_mm"), 1)

                pe.wait_ge(sem("yT_copied"), 1 + pg)
                for n in range(NU):
                    e, f = n // 2, n % 2
                    if n >= 2:
                        pe.wait_ge(sem("hh_ready"), NU * pg + n - 1)
                    T.matmul(psum[:, 2 * (n % 2), :], wg[:, e, f * P:(f + 1) * P], h2T[:, par, :],
                             start=True, stop=True).then_inc(sem("gate_mm"), 1)
                    T.matmul(psum[:, 2 * (n % 2) + 1, :], wu[:, e, f * P:(f + 1) * P], h2T[:, par, :],
                             start=True, stop=True).then_inc(sem("up_mm"), 1)
                    if n >= 1:
                        down(n - 1)
                    if prep and n in PREP_AT_PE:
                        prepare(pg + 1, PREP_AT_PE[n], 1 - par)
                if prep:
                    prepare(pg + 1, 2 + NE, 1 - par)
                down(NU - 1)
                pe.wait_ge(sem("yT_copied"), 1 + pg + 1)
                pe.wait_ge(sem("y_added"), 1 + pg)
                for t in range(4):
                    mm = T.transpose(psum[:, 7, t * P:(t + 1) * P], yT[:, t * P:(t + 1) * P], ident)
                mm.then_inc(sem("y_tok_mm"), 1)

            with pe.Fori(0, L) as l:
                phase_done(pe, 2 * l)
                pe.wait_ge(sem("wattn_in"), N_ATTN_W * (l + 1))
                s0 = l * B
                pe.wait_ge(sem("k_zeroed"), l + 1)
                turn_h(s0, s0 * T_PER, T_QK - 1, False)
                project_qk(s0 * T_PER, s0 * S_PER, S_FIRST, True)
                turn_qk(s0, s0 * T_PER + 1, T_QK, True)
                sequence(s0, True, False)
                with pe.Fori(1, B - 1) as s:
                    sequence(l * B + s, False, False)
                sequence(s0 + B - 1, False, True)
                phase_done(pe, 1 + 2 * l)
                pe.wait_ge(sem("wmoe_in"), N_MOE_W * (l + 1))
                for step in range(11):
                    prepare(l * NP_, step, 0)
                with pe.Fori(0, NP_ // 2 - 1) as i:
                    experts(l * NP_ + 2 * i, 0, True)
                    experts(l * NP_ + 2 * i + 1, 1, True)
                experts(l * NP_ + NP_ - 2, 0, True)
                experts(l * NP_ + NP_ - 1, 1, False)

        @block.scalar
        def _(act):
            A = nc.scalar
            act.wait_ge(sem("pool_const"), 2)
            for name in ACT_FROM_ONE:
                A.copy(done_flags[:, 0:1], done_flags[:, 5:6]).then_inc(sem(name), 1)
                act.wait_ge(sem(name), 1)
            act.wait_ge(sem("c_in"), 16)
            A.activation(scT, cT, ACT.Silu).then_inc(sem("silu_c"), 1)
            for b in range(B):
                act.wait_ge(sem("rowbc_mm"), b + 1)
                A.copy(row_bc[:, b, :], psum[:, 4 + b % 4, :]).then_inc(sem("rowbc_copied"), 1)
            for q in range(4):
                act.wait_ge(sem("rowbc_mm"), B + q + 1)
                A.copy(gb_rows[:, 4 * q:4 * q + 4, :].rearrange("p b c -> p (b c)"), psum[:, 4 + q, :]) \
                    .then_inc(sem("rowbc_copied"), 1)
            act.wait_ge(sem("centred"), 1)
            A.activation(sq, xc_a, ACT.Square).then_inc(sem("squared"), 1)
            act.wait_ge(sem("hp_zeroed"), 1)
            for b in range(B):
                act.wait_ge(sem("xcT_mm"), b + 1)
                A.activation(hp[:, b, 1:S + 1], psum[:, b % 2, 0:S], ACT.Identity, bias=modcol[:, 0, b:b + 1],
                             scale=modcol[:, 1, b:b + 1]).then_inc(sem("hp_ready"), 1)
            act.wait_ge(sem("qmin_ready"), 1)
            A.activation(rden, rden, ACT.Exp).then_inc(sem("qexp_ready"), 1)
            act.wait_ge(sem("qv_tok_mm"), 1)
            for h in range(2):
                A.copy(v_tok[:, 4 * h:4 * h + 4, :].rearrange("p a b -> p (a b)"), psum[:, 4 + h, :]) \
                    .then_inc(sem("v_tok_ready"), 1)
            for b in range(B):
                act.wait_ge(sem("yt_mm"), b + 1)
                A.copy(x[:, ST * b:ST * b + ST, :].rearrange("p a b -> p (a b)"),
                       psum[:, [0, 1, 6, 7][b % 4], 0:S]).then_inc(sem("yt_copied"), 1)
            act.wait_ge(sem("centred"), 2)
            A.activation(sq2, x, ACT.Square).then_inc(sem("squared"), 1)
            act.wait_ge(sem("centred"), 3)
            A.activation(sq2, x, ACT.Square).then_inc(sem("squared"), 1)
            A.copy(done_flags[:, 0:1], done_flags[:, 5:6]).then_inc(sem("phase_end"), 1)

            def exps(qg, q):
                act.wait_ge(sem("negmax_ready"), qg + 1)
                for k in range(8):
                    i, t = k // 2, k % 2
                    a = probs[:, q, i, 0:P] if t == 0 else probs[:, q, i, P:3 * P]
                    ins = A.activation(a, a, ACT.Exp, bias=negmax[:, q, k:k + 1], accum_out=rowsum[:, q, k:k + 1])
                ins.then_inc(sem("exp_done"), 1)

            def copy_probs(q, n, k):
                for i in range(4):
                    act.wait_ge(sem("t_full"), n + i + 1)
                    A.copy(probsT[:, 4 * (q % 2) + i, :], psum[:, t_bank(k + i), 0:3 * P]).then_inc(sem("t_free"), 1)

            def copy_h(n, k):
                act.wait_ge(sem("t_full"), n + 1)
                A.mul(hT, psum[:, t_bank(k), 0:S], lnw_now[:, 0:1]).then_inc(sem("t_free"), 1)

            def copy_qk(n, k):
                for u in range(6):
                    act.wait_ge(sem("t_full"), n + u + 1)
                    src = psum[:, t_bank(k + u), :]
                    if u < 4:
                        ins = A.copy(QT[:, 2 * u:2 * u + 2, :].rearrange("p a b -> p (a b)"), src)
                    else:
                        for h in range(2):
                            r = slice(64 * h, 64 * h + 64)
                            ins = A.copy(KT[r, h, 2 * (u - 4):2 * (u - 4) + 2, :].rearrange("p a b -> p (a b)"),
                                         src[r])
                    ins.then_inc(sem("t_free"), 1)

            def sequence(sg, first, last):
                n = t_index(sg, 0)
                new = T_LAST if last else T_NEW
                if not first:
                    copy_probs(2, n + T_OLD[2], T_OLD[2])
                exps(4 * sg, 0)
                if not first:
                    copy_probs(3, n + T_OLD[3], T_OLD[3])
                exps(4 * sg + 1, 1)
                if not last:
                    copy_h(n + T_H, T_H)
                copy_probs(0, n + new[0], new[0])
                exps(4 * sg + 2, 2)
                copy_probs(1, n + new[1], new[1])
                if not last:
                    copy_qk(n + T_QK, T_QK)
                exps(4 * sg + 3, 3)
                if last:
                    for q in (2, 3):
                        copy_probs(q, n + T_LAST[q], T_LAST[q])

            PREP_AT_ACT = {3: 0, 6: 1, 10: 3, 11: 4, 12: 5, 13: 6, 14: 7, 15: 8}

            def prepare(pg, step, par):
                if step == 0:
                    act.wait_ge(sem("h2T_mm"), pg + 1)
                    A.mul(h2T[:, par, :], psum[:, 5, :], lnw_now[:, 1:2]).then_inc(sem("h2T_ready"), 1)
                if step == 1:
                    act.wait_ge(sem("gap_ready"), pg + 1)
                    A.activation(th, gap, ACT.Tanh, scale=0.5).then_inc(sem("tanh_ready"), 1)
                if step >= 3:
                    e = step - 3
                    act.wait_ge(sem("comb_bc_mm"), NE * pg + e + 1)
                    A.copy(comb_bc[:, par, e, :], psum[:, 5 + e % 2, :]).then_inc(sem("comb_bc_ready"), 1)

            def experts(pg, par, prep):
                NU = 2 * NE
                for n in range(NU):
                    act.wait_ge(sem("gate_mm"), NU * pg + n + 1)
                    if n >= 3:
                        act.wait_ge(sem("silu_c_ready"), NU * pg + n - 2)
                    A.activation(silu_g[:, n % 3, :], psum[:, 2 * (n % 2), :], ACT.Silu).then_inc(sem("silu_ready"), 1)
                    if prep and n in PREP_AT_ACT:
                        prepare(pg + 1, PREP_AT_ACT[n], 1 - par)
                if prep:
                    prepare(pg + 1, 3 + NE - 2, 1 - par)
                    prepare(pg + 1, 3 + NE - 1, 1 - par)
                act.wait_ge(sem("y_mm"), pg + 1)
                act.wait_ge(sem("y_added"), 1 + pg)
                A.copy(yT, psum[:, 4, :]).then_inc(sem("yT_copied"), 1)

            with act.Fori(0, L) as l:
                phase_done(act, 2 * l)
                s0 = l * B
                copy_h(s0 * T_PER, T_QK - 1)
                copy_qk(s0 * T_PER + 1, T_QK)
                sequence(s0, True, False)
                with act.Fori(1, B - 1) as s:
                    sequence(l * B + s, False, False)
                sequence(s0 + B - 1, False, True)
                A.copy(done_flags[:, 0:1], done_flags[:, 5:6]).then_inc(sem("phase_end"), 1)
                phase_done(act, 1 + 2 * l)
                for step in range(11):
                    prepare(l * NP_, step, 0)
                with act.Fori(0, NP_ // 2 - 1) as i:
                    experts(l * NP_ + 2 * i, 0, True)
                    experts(l * NP_ + 2 * i + 1, 1, True)
                experts(l * NP_ + NP_ - 2, 0, True)
                experts(l * NP_ + NP_ - 1, 1, False)
                A.copy(done_flags[:, 0:1], done_flags[:, 5:6]).then_inc(sem("phase_end"), 1)

        @block.gpsimd
        def _(pool):
            G = nc.gpsimd
            G.dma_start(sel_exp[:, :], I["sel_exp"]).then_inc(sem("sel_exp_in"), 16)
            G.memset(minus_half, -0.5).then_inc(sem("pool_const"), 1)
            G.memset(done_flags[:, 5:8], 0.0).then_inc(sem("pool_const"), 1)
            pool.wait_ge(sem("pool_const"), 2)
            for name in POOL_FROM_ONE:
                G.memset(done_flags[:, 1:2], 0.0).then_inc(sem(name), 1)
                pool.wait_ge(sem(name), 1)
            for n in range(3):
                pool.wait_ge(sem("var_ready"), n + 1)
                G.tensor_tensor(rstd0, var, minus_half, ALU.pow).then_inc(sem("rstd0_ready"), 1)
            pool.wait_ge(sem("sel_exp_in"), 16)
            G.memset(done_flags[:, 1:2], 0.0).then_inc(sem("phase_end"), 1)

            def load_x(sg, s):
                pool.wait_ge(sem("z_ready"), 1 + sg)
                G.tensor_tensor(done_flags[:, 6:7], done_flags[:, 7:8], done_flags[:, 7:8], ALU.add)
                G.tensor_copy(xs, x[:, bass.ds(s * ST, ST), :]).then_inc(sem("xs_ready"), 1)

            def root(sg):
                pool.wait_ge(sem("ms_ready"), sg + 1)
                G.tensor_tensor(rstd, ms, minus_half[:, 0:ST], ALU.pow).then_inc(sem("rstd_ready"), 1)

            def normalise(qg, q):
                pool.wait_ge(sem("rinv_ready"), qg + 1)
                r = rinv[:, q, :].rearrange("p (i t) -> p i t", t=2)
                for t in range(2):
                    a = probs[:, q, :, 0:P] if t == 0 else probs[:, q, :, P:3 * P]
                    ins = G.tensor_tensor(a, a, r[:, :, t:t + 1].broadcast_to([P, 4, P * (t + 1)]), ALU.mult)
                ins.then_inc(sem("probs_ready"), 1)

            def rope_adds(sg):
                for u in range(5):
                    pool.wait_ge(sem("rope_parts"), 5 * sg + u + 1)
                    a, b = rope_a[:, u % 2, :], rope_b[:, u % 2, :]
                    if u < 4:
                        G.tensor_tensor(qr[:, u // 2, (u % 2) * 512:(u % 2 + 1) * 512], a, b, ALU.add) \
                            .then_inc(sem("rope_done"), 1)
                    else:
                        for t in range(ST):
                            for d in range(2):
                                dst = kr[:, t, :].rearrange("p (j d e) -> p j d e", j=NKV, d=2)[:, :, d, :]
                                ins = G.tensor_tensor(
                                    dst, a[:, t * 256:(t + 1) * 256].rearrange("p (j e) -> p j e", j=NKV),
                                    b[:, t * 256:(t + 1) * 256].rearrange("p (j e) -> p j e", j=NKV), ALU.add)
                        ins.then_inc(sem("rope_done"), 1)

            def sequence(sg, s, first, last):
                if not last:
                    load_x(sg + 1, s + 1)
                if not first:
                    normalise(4 * sg - 1, 3)
                if not last:
                    root(sg + 1)
                normalise(4 * sg, 0)
                normalise(4 * sg + 1, 1)
                if not last:
                    rope_adds(sg + 1)
                normalise(4 * sg + 2, 2)
                if last:
                    normalise(4 * sg + 3, 3)

            def prepare(pg, p, step):
                if step == 0:
                    pool.wait_ge(sem("z2_ready"), 1 + pg)
                    G.tensor_tensor(done_flags[:, 6:7], done_flags[:, 7:8], done_flags[:, 7:8], ALU.add)
                    G.tensor_copy(xs2, x[:, bass.ds(p * 4, 4), :]).then_inc(sem("xs2_ready"), 1)
                if step == 1:
                    pool.wait_ge(sem("ms2_ready"), pg + 1)
                    G.tensor_tensor(rstd2, ms2, minus_half[:, 0:4], ALU.pow).then_inc(sem("rstd2_ready"), 1)

            def experts(pg, p, par, prep):
                NU = 2 * NE
                for n in range(NU):
                    if prep and n == 0:
                        prepare(pg + 1, p + 1, 0)
                    if n == 0:
                        pool.wait_ge(sem("comb_bc_ready"), 1 + NE * (pg + 1))
                    pool.wait_ge(sem("silu_ready"), NU * pg + n + 1)
                    if n >= 3:
                        pool.wait_ge(sem("hh_ready"), NU * pg + n - 2)
                    G.tensor_tensor(silu_c[:, n % 3, :], silu_g[:, n % 3, :], comb_bc[:, par, n // 2, :], ALU.mult) \
                        .then_inc(sem("silu_c_ready"), 1)
                    if prep and n == 0:
                        prepare(pg + 1, p + 1, 1)

            with pool.Fori(0, L) as l:
                phase_done(pool, 2 * l)
                pool.wait_ge(sem("small_in"), 32)
                for j in range(2):
                    ins = G.tensor_copy(lnw_now[:, j:j + 1], lnw[:, j, bass.ds(l, 1)])
                s0 = l * B
                load_x(s0, 0)
                root(s0)
                rope_adds(s0)
                sequence(s0, 0, True, False)
                with pool.Fori(1, B - 1) as s:
                    sequence(l * B + s, s, False, False)
                sequence(s0 + B - 1, B - 1, False, True)
                G.memset(done_flags[:, 1:2], 0.0).then_inc(sem("phase_end"), 1)
                phase_done(pool, 1 + 2 * l)
                prepare(l * NP_, 0, 0)
                prepare(l * NP_, 0, 1)
                with pool.Fori(0, NP_ // 2 - 1) as i:
                    experts(l * NP_ + 2 * i, 2 * i, 0, True)
                    experts(l * NP_ + 2 * i + 1, 2 * i + 1, 1, True)
                experts(l * NP_ + NP_ - 2, NP_ - 2, 0, True)
                experts(l * NP_ + NP_ - 1, NP_ - 1, 1, False)
                G.memset(done_flags[:, 1:2], 0.0).then_inc(sem("phase_end"), 1)

        @block.vector
        def _(dve):
            V = nc.vector

            class Steps:

                def __init__(self, base):
                    self.base, self.n = base, 0

                def __call__(self, ins):
                    ins.then_inc(sem("dve_step"), 1)
                    self.n += 1
                    dve.wait_ge(sem("dve_step"), self.base + self.n)

            step = Steps(0)
            D = S // 4
            for name in DVE_FROM_ONE:
                V.memset(done_flags[:, 2:3], 0.0).then_inc(sem(name), 1)
                dve.wait_ge(sem(name), 1)
            step(V.memset(hp, 0.0))
            step(V.memset(low1, 0.0))
            step(V.memset(high1, 0.0))
            step(V.memset(high2, 0.0))
            V.memset(low2, 0.0).then_inc(sem("hp_zeroed"), 1)
            dve.wait_ge(sem("hp_zeroed"), 1)
            dve.wait_ge(sem("consts_in"), 16)
            step(V.tensor_copy(ident_bf[:, :], ident))
            dve.wait_ge(sem("mod_mm"), 1)
            dve.wait_ge(sem("rows_in"), 48)
            step(V.tensor_copy(modcol[:, 0, :], psum[:, 0, 0:B]))
            step(V.tensor_scalar(modcol[:, 1, :], psum[:, 0, B:2 * B], 1.0, None, ALU.add))
            rt = rtmp[0:B]
            rw = rows[0:B]
            for src, dst in ((0, rt[:, 2, :]), (3, rw[:, 4, :])):
                g = psum[0:B, 1, src * C:(src + 1) * C]
                step(V.tensor_copy(rt[:, 3, :], g))
                step(V.scalar_tensor_tensor(rt[:, 0, :], rt[:, 3, :], -1.0, rt[:, 3, :], ALU.mult, ALU.max))
                step(V.tensor_scalar(rt[:, 0, :], rt[:, 0, :], 0.25, None, ALU.max))
                step(V.tensor_scalar(rt[:, 1, :], rt[:, 3, :], 0.0, 2.0, ALU.is_ge, ALU.mult))
                step(V.scalar_tensor_tensor(dst, rt[:, 1, :], -1.0, rt[:, 0, :], ALU.add, ALU.mult))
            step(V.tensor_tensor(rw[:, 0, :], rt[:, 2, :], gamma_beta[0:B, 0, :], ALU.mult))
            step(V.tensor_tensor(rw[:, 1, :], rt[:, 2, :], gamma_beta[0:B, 1, :], ALU.mult))
            step(V.tensor_scalar(rw[:, 2, :], psum[0:B, 1, 2 * C:3 * C], 1.0, None, ALU.add))
            V.tensor_copy(rw[:, 3, :], psum[0:B, 1, C:2 * C]).then_inc(sem("rows_ready"), 1)
            V.memset(done_flags[:, 3:4], 0.0).then_inc(sem("mod_copied"), 1)
            dve.wait_ge(sem("mod_copied"), 1)
            dve.wait_ge(sem("rows_ready"), 1)

            def per_row(a):
                return a.rearrange("p (t a) -> p t a", a=1).broadcast_to([P, NT, C])

            def layer_norm(src, dst, squares, n, wait_src):
                wait_src()
                step(V.tensor_reduce(mean, src, AX, ALU.add))
                step(V.tensor_scalar(mean, mean, 1.0 / C, None, ALU.mult))
                V.tensor_tensor(dst, src, per_row(mean), ALU.subtract).then_inc(sem("centred"), 1)
                dve.wait_ge(sem("squared"), n + 1)
                step(V.tensor_reduce(var, squares, AX, ALU.add))
                V.tensor_scalar(var, var, 1.0 / C, EPS, ALU.mult, ALU.add).then_inc(sem("var_ready"), 1)
                dve.wait_ge(sem("rstd0_ready"), n + 1)

            layer_norm(x1, xc_a, sq, 0, lambda: dve.wait_ge(sem("x_in"), 64))
            V.tensor_tensor(xc_a, xc_a, per_row(rstd0), ALU.mult).then_inc(sem("xc_ready"), 1)
            dve.wait_ge(sem("filt_in"), 64)
            dve.wait_ge(sem("hp_ready"), B)

            def analyse(src, dst, f, n):
                for k in range(TAPS):
                    a = src[:, :, k:k + 2 * n - 1:2]
                    tap = filt[:, f, k:k + 1]
                    if k == 0:
                        step(V.tensor_scalar(dst, a, tap, None, ALU.mult))
                    else:
                        step(V.scalar_tensor_tensor(dst, a, tap, dst, ALU.mult, ALU.add))

            analyse(hp, low1[:, :, 1:1 + S // 2], 0, S // 2)
            analyse(hp, high1[:, :, 1:1 + S // 2], 1, S // 2)
            analyse(low1, low2[:, :, 1:1 + D], 0, D)
            analyse(low1, high2[:, :, 1:1 + D], 1, D)
            lc = low2[:, :, 1:1 + D]
            step(V.tensor_copy(syn_v.rearrange("p (b n) -> p b n", b=B), lc))
            V.tensor_scalar(rden, lc, 0.0, None, ALU.min).then_inc(sem("qmin_ready"), 1)
            dve.wait_ge(sem("qexp_ready"), 1)
            V.scalar_tensor_tensor(qf, lc, 0.0, rden, ALU.max, ALU.add).then_inc(sem("qf_ready"), 1)
            V.memset(done_flags[:, 3:4], 0.0).then_inc(sem("lowc_ready"), 1)
            dve.wait_ge(sem("qf_ready"), 1)
            step(V.tensor_reduce(zsum, qf, AX, ALU.add))
            dve.wait_ge(sem("qv_tok_mm"), 1)
            for h in range(2):
                step(V.tensor_copy(q_tok[:, 4 * h:4 * h + 4, :].rearrange("p a b -> p (a b)"), psum[:, 2 + h, :]))
            dve.wait_ge(sem("v_tok_ready"), 2)
            V.memset(done_flags[:, 3:4], 0.0).then_inc(sem("qv_tok_ready"), 1)
            bd4 = blockdiag.rearrange("p (a c) -> p a c", a=1).broadcast_to([P, 4, P])
            for g in range(4):
                zs = zsum[:, 4 * g:4 * g + 4].rearrange("p (b a) -> p b a", a=1).broadcast_to([P, 4, P])
                step(V.tensor_tensor(zmat[:, 4 * g:4 * g + 4, :], bd4, zs, ALU.mult))
            dve.wait_ge(sem("kv_mm"), 1)
            for g in range(4):
                bank, odd, b0 = [6, 7, 0, 1][g], g // 2, 8 * (g % 2)
                ins = V.tensor_tensor(kvm[:, b0 + odd:b0 + odd + 7:2, :],
                                      psum[:, bank, :].rearrange("p (a c) -> p a c", a=4), bd4, ALU.mult)
            ins.then_inc(sem("kvz_ready"), 1)
            dve.wait_ge(sem("numden_mm"), 1)
            for h in range(2):
                den = psum[:, 4 + h, :].rearrange("p (b n) -> p b n", b=8)
                num = psum[:, 2 + h, :].rearrange("p (b n) -> p b n", b=8)
                rd = rden[:, 8 * h:8 * h + 8, :]
                step(V.tensor_scalar(rd, den, ATTN_EPS, None, ALU.add))
                step(V.reciprocal(rd, rd))
                step(V.tensor_tensor(low2[:, 8 * h:8 * h + 8, 1:1 + D], num, rd, ALU.mult))
            for f in range(2):
                for j, (a, b) in enumerate(((1, 2), (0, 1), (2, 3))):
                    step(V.tensor_tensor(fsum[:, f, j:j + 1], filt[:, 2 + f, a:a + 1], filt[:, 2 + f, b:b + 1],
                                         ALU.add))

            def synthesise(low, high, dst, n, start):
                even, odd = dst[:, :, 0:2 * n - 1:2], dst[:, :, 1:2 * n:2]
                for f, src in enumerate((low, high)):
                    before, at, after = src[:, :, 0:n], src[:, :, 1:n + 1], src[:, :, 2:n + 2]
                    terms = (((before, filt[:, 2 + f, 0:1]), (at, fsum[:, f, 0:1]), (after, filt[:, 2 + f, 3:4])),
                             ((at, fsum[:, f, 1:2]), (after, fsum[:, f, 2:3])))
                    for o, ts in zip((even, odd), terms):
                        for k, (a, tap) in enumerate(ts):
                            if f == 0 and k == 0 and start is None:
                                step(V.tensor_scalar(o, a, tap, None, ALU.mult))
                            elif f == 0 and k == 0:
                                base = start[:, :, 0:2 * n - 1:2] if o is even else start[:, :, 1:2 * n:2]
                                step(V.scalar_tensor_tensor(o, a, tap, base, ALU.mult, ALU.add))
                            else:
                                step(V.scalar_tensor_tensor(o, a, tap, o, ALU.mult, ALU.add))

            synthesise(low2, high2, low1[:, :, 1:1 + S // 2], D, None)
            step(V.memset(low1[:, :, 0:1], 0.0))
            step(V.memset(low1[:, :, 1 + S // 2:4 + S // 2], 0.0))
            synthesise(low1, high1, syn, S // 2, hp[:, :, 1:S + 1])
            V.memset(done_flags[:, 3:4], 0.0).then_inc(sem("syn_ready"), 1)
            rb = row_bc.rearrange("p b (k c) -> p b k c", k=4)

            def by_row(k):
                return rb[:, :, k:k + 1, :].broadcast_to([P, B, ST, C])

            def seqs(a):
                return a.rearrange("p (b t) c -> p b t c", t=ST)

            layer_norm(x, x, sq2, 1, lambda: dve.wait_ge(sem("yt_copied"), B))
            step(V.tensor_tensor(x, x, per_row(rstd0), ALU.mult))
            step(V.tensor_tensor(seqs(x), seqs(x), by_row(0), ALU.mult))
            step(V.tensor_tensor(seqs(x), seqs(x), by_row(1), ALU.add))
            step(V.tensor_tensor(x1, x1, x, ALU.add))
            layer_norm(x1, x, sq2, 2, lambda: None)
            step(V.tensor_tensor(x, x, per_row(rstd0), ALU.mult))
            step(V.tensor_tensor(seqs(x), seqs(x), by_row(2), ALU.mult))
            step(V.tensor_tensor(seqs(x), seqs(x), by_row(3), ALU.add))
            V.memset(done_flags[:, 2:3], 0.0).then_inc(sem("phase_end"), 1)
            STEPS0 = step.n

            def mean_square(sg):
                dve.wait_ge(sem("xs_ready"), sg + 1)
                for t in range(ST):
                    ins = V.tensor_tensor_reduce(junk[:, t, :], xs[:, t, :], xs[:, t, :], 1.0 / C, EPS, ALU.mult, ALU.add,
                                                 ms[:, t:t + 1])
                ins.then_inc(sem("ms_ready"), 1)

            def scale_rows(sg):
                dve.wait_ge(sem("rstd_ready"), sg + 1)
                for t in range(ST):
                    ins = V.tensor_scalar(z[:, t, :], xs[:, t, :], rstd[:, t:t + 1], None, ALU.mult)
                ins.then_inc(sem("z_ready"), 1)

            def rope(sg, n, k0):
                for u in range(5):
                    dve.wait_ge(sem("s_full"), n + u + 1)
                    dve.wait_ge(sem("rope_done"), 1 + 5 * sg + max(u - 1, 0))
                    bank = psum[:, s_bank(k0 + u), :]
                    a, b = rope_a[:, u % 2, :], rope_b[:, u % 2, :]
                    if u < 4:
                        parts = [(slice(0, 512), u // 2, 8)]
                    else:
                        parts = [(slice(0, 256), 0, 4), (slice(256, 512), 1, 4)]
                    for sl, t, nh in parts:
                        src = bank[:, sl].rearrange("p (h d) -> p h d", h=nh)
                        aa = a[:, sl].rearrange("p (h d) -> p h d", h=nh)
                        bb = b[:, sl].rearrange("p (h d) -> p h d", h=nh)
                        cos = consts[:, K_COS + t * HD:K_COS + (t + 1) * HD].rearrange("p (a d) -> p a d", a=1)
                        sin = consts[:, K_SIN + t * HD:K_SIN + (t + 1) * HD].rearrange("p (a d) -> p a d", a=1)
                        hf = HD // 2
                        V.tensor_tensor(aa, src, cos.broadcast_to([P, nh, HD]), ALU.mult)
                        V.tensor_tensor(bb[:, :, 0:hf], src[:, :, hf:HD], sin[:, :, 0:hf].broadcast_to([P, nh, hf]),
                                        ALU.mult)
                        ins = V.tensor_tensor(bb[:, :, hf:HD], src[:, :, 0:hf],
                                              sin[:, :, hf:HD].broadcast_to([P, nh, hf]), ALU.mult)
                    ins.then_inc(sem("rope_parts"), 1)
                    dve.wait_ge(sem("rope_parts"), 5 * sg + u + 1)
                    V.memset(done_flags[:, 3:4], 0.0).then_inc(sem("s_free"), 1)

            def copy_v(n):
                dve.wait_ge(sem("s_full"), n + 1)
                V.tensor_copy(v.rearrange("p t c -> p (t c)"), psum[:, s_bank(S_V), :]).then_inc(sem("s_free"), 1)

            def mask_and_max(sg, q, first, last):
                for i in range(4):
                    k = s_place(S_HEAD[q] + i, last)
                    n = s_index(sg, k, first)
                    dve.wait_ge(sem("s_full"), n + 1)
                    V.memset(done_flags[:, 8 + i:9 + i], 0.0)
                    V.tensor_tensor_reduce(probs[:, q, i, 0:P], psum[:, s_bank(k), 0:P], mask[:, P:2 * P],
                                           SCALE, -3.0e38, ALU.add, ALU.max, rowmax[:, q, 2 * i:2 * i + 1])
                    V.tensor_tensor_reduce(probs[:, q, i, P:3 * P], psum[:, s_bank(k), P:3 * P], mask,
                                           SCALE, -3.0e38, ALU.add, ALU.max,
                                           rowmax[:, q, 2 * i + 1:2 * i + 2]).then_inc(sem("s_free"), 1)
                dve.wait_ge(sem("s_free"), 1 + n + 1)
                V.tensor_scalar(negmax[:, q, :], rowmax[:, q, :], -1.0, None, ALU.mult) \
                    .then_inc(sem("negmax_ready"), 1)

            def invert(qg, q):
                dve.wait_ge(sem("exp_done"), qg + 1)
                V.reciprocal(rinv[:, q, :], rowsum[:, q, :]).then_inc(sem("rinv_ready"), 1)

            def copy_o(qg, q):
                dve.wait_ge(sem("o_full"), qg + 1)
                V.tensor_copy(oT[:, 2 * q:2 * q + 2, :].rearrange("p a b -> p (a b)"), psum[:, O_BANK, :]) \
                    .then_inc(sem("o_free"), 1)

            def update_x(sg, s, k, n):
                dve.wait_ge(sem("s_full"), n + 1)
                xv = x[:, bass.ds(s * ST, ST), :]
                V.tensor_tensor(xv, xv, psum[:, s_bank(k), 0:S].rearrange("p (t c) -> p t c", t=ST), ALU.add) \
                    .then_inc(sem("s_free"), 1)
                dve.wait_ge(sem("s_free"), 1 + n + 1)
                V.tensor_scalar(xv, xv, 100.0, -100.0, ALU.min, ALU.max)

            def sequence(sg, s, first, last):
                mask_and_max(sg, 0, first, last)
                if not first:
                    invert(4 * sg - 1, 3)
                    copy_o(4 * sg - 2, 2)
                if not last:
                    mean_square(sg + 1)
                mask_and_max(sg, 1, first, last)
                invert(4 * sg, 0)
                if not last:
                    scale_rows(sg + 1)
                if not first:
                    copy_o(4 * sg - 1, 3)
                copy_v(s_index(sg, S_V, first))
                if not first:
                    update_x(sg - 1, s - 1, S_OUT, s_index(sg, S_OUT))
                mask_and_max(sg, 2, first, last)
                invert(4 * sg + 1, 1)
                if not last:
                    rope(sg + 1, s_index(sg, S_QK), S_QK)
                copy_o(4 * sg, 0)
                mask_and_max(sg, 3, first, last)
                invert(4 * sg + 2, 2)
                copy_o(4 * sg + 1, 1)
                if last:
                    invert(4 * sg + 3, 3)
                    copy_o(4 * sg + 2, 2)
                    copy_o(4 * sg + 3, 3)
                    k = s_place(S_END, True)
                    update_x(sg, s, k, s_index(sg, k))

            PREP_STEPS = 15

            def prepare(pg, part, par):
                st = Steps(STEPS0 + pg * PREP_STEPS)
                if part == 0:
                    dve.wait_ge(sem("xs2_ready"), pg + 1)
                    for t in range(4):
                        ins = V.tensor_tensor_reduce(junk2[:, t, :], xs2[:, t, :], xs2[:, t, :], 1.0 / C, EPS,
                                                     ALU.mult, ALU.add, ms2[:, t:t + 1])
                    ins.then_inc(sem("ms2_ready"), 1)
                    return
                if part == 1:
                    dve.wait_ge(sem("rstd2_ready"), pg + 1)
                    for t in range(4):
                        ins = V.tensor_scalar(z2[:, t, :], xs2[:, t, :], rstd2[:, t:t + 1], None, ALU.mult)
                    ins.then_inc(sem("z2_ready"), 1)
                    return
                if part == 2:
                    dve.wait_ge(sem("logits_mm"), pg + 1)
                    st(V.tensor_copy(logits.rearrange("p a b -> p (a b)"), psum[:, 6, 0:4 * NE]))
                    V.memset(done_flags[:, 4:5], 0.0)
                    for t in range(4):
                        ins = V.max(max8[:, t, :], logits[:, t, :])
                    st(ins)
                    V.tensor_tensor(gap.rearrange("p (t a) -> p t a", a=1), max8[:, :, 0:1], max8[:, :, 1:2],
                                    ALU.subtract).then_inc(sem("gap_ready"), 1)
                    for t in range(4):
                        ins = V.max_index(idx8[:, t, :].bitcast(U32), max8[:, t, :], logits[:, t, :])
                    st(ins)
                    st(V.tensor_copy(idxf, idx8[:, :, 0:2].bitcast(U32)))
                    io = iota8.rearrange("p (a e) -> p a e", a=1).broadcast_to([P, 4, NE])
                    for j in range(2):
                        st(V.tensor_tensor(pick[:, j], io, idxf[:, :, j:j + 1].broadcast_to([P, 4, NE]), ALU.is_equal))
                    return
                if part == 4:
                    dve.wait_ge(sem("combT_mm"), pg + 1)
                    V.tensor_copy(combT[:, :], psum[0:3 * NE, 6, 0:256].bitcast(BF16)).then_inc(sem("combT_ready"), 1)
                    return
                st.n = 6
                dve.wait_ge(sem("tanh_ready"), pg + 1)
                st(V.tensor_scalar(c12[:, 0, :], th, 0.5, 0.5, ALU.mult, ALU.add))
                st(V.tensor_scalar(c12[:, 1, :], th, -0.5, 0.5, ALU.mult, ALU.add))
                for j in range(2):
                    cj = c12[:, j, :].rearrange("p (t a) -> p t a", a=1).broadcast_to([P, 4, NE])
                    st(V.tensor_tensor(pick[:, j], pick[:, j], cj, ALU.mult))
                st(V.tensor_tensor(comb, pick[:, 0], pick[:, 1], ALU.add))
                st(V.tensor_copy(comb_parts[:, :, 0:NE], comb))
                st(V.tensor_tensor(rest, comb, comb_parts[:, :, 0:NE], ALU.subtract))
                st(V.tensor_copy(comb_parts[:, :, NE:2 * NE], rest))
                st(V.tensor_tensor(rest, rest, comb_parts[:, :, NE:2 * NE], ALU.subtract))
                V.tensor_copy(comb_parts[:, :, 2 * NE:3 * NE], rest).then_inc(sem("comb_ready"), 1)
                assert st.n == PREP_STEPS, st.n

            def experts(pg, p, par, prep):
                NU = 2 * NE
                for n in range(NU):
                    dve.wait_ge(sem("silu_c_ready"), NU * pg + n + 1)
                    dve.wait_ge(sem("up_mm"), NU * pg + n + 1)
                    V.tensor_tensor(hh[:, n % 3, :], silu_c[:, n % 3, :], psum[:, 2 * (n % 2) + 1, :], ALU.mult) \
                        .then_inc(sem("hh_ready"), 1)
                    if prep and n == 0:
                        prepare(pg + 1, 0, 1 - par)
                    if prep and n == 1:
                        prepare(pg + 1, 1, 1 - par)
                    if prep and n == 5:
                        prepare(pg + 1, 2, 1 - par)
                    if prep and n == 6:
                        prepare(pg + 1, 3, 1 - par)
                    if prep and n == 9:
                        prepare(pg + 1, 4, 1 - par)
                dve.wait_ge(sem("y_tok_mm"), pg + 1)
                xv = x[:, bass.ds(p * 4, 4), :]
                V.tensor_tensor(xv, xv, psum[:, 7, :].rearrange("p (t c) -> p t c", t=4), ALU.add) \
                    .then_inc(sem("y_added"), 1)
                dve.wait_ge(sem("y_added"), 1 + pg + 1)
                V.tensor_scalar(xv, xv, 100.0, -100.0, ALU.min, ALU.max).then_inc(sem("x2_updated"), 1)

            with dve.Fori(0, L) as l:
                phase_done(dve, 2 * l)
                s0 = l * B
                V.memset(KT[64:P, 0], 0.0)
                V.memset(KT[0:64, 1], 0.0).then_inc(sem("k_zeroed"), 1)
                mean_square(s0)
                scale_rows(s0)
                rope(s0, s0 * S_PER, S_FIRST)
                sequence(s0, 0, True, False)
                with dve.Fori(1, B - 1) as s:
                    sequence(l * B + s, s, False, False)
                sequence(s0 + B - 1, B - 1, False, True)
                V.memset(done_flags[:, 2:3], 0.0).then_inc(sem("phase_end"), 1)
                phase_done(dve, 1 + 2 * l)
                for part in range(5):
                    prepare(l * NP_, part, 0)
                with dve.Fori(0, NP_ // 2 - 1) as i:
                    experts(l * NP_ + 2 * i, 2 * i, 0, True)
                    experts(l * NP_ + 2 * i + 1, 2 * i + 1, 1, True)
                experts(l * NP_ + NP_ - 2, NP_ - 2, 0, True)
                experts(l * NP_ + NP_ - 1, NP_ - 1, 1, False)
                V.memset(done_flags[:, 2:3], 0.0).then_inc(sem("phase_end"), 1)
            dve.wait_ge(sem("x2_updated"), L * NP_)
            NQ = B // 4
            for q in range(4):
                xq = seqs(x)[:, q * NQ:(q + 1) * NQ]
                gq = gb_rows[:, q * NQ:(q + 1) * NQ, :].rearrange("p b (a c) -> p b a c", a=1)
                V.tensor_tensor(xq, xq, gq.broadcast_to([P, NQ, ST, C]), ALU.mult).then_inc(sem("gated"), 1)
                dve.wait_ge(sem("gated"), q + 1)
                V.tensor_tensor(seqs(x1)[:, q * NQ:(q + 1) * NQ], seqs(x1)[:, q * NQ:(q + 1) * NQ], xq, ALU.add) \
                    .then_inc(sem("out_ready"), 1)


def kernel(**inputs):
    import concourse.bacc as _bacc
    from concourse.bass_utils import run_bass_kernel_spmd as _run

    nc = _bacc.Bacc("TRN2", target_bir_lowering=False, num_devices=1)
    k, sel_seq, sel_exp = shape_constants()
    given = {n: inputs[n] for n in ("L0_attn_x", "L0_wmod", "L0_attn_norm_gamma", "L0_attn_norm_beta", "L0_ffn_wq",
                                    "L0_ffn_wk", "L0_ffn_wv", "L0_ffn_wo", "L0_ffn_wr", "L0_ffn_wg", "L0_ffn_wu",
                                    "L0_ffn_wd")}
    given["cT"] = np.asarray(inputs["L0_c"]).T
    for n in ("h_filter", "g_filter", "h_synth", "g_synth"):
        given[n + "_T"] = np.asarray(inputs["L0_attn_" + n]).T
    given["ln1_T"] = np.asarray(inputs["L0_ffn_ln1_w"]).T
    given["ln2_T"] = np.asarray(inputs["L0_ffn_ln2_w"]).T
    given.update(consts=k, sel_seq=sel_seq, sel_exp=sel_exp)
    arrays, aps = {}, {}
    for n, a in given.items():
        a = np.ascontiguousarray(a)
        arrays["in_" + n] = a
        aps[n] = nc.dram_tensor("in_" + n, a.shape, mybir.dt.from_np(a.dtype), kind="ExternalInput").ap()
    out = nc.dram_tensor("out_0", (B, S, C), F32, kind="ExternalOutput").ap()
    bass_program(nc, aps, out)
    r = _run(nc, [arrays], core_ids=[0])
    return r.results[0]["out_0"]
```

```python
from contextlib import ExitStack

import numpy as np
import concourse.bass as bass
from concourse import mybir

F32 = mybir.dt.float32
F32R = mybir.dt.float32r
BF16 = mybir.dt.bfloat16
U32 = mybir.dt.uint32
ALU = mybir.AluOpType
ACT = mybir.ActivationFunctionType
AX = mybir.AxisListType.X

P = 128
B, S, C = 16, 256, 128
NT = B * S // P
ST = S // P
L, NH, NKV, HD, FF, NE = 4, 16, 4, 64, 256, 8
TAPS = 4
LH = 8
EPS = 1e-5
ATTN_EPS = 1e-6
NEG = -8.0e9
SCALE = HD ** -0.5
PAIR = 2 * S
NP_ = B * S // PAIR

K_ID, K_MASK, K_COS, K_SIN, K_BD, K_IOTA, K_END = 0, 128, 384, 512, 640, 768, 776


def shape_constants():
    pos = np.arange(S, dtype=np.float32)
    inv = (1.0 / np.float32(10000.0) ** (np.arange(0, HD, 2, dtype=np.float32) / np.float32(HD))).astype(np.float32)
    ang = (pos[:, None] * inv).astype(np.float32)
    emb = np.concatenate([ang, ang], axis=-1)
    cos, sin = np.cos(emb).astype(np.float32), np.sin(emb).astype(np.float32)
    sin[:, :HD // 2] *= -1.0
    k = np.zeros((P, K_END), np.float32)
    k[:, K_ID:K_ID + P] = np.eye(P)
    k[:, K_MASK + P:K_MASK + 2 * P] = np.where(np.tril(np.ones((P, P))) > 0, 0.0, NEG)
    for t in range(ST):
        k[:, K_COS + t * HD:K_COS + (t + 1) * HD] = cos[t * P:(t + 1) * P]
        k[:, K_SIN + t * HD:K_SIN + (t + 1) * HD] = sin[t * P:(t + 1) * P]
    g = np.arange(P) // LH
    k[:, K_BD:K_BD + P] = g[:, None] == g[None, :]
    k[:, K_IOTA:K_IOTA + NE] = np.arange(NE)
    sel_seq = np.repeat(np.eye(B, dtype=np.float32), P, axis=1)
    sel_exp = np.repeat(np.tile(np.eye(NE, dtype=np.float32), (3, 1)), P, axis=1)
    return k, sel_seq, sel_exp


class Arena:

    def __init__(self, tensor, size):
        self.t, self.size, self.at = tensor, size, 0

    def take(self, *shape):
        n = int(np.prod(shape))
        ap = self.t[:, self.at:self.at + n]
        self.at += n
        assert self.at <= self.size, self.at
        if len(shape) == 2:
            ap = ap.rearrange("p (a b) -> p a b", a=shape[0])
        if len(shape) == 3:
            ap = ap.rearrange("p (a b c) -> p a b c", a=shape[0], b=shape[1])
        return ap


def bass_program(nc, I, out):
    ctx = ExitStack()
    with ctx:
        ARENA_AT, SIZE = 20480, 52200
        arena = Arena(nc.alloc_sbuf_tensor_at("arena", [P, SIZE], F32, offset=ARENA_AT), SIZE)

        def take_f32r(name, *shape):
            n = int(np.prod(shape))
            arena.at += -arena.at % 8
            t = nc.alloc_sbuf_tensor_at(name, [P, n], F32R, offset=ARENA_AT + 4 * arena.at)
            arena.take(n)
            return Arena(t, n).take(*shape)

        sel_exp = ctx.enter_context(nc.sbuf_tensor("sel_exp", [3 * NE, NE * P], BF16))
        comb_parts = ctx.enter_context(nc.sbuf_tensor("comb_parts", [P, 4, 3 * NE], BF16))
        combT = ctx.enter_context(nc.sbuf_tensor("combT", [3 * NE, PAIR], BF16))
        ident_bf = ctx.enter_context(nc.sbuf_tensor("ident_bf", [P, P], BF16))
        psum = ctx.enter_context(nc.psum_tensor("psum", [P, 8, 512], F32))
        sems = {}

        def sem(name):
            if name not in sems:
                sems[name] = ctx.enter_context(nc.semaphore(name))
            return sems[name]

        x = arena.take(NT, C)
        x1 = arena.take(NT, C)
        gb_rows = arena.take(B, C)
        consts = arena.take(K_END)
        ident = consts[:, K_ID:K_ID + P]
        mask = consts[:, K_MASK:K_MASK + 2 * P]
        blockdiag = consts[:, K_BD:K_BD + P]
        iota8 = consts[:, K_IOTA:K_IOTA + NE]
        lnw = arena.take(2, L)
        lnw_now = arena.take(2)
        minus_half = arena.take(NT)
        arena.at += -arena.at % 8
        at_wq = arena.at
        wq = arena.take(NH * HD)
        wk = arena.take(NKV * HD)
        wv = arena.take(NKV * HD)
        wo = arena.take(NH // 2, C)
        wr = arena.take(NE)
        done_flags = arena.take(16)
        arena.at += -arena.at % 8
        before_moe_w = arena.at
        wg = arena.take(NE, FF)
        wu = arena.take(NE, FF)
        wd = arena.take(NE, 2, C)
        w_all = [arena.t[:, before_moe_w + m * NE * FF:before_moe_w + (m + 1) * NE * FF] for m in range(3)]
        shared = arena.at

        arena.at = before_moe_w
        cT = arena.take(B)
        scT = arena.take(B)
        wmod = arena.take(6 * C)
        filt = arena.take(4, TAPS)
        fsum = arena.take(2, 3)
        modcol = arena.take(2, B)
        rows = arena.take(5, C)
        rtmp = arena.take(4, C)
        gamma_beta = arena.take(2, C)
        sel_seq = arena.take(B, P)
        row_bc = arena.take(B, 4 * C)
        mean = arena.take(NT)
        var = arena.take(NT)
        rstd0 = arena.take(NT)
        HPW = S + 4
        hp = arena.take(B, HPW)
        low1 = arena.take(B, S // 2 + 4)
        high1 = arena.take(B, S // 2 + 2)
        low2 = arena.take(B, S // 4 + 2)
        high2 = arena.take(B, S // 4 + 2)
        at_q = arena.at
        qf = arena.take(B, S // 4)
        q_tok = arena.take(8, P)
        v_tok = arena.take(8, P)
        kvm = arena.take(B, P)
        zmat = arena.take(B, P)
        zsum = arena.take(B)
        rden = arena.take(B, S // 4)
        syn_v = arena.take(B * S // 4)
        arena.at = at_q
        xc_a = arena.take(NT, C)
        arena.at = at_q
        syn = arena.take(B, S)
        arena.at = at_q
        sq2 = arena.take(NT, C)
        sq = x

        arena.at = shared
        hT = arena.take(S)
        after_hT = arena.at
        xs = arena.take(ST, C)
        z = arena.take(ST, C)
        junk = arena.take(ST, C)
        ms = arena.take(ST)
        rstd = arena.take(ST)
        qk_raw = arena.take(5, 512)
        rope_b = arena.take(4, 512)
        qr = arena.take(ST, NH * HD)
        kr = arena.take(ST, NKV * 2 * HD)
        next_qk_end = arena.at
        QT = arena.take(NH // 2, S)
        KT = arena.take(2, NKV, S)
        v = arena.take(ST, NKV * HD)
        probs = arena.take(4, 4, 3 * P)
        rowmax = arena.take(4, 8)
        negmax = arena.take(4, 8)
        rowsum = arena.take(4, 8)
        rinv = arena.take(4, 8)
        probsT = arena.take(8, 3 * P)
        oT = arena.take(NH // 2, S)
        wq_hi = take_f32r("wq_hi", NH * HD)
        h_hi = take_f32r("h_hi", S)
        h_lo = take_f32r("h_lo", S)
        attention_end = arena.at
        arena.at = at_wq
        wq_lo = take_f32r("wq_lo", NH * HD)
        arena.at = after_hT
        xs2 = arena.take(4, C)
        z2 = arena.take(4, C)
        junk2 = arena.take(4, C)
        ms2 = arena.take(4)
        rstd2 = arena.take(4)
        h2T = arena.take(PAIR)
        logits = arena.take(4, NE)
        max8 = arena.take(4, NE)
        idx8 = arena.take(4, NE)
        idxf = arena.take(4, 2)
        gap = arena.take(4)
        th = arena.take(4)
        c12 = arena.take(2, 4)
        pick = arena.take(2, 4, NE)
        comb = arena.take(4, NE)
        rest = arena.take(4, NE)
        h2_hi = take_f32r("h2_hi", 2, PAIR)
        h2_lo = take_f32r("h2_lo", 2, PAIR)
        assert arena.at <= next_qk_end
        comb_bc = arena.take(2, NE, PAIR)
        RING = 4
        silu_g = arena.take(2, PAIR)
        gated = arena.take(RING, PAIR)
        hh = arena.take(RING, PAIR)
        yT = arena.take(PAIR)
        hh_hi = take_f32r("hh_hi", RING, PAIR)
        hh_lo = take_f32r("hh_lo", RING, PAIR)
        experts_end = arena.at
        arena.at = SIZE - 3 * NE * FF - 8
        assert arena.at >= max(experts_end, attention_end)
        w_hi = [take_f32r(f"w{m}_hi", NE * FF) for m in range(3)]
        arena.at = before_moe_w
        w_lo = [take_f32r(f"w{m}_lo", NE * FF) for m in range(3)]
        W_PIECE = NE * FF // B

        def expert_w(w, m, e, f):
            return w[m][:, e * FF + f * P:e * FF + (f + 1) * P]

        block = ctx.enter_context(nc.Block())
        POOL_FROM_ONE = ("rope_done",)
        ACT_FROM_ONE = ("t_free", "yT_copied", "comb_bc_ready")
        DVE_FROM_ONE = ("s_free", "o_free", "z_ready", "y_added", "z2_ready")
        PH = 3

        def phase_done(eng, k):
            eng.wait_ge(sem("phase_end"), PH * (k + 1))

        @block.sync
        def _(sp):
            def load(dst, src, name):
                sp.dma_start(dst, src).then_inc(sem(name), 16)

            load(cT, I["cT"], "c_in")
            load(wmod, I["L0_wmod"], "wmod_in")
            load(consts, I["consts"], "consts_in")
            xv = I["L0_attn_x"].rearrange("b (t p) c -> p (b t) c", p=P)
            for q in range(4):
                load(x1[:, q * 8:(q + 1) * 8, :], xv[:, q * 8:(q + 1) * 8, :], "x_in")
            for q, n in enumerate(["h_filter", "g_filter", "h_synth", "g_synth"]):
                load(filt[:, q, :], I[n + "_T"], "filt_in")
            for q, n in enumerate(["L0_attn_norm_gamma", "L0_attn_norm_beta"]):
                load(gamma_beta[0:B, q, :], I[n].rearrange("(a c) -> a c", a=1).partition_broadcast(B), "rows_in")
            load(sel_seq[0:B].rearrange("p b m -> p (b m)"), I["sel_seq"], "rows_in")
            load(lnw[:, 0, :], I["ln1_T"], "small_in")
            load(lnw[:, 1, :], I["ln2_T"], "small_in")

            def attn_weights(l):
                d = bass.ds(l, 1) if not isinstance(l, int) else slice(l, l + 1)
                sp.dma_start(wq, I["L0_ffn_wq"][d].rearrange("l h n -> (l h) n")).then_inc(sem("wattn_in"), 16)
                sp.dma_start(wk, I["L0_ffn_wk"][d].rearrange("l h n -> (l h) n")).then_inc(sem("wattn_in"), 16)
                sp.dma_start(wv, I["L0_ffn_wv"][d].rearrange("l h n -> (l h) n")).then_inc(sem("wattn_in"), 16)
                sp.dma_start(wo, I["L0_ffn_wo"][d].rearrange("l (c p) n -> (l p) c n", p=P)).then_inc(sem("wattn_in"), 16)

            def moe_weights(l):
                d = bass.ds(l, 1) if not isinstance(l, int) else slice(l, l + 1)
                sp.dma_start(wg, I["L0_ffn_wg"][d].rearrange("l e h f -> (l h) e f")).then_inc(sem("wmoe_in"), 16)
                sp.dma_start(wu, I["L0_ffn_wu"][d].rearrange("l e h f -> (l h) e f")).then_inc(sem("wmoe_in"), 16)
                wdv = I["L0_ffn_wd"][d].rearrange("l e (f p) n -> (l p) e f n", p=P)
                for f in range(2):
                    sp.dma_start(wd[:, :, f, :], wdv[:, :, f, :]).then_inc(sem("wmoe_in"), 16)
                sp.dma_start(wr, I["L0_ffn_wr"][d].rearrange("l h n -> (l h) n")).then_inc(sem("wmoe_in"), 16)

            attn_weights(0)
            phase_done(sp, 0)
            moe_weights(0)
            with sp.Fori(0, L - 1) as l:
                phase_done(sp, 1 + 2 * l)
                attn_weights(l + 1)
                phase_done(sp, 2 + 2 * l)
                moe_weights(l + 1)
            ov = out.rearrange("b (t p) c -> p (b t) c", p=P)
            for q in range(4):
                sp.wait_ge(sem("out_ready"), q + 1)
                sp.dma_start(ov[:, q * 8:(q + 1) * 8, :], x1[:, q * 8:(q + 1) * 8, :]).then_inc(sem("out_written"), 16)
            sp.wait_ge(sem("out_written"), 64)

        N_ATTN_W, N_MOE_W = 4 * 16, 5 * 16

        S_BANK, T_BANK, O_BANK = 0, 4, 7

        S_PER, T_PER = NH + 7, NH + 7
        S_HEAD = {0: 0, 1: 4, 2: 10, 3: 19}
        S_V, S_OUT, S_QK, S_END = 8, 9, 14, 23
        T_OLD, T_H, T_NEW, T_QK = {2: 0, 3: 4}, 8, {0: 9, 1: 19}, 13
        T_FIRST = T_PER - 6
        T_LAST = {0: 8, 1: 12, 2: 16, 3: 20}

        S_FIRST = S_END - 5

        def s_place(k, last):
            return k - 5 if last and k >= S_QK else k

        def s_bank(k):
            return S_BANK + k % 4

        def s_index(sg, k, first=False):
            return sg * S_PER + (5 if first and k < S_OUT else 4) + k

        def s_waited(sg, k, first=False, last=False):
            lag = 3 if k < 3 or (first and k > S_OUT) else 4
            return s_index(sg, k, first) - lag + 1

        def t_index(sg, k):
            return sg * T_PER - 1 + k

        def t_waited(n, k):
            return n - (1 if k < 2 else 2)

        def t_turned(sg, first):
            return sg * T_PER + 7 if first else t_index(sg, 0) - 4

        def t_bank(k):
            return T_BANK + k % 3

        def half(h):
            return slice(h * NT // 2, (h + 1) * NT // 2)

        def prep_bank(running, k):
            return (5 if running else 0) + k

        def as_heads(a):
            return a.rearrange("p (t j e) -> p t j e", t=ST, j=NKV)

        def k_copy(d):
            return kr.rearrange("p t (j d e) -> p t j d e", j=NKV, d=2)[:, :, :, d, :]

        def middle_sequences(eng, sequence):
            with eng.Fori(0, (B - 2) // 2) as i:
                for j in (1, 2):
                    sequence(2 * i + j)

        NU = 2 * NE
        DOWN_LAG = 4
        ROUND_LAG = 2

        def all_pairs(eng, l, experts):
            experts(l * NP_, 0, 0, True, False)
            with eng.Fori(0, NP_ // 2 - 1) as i:
                for j in (1, 2):
                    experts(l * NP_ + 2 * i + j, 2 * i + j, j % 2, False, False)
            experts(l * NP_ + NP_ - 1, NP_ - 1, 1, False, True)

        @block.tensor
        def _(pe):
            T = nc.tensor
            pe.wait_ge(sem("silu_c"), 1)
            pe.wait_ge(sem("wmod_in"), 16)
            for j in range(2):
                T.matmul(psum[:, 0, j * B:(j + 1) * B], wmod[:, j * C:(j + 1) * C], scT, start=True, stop=True)
            T.matmul(psum[0:B, 1, :], scT, wmod[:, 2 * C:6 * C], start=True, stop=True).then_inc(sem("mod_mm"), 1)
            pe.wait_ge(sem("consts_in"), 16)
            for b in range(B):
                pe.wait_ge(sem("xc_ready"), 1 + 2 * b // B)
                if b < 2:
                    pe.wait_ge(sem("mod_copied"), 1)
                if b >= 2:
                    pe.wait_ge(sem("hp_ready"), b - 1)
                for t in range(ST):
                    mm = T.transpose(psum[:, b % 2, t * P:(t + 1) * P], xc_a[:, b * ST + t, :], ident)
                mm.then_inc(sem("xcT_mm"), 1)
            pe.wait_ge(sem("rows_ready"), 1)
            pe.wait_ge(sem("rows_in"), 48)
            for b in range(B):
                if b >= 4:
                    pe.wait_ge(sem("rowbc_copied"), b - 3)
                T.matmul(psum[:, 4 + b % 4, :], sel_seq[0:B, b, :], rows[0:B, 0:4, :].rearrange("p a c -> p (a c)"),
                         start=True, stop=True).then_inc(sem("rowbc_mm"), 1)
            for q in range(4):
                pe.wait_ge(sem("rowbc_copied"), B - 3 + q)
                for j in range(4):
                    mm = T.matmul(psum[:, 4 + q, j * C:(j + 1) * C], sel_seq[0:B, 4 * q + j, :], rows[0:B, 4, :],
                                  start=True, stop=True)
                mm.then_inc(sem("rowbc_mm"), 1)
            pe.wait_ge(sem("rowbc_copied"), B + 4)
            pe.wait_ge(sem("qf_ready"), 1)
            for g in range(8):
                T.transpose(psum[:, 2 + g // 4, (g % 4) * P:(g % 4 + 1) * P],
                            qf[:, 2 * g:2 * g + 2, :].rearrange("p b n -> p (b n)"), ident)
            pe.wait_ge(sem("rowbc_copied"), B + 4)
            pe.wait_ge(sem("lowc_ready"), 1)
            for g in range(8):
                mm = T.transpose(psum[:, 4 + g // 4, (g % 4) * P:(g % 4 + 1) * P],
                                 syn_v[:, g * P:(g + 1) * P], ident)
            mm.then_inc(sem("qv_tok_mm"), 1)
            pe.wait_ge(sem("qv_tok_ready"), 1)
            for b in range(B):
                r = slice(64 * (b % 2), 64 * (b % 2) + 64)
                bank = [6, 7][b // 8] if b % 2 == 0 else [0, 1][b // 8]
                mm = T.matmul(psum[:, bank, (b // 2 % 4) * P:(b // 2 % 4 + 1) * P], q_tok[r, b // 2, :], v_tok[r, b // 2, :],
                              start=True, stop=True)
            mm.then_inc(sem("kv_mm"), 1)
            pe.wait_ge(sem("kvz_ready"), 1)
            for b in range(B):
                T.matmul(psum[:, 2 + b // 8, (b % 8) * 64:(b % 8 + 1) * 64], kvm[:, b, :], qf[:, b, :],
                         start=True, stop=True)
            for b in range(B):
                mm = T.matmul(psum[:, 4 + b // 8, (b % 8) * 64:(b % 8 + 1) * 64], zmat[:, b, :], qf[:, b, :],
                              start=True, stop=True)
            mm.then_inc(sem("numden_mm"), 1)
            for b in range(B):
                pe.wait_ge(sem("syn_ready"), 1)
                if b >= 4:
                    pe.wait_ge(sem("yt_copied"), b - 3)
                bank = [0, 1, 6, 7][b % 4]
                for t in range(ST):
                    mm = T.transpose(psum[:, bank, t * P:(t + 1) * P], syn[:, b, t * P:(t + 1) * P], ident)
                mm.then_inc(sem("yt_mm"), 1)

            def scores(sg, q, first, last):
                if q == 0:
                    pe.wait_ge(sem("t_free"), 1 + t_turned(sg, first))
                    pe.wait_ge(sem("k_odd_copied"), 2 * (sg + 1))
                for i in range(4):
                    k = s_place(S_HEAD[q] + i, last)
                    if q == 3 and not last:
                        pe.wait_ge(sem("qk_copied"), 5 * (sg + 1) + 2 + i)
                    else:
                        pe.wait_ge(sem("s_free"), 1 + s_waited(sg, k, first))
                    c, bank = (4 * q + i) // 2, s_bank(k)
                    T.matmul(psum[:, bank, 0:P], QT[:, c, 0:P], KT[:, i % 2, q, 0:P], start=True, stop=True)
                    T.matmul(psum[:, bank, P:3 * P], QT[:, c, P:2 * P], KT[:, i % 2, q, :],
                             start=True, stop=True).then_inc(sem("s_full"), 1)

            def attend(qg, q, n, k, after_k=None):
                pe.wait_ge(sem("probs_ready"), qg + 1)
                pe.wait_ge(sem("o_free"), 1 + qg)
                for i in range(4):
                    pe.wait_ge(sem("t_free"), 1 + t_waited(n + i, k + i))
                    if after_k is not None and i in (1, 2):
                        pe.wait_ge(sem("k_odd_copied"), 2 * after_k + i)
                    for j in range(3):
                        mm = T.transpose(psum[:, t_bank(k + i), j * P:(j + 1) * P],
                                         probs[:, q, i, j * P:(j + 1) * P], ident)
                    mm.then_inc(sem("t_full"), 1)
                    if i >= 2:
                        weigh(q, i - 2, n)
                weigh(q, 2, n)
                weigh(q, 3, n).then_inc(sem("o_full"), 1)

            def weigh(q, i, n):
                pe.wait_ge(sem("t_free"), 1 + n + i + 1)
                r = slice(64 * (i % 2), 64 * (i % 2) + 64)
                c0 = 256 * (i // 2)
                pt = probsT[:, 4 * (q % 2) + i, :]
                T.matmul(psum[r, O_BANK, c0:c0 + S], v[:, 0, q * HD:(q + 1) * HD], pt[:, 0:S],
                         start=True, stop=False, skip_group_check=True)
                return T.matmul(psum[r, O_BANK, c0 + P:c0 + S], v[:, 1, q * HD:(q + 1) * HD], pt[:, S:S + P],
                                start=False, stop=True, skip_group_check=True)

            def turn_h(sg, n, k, started):
                pe.wait_ge(sem("z_ready"), 1 + sg + 1)
                if started:
                    pe.wait_ge(sem("t_free"), 1 + t_waited(n, k))
                for t in range(ST):
                    mm = T.transpose(psum[:, t_bank(k), t * P:(t + 1) * P], z[:, t, :], ident)
                mm.then_inc(sem("t_full"), 1)

            def project_qk(sg, h_n, n, k0, first):
                pe.wait_ge(sem("t_free"), 1 + h_n + 1)
                pe.wait_ge(sem("h_lo_ready"), sg + 1)
                for u in range(5):
                    if u == 4:
                        pe.wait_ge(sem("qk_copied"), 5 * sg + 1)
                    elif not first:
                        pe.wait_ge(sem("s_free"), 1 + n + u - 3)
                    bank = s_bank(k0 + u)
                    if u < 4:
                        rows, cols = slice(u // 2 * P, (u // 2 + 1) * P), slice(u % 2 * 512, (u % 2 + 1) * 512)
                        T.matmul(psum[:, bank, :], h_hi[:, rows], wq_hi[:, cols], start=True, stop=False)
                        T.matmul(psum[:, bank, :], h_hi[:, rows], wq_lo[:, cols], start=False, stop=False)
                        mm = T.matmul(psum[:, bank, :], h_lo[:, rows], wq_hi[:, cols], start=False, stop=True)
                    else:
                        for t in range(ST):
                            mm = T.matmul(psum[:, bank, t * 256:(t + 1) * 256], hT[:, t * P:(t + 1) * P], wk,
                                          start=True, stop=True)
                    mm.then_inc(sem("s_full"), 1)

            def project_v(sg, first):
                pe.wait_ge(sem("s_free"), 1 + s_waited(sg, S_V, first))
                for t in range(ST):
                    mm = T.matmul(psum[:, s_bank(S_V), t * 256:(t + 1) * 256], hT[:, t * P:(t + 1) * P], wv,
                                  start=True, stop=True)
                mm.then_inc(sem("s_full"), 1)

            def turn_qk(sg, n, k0, first=False):
                for u in range(6):
                    if u == 0:
                        pe.wait_ge(sem("rope_done"), 1 + 5 * sg + 4)
                    if u == 4:
                        pe.wait_ge(sem("rope_done"), 1 + 5 * sg + 5)
                        pe.wait_ge(sem("k_copy_ready"), sg + 1)
                    if u >= 2 or not first:
                        pe.wait_ge(sem("t_free"), 1 + n + u - 2)
                    for i in range(2):
                        for t in range(ST):
                            if u < 4:
                                src = qr[:, t, (2 * u + i) * P:(2 * u + i + 1) * P]
                            else:
                                src = kr[:, t, (2 * (u - 4) + i) * P:(2 * (u - 4) + i + 1) * P]
                            mm = T.transpose(psum[:, t_bank(k0 + u), (2 * i + t) * P:(2 * i + t + 1) * P],
                                             src, ident)
                    mm.then_inc(sem("t_full"), 1)

            def project_out(sg, k, waited):
                pe.wait_ge(sem("o_free"), 1 + 4 * sg + 4)
                pe.wait_ge(sem("s_free"), 1 + waited)
                for t in range(ST):
                    for c in range(NH // 2):
                        mm = T.matmul(psum[:, s_bank(k), t * P:(t + 1) * P], oT[:, c, t * P:(t + 1) * P], wo[:, c, :],
                                      start=(c == 0), stop=(c == NH // 2 - 1))
                mm.then_inc(sem("s_full"), 1)

            def sequence(l, s, first, last):
                sg = l * B + s
                n = t_index(sg, 0)
                new = T_LAST if last else T_NEW
                scores(sg, 0, first, last)
                if not first:
                    attend(4 * sg - 2, 2, n + T_OLD[2], T_OLD[2])
                scores(sg, 1, first, last)
                if not first:
                    attend(4 * sg - 1, 3, n + T_OLD[3], T_OLD[3])
                project_v(sg, first)
                if not first:
                    project_out(sg - 1, S_OUT, s_waited(sg, S_OUT))
                if not last:
                    turn_h(sg + 1, n + T_H, T_H, True)
                scores(sg, 2, first, last)
                if not last:
                    project_qk(sg + 1, n + T_H, s_index(sg, S_QK), S_QK, False)
                attend(4 * sg, 0, n + new[0], new[0])
                scores(sg, 3, first, last)
                if not last:
                    turn_qk(sg + 1, n + T_QK, T_QK)
                attend(4 * sg + 1, 1, n + new[1], new[1], None if last else sg + 1)
                if last:
                    pe.wait_ge(sem("wmoe_in"), N_MOE_W * (l + 1))
                    for q in (2, 3):
                        prepare(l * NP_, q - 2, False, sg)
                        attend(4 * sg + q, q, n + T_LAST[q], T_LAST[q])
                    k = s_place(S_END, True)
                    project_out(sg, k, s_waited(sg, k))

            PREP_AT_PE = {2: 0, 4: 1, 8: 2, 10: 3, 11: 4, 12: 5, 13: 6, 14: 7, 15: 8}
            OWN_AT_PE = {0: 9, 1: 10}

            def prepare(pg, step, running=True, last_sg=None):
                if step == 0:
                    pe.wait_ge(sem("z2_ready"), 1 + pg + 1)
                    if not running:
                        pe.wait_ge(sem("s_free"), 1 + s_index(last_sg, s_place(S_HEAD[3] + 3, True)) + 1)
                    pe.wait_ge(sem("comb_bc_ready"), 1 + NE * pg - (1 if running else 0))
                    for t in range(4):
                        mm = T.transpose(psum[:, prep_bank(running, 0), t * P:(t + 1) * P], z2[:, t, :], ident)
                    mm.then_inc(sem("h2T_mm"), 1)
                if step == 1:
                    pe.wait_ge(sem("h2T_ready"), pg + 1)
                    pe.wait_ge(sem("comb_bc_ready"), 1 + NE * pg)
                    for t in range(4):
                        mm = T.matmul(psum[:, prep_bank(running, 1), t * NE:(t + 1) * NE], h2T[:, t * P:(t + 1) * P], wr,
                                      start=True, stop=True)
                    mm.then_inc(sem("logits_mm"), 1)
                if step == 2:
                    pe.wait_ge(sem("comb_ready"), pg + 1)
                    for t in range(4):
                        mm = T.transpose(psum[0:3 * NE, 6, t * 64:(t + 1) * 64].bitcast(BF16), comb_parts[:, t, :],
                                         ident_bf[:, :])
                    mm.then_inc(sem("combT_mm"), 1)
                if step >= 3:
                    e = step - 3
                    if e == 0:
                        pe.wait_ge(sem("combT_ready"), pg + 1)
                    else:
                        pe.wait_ge(sem("comb_bc_ready"), 1 + NE * pg + e - 1)
                    T.matmul(psum[:, 5 + e % 2, :], sel_exp[:, e * P:(e + 1) * P], combT[:, :],
                             start=True, stop=True).then_inc(sem("comb_bc_mm"), 1)

            def split_product(out, m, e, f, hi, lo, start, stop):
                T.matmul(out, expert_w(w_hi, m, e, f), hi, start=start, stop=False, skip_group_check=True)
                T.matmul(out, expert_w(w_hi, m, e, f), lo, start=False, stop=False, skip_group_check=True)
                return T.matmul(out, expert_w(w_lo, m, e, f), hi, start=False, stop=stop, skip_group_check=True)

            def down(pg, n):
                pe.wait_ge(sem("hh_lo_ready"), NU * pg + n + 1)
                if n == 0:
                    pe.wait_ge(sem("yT_copied"), 1 + pg)
                mm = split_product(psum[:, 4, :], 2, n // 2, n % 2, hh_hi[:, n % RING, :], hh_lo[:, n % RING, :],
                                   n == 0, n == NU - 1)
                if n == NU - 1:
                    mm.then_inc(sem("y_mm"), 1)
                if n == NU - 1 - RING:
                    mm.then_inc(sem("last_slot_free"), 1)

            def turn_y(pg):
                pe.wait_ge(sem("yT_copied"), 1 + pg + 1)
                pe.wait_ge(sem("y_added"), 1 + pg)
                for t in range(4):
                    mm = T.transpose(psum[:, 7, t * P:(t + 1) * P], yT[:, t * P:(t + 1) * P], ident)
                mm.then_inc(sem("y_tok_mm"), 1)

            def experts(pg, p, par, first, last):
                pe.wait_ge(sem("h2_lo_ready"), pg + 1)
                for n in range(NU):
                    e, f = n // 2, n % 2
                    if n >= 2 or not first:
                        pe.wait_ge(sem("gated_ready"), NU * pg + n - 1)
                    hi, lo = h2_hi[:, par, :], h2_lo[:, par, :]
                    split_product(psum[:, 2 * (n % 2), :], 0, e, f, hi, lo, True, True).then_inc(sem("gate_mm"), 1)
                    split_product(psum[:, 2 * (n % 2) + 1, :], 1, e, f, hi, lo, True, True).then_inc(sem("up_mm"), 1)
                    if n >= DOWN_LAG:
                        down(pg, n - DOWN_LAG)
                    elif not first:
                        down(pg - 1, NU - DOWN_LAG + n)
                    if n == DOWN_LAG + 1 and not first:
                        turn_y(pg - 1)
                    if n in OWN_AT_PE:
                        prepare(pg, OWN_AT_PE[n])
                    if not last and n in PREP_AT_PE:
                        prepare(pg + 1, PREP_AT_PE[n])
                if last:
                    for n in range(NU - DOWN_LAG, NU):
                        down(pg, n)
                    turn_y(pg)

            with pe.Fori(0, L) as l:
                phase_done(pe, 2 * l)
                pe.wait_ge(sem("wattn_in"), N_ATTN_W * (l + 1))
                s0 = l * B
                turn_h(s0, s0 * T_PER, T_FIRST - 1, False)
                pe.wait_ge(sem("wq_lo_ready"), l + 1)
                project_qk(s0, s0 * T_PER, s0 * S_PER, S_FIRST, True)
                turn_qk(s0, s0 * T_PER + 1, T_FIRST, True)
                pe.wait_ge(sem("k_zeroed"), l + 1)
                sequence(l, 0, True, False)
                middle_sequences(pe, lambda s: sequence(l, s, False, False))
                sequence(l, B - 1, False, True)
                phase_done(pe, 1 + 2 * l)
                pe.wait_ge(sem("wmoe_in"), N_MOE_W * (l + 1))
                for step in range(2, 9):
                    prepare(l * NP_, step, False)
                pe.wait_ge(sem("w_lo_ready"), 3 * B * (l + 1))
                all_pairs(pe, l, experts)

        @block.scalar
        def _(act):
            A = nc.scalar
            act.wait_ge(sem("pool_const"), 2)
            for name in ACT_FROM_ONE:
                A.copy(done_flags[:, 0:1], done_flags[:, 5:6]).then_inc(sem(name), 1)
                act.wait_ge(sem(name), 1)
            act.wait_ge(sem("c_in"), 16)
            A.activation(scT, cT, ACT.Silu).then_inc(sem("silu_c"), 1)
            def square(dst, src, n):
                for h in range(2):
                    act.wait_ge(sem("centred"), 2 * n + h + 1)
                    A.activation(dst[:, half(h), :], src[:, half(h), :], ACT.Square).then_inc(sem("squared"), 1)

            square(sq, xc_a, 0)
            act.wait_ge(sem("hp_zeroed"), 1)
            for b in range(B):
                act.wait_ge(sem("xcT_mm"), b + 1)
                A.activation(hp[:, b, 1:S + 1], psum[:, b % 2, 0:S], ACT.Identity, bias=modcol[:, 0, b:b + 1],
                             scale=modcol[:, 1, b:b + 1]).then_inc(sem("hp_ready"), 1)
            for b in range(B):
                act.wait_ge(sem("rowbc_mm"), b + 1)
                A.copy(row_bc[:, b, :], psum[:, 4 + b % 4, :]).then_inc(sem("rowbc_copied"), 1)
            for q in range(4):
                act.wait_ge(sem("rowbc_mm"), B + q + 1)
                A.copy(gb_rows[:, 4 * q:4 * q + 4, :].rearrange("p b c -> p (b c)"), psum[:, 4 + q, :]) \
                    .then_inc(sem("rowbc_copied"), 1)
            act.wait_ge(sem("qmin_ready"), 1)
            A.activation(rden, rden, ACT.Exp).then_inc(sem("qexp_ready"), 1)
            act.wait_ge(sem("qv_tok_mm"), 1)
            for h in range(2):
                A.copy(v_tok[:, 4 * h:4 * h + 4, :].rearrange("p a b -> p (a b)"), psum[:, 4 + h, :]) \
                    .then_inc(sem("v_tok_ready"), 1)
            for b in range(B):
                act.wait_ge(sem("yt_mm"), b + 1)
                A.copy(x[:, ST * b:ST * b + ST, :].rearrange("p a b -> p (a b)"),
                       psum[:, [0, 1, 6, 7][b % 4], 0:S]).then_inc(sem("yt_copied"), 1)
            square(sq2, x, 1)
            square(sq2, x, 2)
            A.copy(done_flags[:, 0:1], done_flags[:, 5:6]).then_inc(sem("phase_end"), 1)

            def exps(qg, q):
                act.wait_ge(sem("negmax_ready"), qg + 1)
                for k in range(8):
                    i, t = k // 2, k % 2
                    a = probs[:, q, i, 0:P] if t == 0 else probs[:, q, i, P:3 * P]
                    ins = A.activation(a, a, ACT.Exp, bias=negmax[:, q, k:k + 1], accum_out=rowsum[:, q, k:k + 1])
                ins.then_inc(sem("exp_done"), 1)

            def copy_probs(q, n, k):
                for i in range(4):
                    act.wait_ge(sem("t_full"), n + i + 1)
                    A.copy(probsT[:, 4 * (q % 2) + i, :], psum[:, t_bank(k + i), 0:3 * P]).then_inc(sem("t_free"), 1)

            def copy_h(n, k):
                act.wait_ge(sem("t_full"), n + 1)
                A.mul(h_hi, psum[:, t_bank(k), 0:S], lnw_now[:, 0:1])
                A.mul(hT, psum[:, t_bank(k), 0:S], lnw_now[:, 0:1]).then_inc(sem("t_free"), 1)

            def copy_raw(n, k):
                for u in range(5):
                    act.wait_ge(sem("s_full"), n + u + 1)
                    A.copy(qk_raw[:, u, :], psum[:, s_bank(k + u), :]).then_inc(sem("qk_copied"), 1)

            def copy_qk(n, k):
                for u in range(6):
                    act.wait_ge(sem("t_full"), n + u + 1)
                    src = psum[:, t_bank(k + u), :]
                    if u < 4:
                        ins = A.copy(QT[:, 2 * u:2 * u + 2, :].rearrange("p a b -> p (a b)"), src)
                    else:
                        ins = A.copy(KT[0:64, 0, 2 * (u - 4):2 * (u - 4) + 2, :].rearrange("p a b -> p (a b)"),
                                     src[0:64])
                    ins.then_inc(sem("t_free"), 1)

            def round_weights(l, s):
                act.wait_ge(sem("wmoe_in"), N_MOE_W * (l + 1))
                for m in range(3):
                    c = bass.ds(s * W_PIECE, W_PIECE)
                    A.copy(w_hi[m][:, c], w_all[m][:, c]).then_inc(sem("w_hi_ready"), 1)

            def sequence(l, s, first, last):
                sg = l * B + s
                n = t_index(sg, 0)
                new = T_LAST if last else T_NEW
                if not first:
                    copy_probs(2, n + T_OLD[2], T_OLD[2])
                exps(4 * sg, 0)
                if not first:
                    copy_probs(3, n + T_OLD[3], T_OLD[3])
                exps(4 * sg + 1, 1)
                if not last:
                    copy_h(n + T_H, T_H)
                round_weights(l, s)
                if not last:
                    copy_raw(s_index(sg, S_QK), S_QK)
                copy_probs(0, n + new[0], new[0])
                exps(4 * sg + 2, 2)
                if not last:
                    copy_qk(n + T_QK, T_QK)
                copy_probs(1, n + new[1], new[1])
                exps(4 * sg + 3, 3)
                if last:
                    prepare(l * NP_, 0, 0, False)
                    for q in (2, 3):
                        copy_probs(q, n + T_LAST[q], T_LAST[q])
                    prepare(l * NP_, 1, 0, False)

            PREP_AT_ACT = {3: 0, 5: 1, 11: 3, 12: 4, 13: 5, 14: 6, 15: 7}
            OWN_AT_ACT = {0: 8, 1: 9, 2: 10}

            def prepare(pg, step, par, running=True):
                if step == 0:
                    act.wait_ge(sem("h2T_mm"), pg + 1)
                    A.mul(h2_hi[:, par, :], psum[:, prep_bank(running, 0), :], lnw_now[:, 1:2])
                    A.mul(h2T, psum[:, prep_bank(running, 0), :], lnw_now[:, 1:2]).then_inc(sem("h2T_ready"), 1)
                if step == 1:
                    act.wait_ge(sem("gap_ready"), pg + 1)
                    A.activation(th, gap, ACT.Tanh, scale=0.5).then_inc(sem("tanh_ready"), 1)
                if step >= 3:
                    e = step - 3
                    act.wait_ge(sem("comb_bc_mm"), NE * pg + e + 1)
                    A.copy(comb_bc[:, par, e, :], psum[:, 5 + e % 2, :]).then_inc(sem("comb_bc_ready"), 1)

            def round_h(pg, n):
                act.wait_ge(sem("hh_ready"), NU * pg + n + 1)
                A.copy(hh_hi[:, n % RING, :], hh[:, n % RING, :]).then_inc(sem("hh_hi_ready"), 1)

            def copy_y(pg):
                act.wait_ge(sem("y_mm"), pg + 1)
                act.wait_ge(sem("y_added"), 1 + pg)
                A.copy(yT, psum[:, 4, :]).then_inc(sem("yT_copied"), 1)

            def experts(pg, p, par, first, last):
                for n in range(NU):
                    act.wait_ge(sem("gate_mm"), NU * pg + n + 1)
                    A.activation(silu_g[:, n % 2, :], psum[:, 2 * (n % 2), :], ACT.Silu) \
                        .then_inc(sem("silu_ready"), 1)
                    if n >= ROUND_LAG:
                        round_h(pg, n - ROUND_LAG)
                    elif not first:
                        round_h(pg - 1, NU - ROUND_LAG + n)
                    if n == DOWN_LAG - 1 and not first:
                        copy_y(pg - 1)
                    if n in OWN_AT_ACT:
                        prepare(pg, OWN_AT_ACT[n], par)
                    if not last and n in PREP_AT_ACT:
                        prepare(pg + 1, PREP_AT_ACT[n], 1 - par)
                if last:
                    for n in range(NU - ROUND_LAG, NU):
                        if n == NU - 1:
                            act.wait_ge(sem("last_slot_free"), pg + 1)
                        round_h(pg, n)
                    copy_y(pg)

            with act.Fori(0, L) as l:
                phase_done(act, 2 * l)
                s0 = l * B
                act.wait_ge(sem("wattn_in"), N_ATTN_W * (l + 1))
                A.copy(wq_hi, wq).then_inc(sem("wq_hi_ready"), 1)
                copy_h(s0 * T_PER, T_FIRST - 1)
                copy_raw(s0 * S_PER, S_FIRST)
                copy_qk(s0 * T_PER + 1, T_FIRST)
                sequence(l, 0, True, False)
                middle_sequences(act, lambda s: sequence(l, s, False, False))
                sequence(l, B - 1, False, True)
                A.copy(done_flags[:, 0:1], done_flags[:, 5:6]).then_inc(sem("phase_end"), 1)
                phase_done(act, 1 + 2 * l)
                for step in range(3, 8):
                    prepare(l * NP_, step, 0)
                all_pairs(act, l, experts)
                A.copy(done_flags[:, 0:1], done_flags[:, 5:6]).then_inc(sem("phase_end"), 1)

        @block.gpsimd
        def _(pool):
            G = nc.gpsimd
            G.dma_start(sel_exp[:, :], I["sel_exp"]).then_inc(sem("sel_exp_in"), 16)
            G.memset(minus_half, -0.5).then_inc(sem("pool_const"), 1)
            G.memset(done_flags[:, 5:8], 0.0).then_inc(sem("pool_const"), 1)
            pool.wait_ge(sem("pool_const"), 2)
            for name in POOL_FROM_ONE:
                G.memset(done_flags[:, 1:2], 0.0).then_inc(sem(name), 1)
                pool.wait_ge(sem(name), 1)
            for a, n in ((hp, S), (low1, S // 2), (high1, S // 2), (low2, S // 4), (high2, S // 4)):
                G.memset(a[:, :, 0:1], 0.0)
                ins = G.memset(a[:, :, n + 1:a.shape[-1]], 0.0)
            ins.then_inc(sem("hp_zeroed"), 1)
            for n in range(3):
                for h in range(2):
                    pool.wait_ge(sem("var_ready"), 2 * n + h + 1)
                    G.tensor_tensor(rstd0[:, half(h)], var[:, half(h)], minus_half[:, half(h)], ALU.pow) \
                        .then_inc(sem("rstd0_ready"), 1)
            pool.wait_ge(sem("sel_exp_in"), 16)
            G.memset(done_flags[:, 1:2], 0.0).then_inc(sem("phase_end"), 1)

            def load_x(sg, s):
                pool.wait_ge(sem("z_ready"), 1 + sg)
                G.tensor_tensor(done_flags[:, 6:7], done_flags[:, 7:8], done_flags[:, 7:8], ALU.add)
                G.tensor_copy(xs, x[:, bass.ds(s * ST, ST), :]).then_inc(sem("xs_ready"), 1)

            def root(sg):
                pool.wait_ge(sem("ms_ready"), sg + 1)
                G.tensor_tensor(rstd, ms, minus_half[:, 0:ST], ALU.pow).then_inc(sem("rstd_ready"), 1)

            def normalise(qg, q):
                pool.wait_ge(sem("rinv_ready"), qg + 1)
                r = rinv[:, q, :].rearrange("p (i t) -> p i t", t=2)
                for t in range(2):
                    a = probs[:, q, :, 0:P] if t == 0 else probs[:, q, :, P:3 * P]
                    ins = G.tensor_tensor(a, a, r[:, :, t:t + 1].broadcast_to([P, 4, P * (t + 1)]), ALU.mult)
                ins.then_inc(sem("probs_ready"), 1)

            def rope_adds(sg, n):
                for u in range(5):
                    pool.wait_ge(sem("s_free"), 1 + n + u + 1)
                    a, b = qk_raw[:, u, :], rope_b[:, u % 4, :]
                    if u < 4:
                        G.tensor_tensor(qr[:, u // 2, (u % 2) * 512:(u % 2 + 1) * 512], a, b, ALU.add) \
                            .then_inc(sem("rope_done"), 1)
                    else:
                        G.tensor_tensor(k_copy(0), as_heads(a), as_heads(b), ALU.add).then_inc(sem("rope_done"), 1)

            def sequence(l, s, first, last):
                sg = l * B + s
                if not last:
                    load_x(sg + 1, s + 1)
                if not first:
                    normalise(4 * sg - 1, 3)
                if not last:
                    root(sg + 1)
                normalise(4 * sg, 0)
                if last:
                    prepare(l * NP_, 0, 0)
                    prepare(l * NP_, 0, 1)
                normalise(4 * sg + 1, 1)
                if not last:
                    rope_adds(sg + 1, s_index(sg, S_QK))
                normalise(4 * sg + 2, 2)
                if last:
                    normalise(4 * sg + 3, 3)

            def prepare(pg, p, step):
                if step == 0:
                    pool.wait_ge(sem("z2_ready"), 1 + pg)
                    G.tensor_tensor(done_flags[:, 6:7], done_flags[:, 7:8], done_flags[:, 7:8], ALU.add)
                    G.tensor_copy(xs2, x[:, bass.ds(p * 4, 4), :]).then_inc(sem("xs2_ready"), 1)
                if step == 1:
                    pool.wait_ge(sem("ms2_ready"), pg + 1)
                    G.tensor_tensor(rstd2, ms2, minus_half[:, 0:4], ALU.pow).then_inc(sem("rstd2_ready"), 1)

            def experts(pg, p, par, first, last):
                for n in range(NU):
                    if n == 0 and not last:
                        prepare(pg + 1, p + 1, 0)
                    if n % 2 == 0:
                        pool.wait_ge(sem("comb_bc_ready"), 1 + NE * pg + n // 2 + 1)
                    pool.wait_ge(sem("gated_ready"), NU * pg + n + 1)
                    G.tensor_tensor(hh[:, n % RING, :], gated[:, n % RING, :], comb_bc[:, par, n // 2, :], ALU.mult) \
                        .then_inc(sem("hh_ready"), 1)
                    if not last and n == 0:
                        prepare(pg + 1, p + 1, 1)

            with pool.Fori(0, L) as l:
                phase_done(pool, 2 * l)
                pool.wait_ge(sem("small_in"), 32)
                for j in range(2):
                    ins = G.tensor_copy(lnw_now[:, j:j + 1], lnw[:, j, bass.ds(l, 1)])
                s0 = l * B
                load_x(s0, 0)
                root(s0)
                rope_adds(s0, s0 * S_PER)
                sequence(l, 0, True, False)
                middle_sequences(pool, lambda s: sequence(l, s, False, False))
                sequence(l, B - 1, False, True)
                G.memset(done_flags[:, 1:2], 0.0).then_inc(sem("phase_end"), 1)
                phase_done(pool, 1 + 2 * l)
                all_pairs(pool, l, experts)
                G.memset(done_flags[:, 1:2], 0.0).then_inc(sem("phase_end"), 1)

        @block.vector
        def _(dve):
            V = nc.vector

            class Steps:

                def __init__(self, base):
                    self.base, self.n = base, 0

                def __call__(self, ins):
                    ins.then_inc(sem("dve_step"), 1)
                    self.n += 1
                    dve.wait_ge(sem("dve_step"), self.base + self.n)

            step = Steps(0)
            D = S // 4
            for name in DVE_FROM_ONE:
                V.memset(done_flags[:, 2:3], 0.0).then_inc(sem(name), 1)
                dve.wait_ge(sem(name), 1)
            dve.wait_ge(sem("consts_in"), 16)
            step(V.tensor_copy(ident_bf[:, :], ident))
            def per_row(a):
                return a.rearrange("p (t a) -> p t a", a=1).broadcast_to([P, NT // 2, C])

            def centre(src, dst, n, wait_src):
                for h in range(2):
                    t = half(h)
                    wait_src(h)
                    step(V.tensor_reduce(mean[:, t], src[:, t, :], AX, ALU.add))
                    step(V.tensor_scalar(mean[:, t], mean[:, t], 1.0 / C, None, ALU.mult))
                    V.tensor_tensor(dst[:, t, :], src[:, t, :], per_row(mean[:, t]), ALU.subtract) \
                        .then_inc(sem("centred"), 1)

            def variance(squares, n):
                for h in range(2):
                    t = half(h)
                    dve.wait_ge(sem("squared"), 2 * n + h + 1)
                    step(V.tensor_reduce(var[:, t], squares[:, t, :], AX, ALU.add))
                    V.tensor_scalar(var[:, t], var[:, t], 1.0 / C, EPS, ALU.mult, ALU.add) \
                        .then_inc(sem("var_ready"), 1)

            def divide(a, n, h):
                dve.wait_ge(sem("rstd0_ready"), 2 * n + h + 1)
                return V.tensor_tensor(a[:, half(h), :], a[:, half(h), :], per_row(rstd0[:, half(h)]), ALU.mult)

            def modulation():
                dve.wait_ge(sem("mod_mm"), 1)
                dve.wait_ge(sem("rows_in"), 48)
                step(V.tensor_copy(modcol[:, 0, :], psum[:, 0, 0:B]))
                step(V.tensor_scalar(modcol[:, 1, :], psum[:, 0, B:2 * B], 1.0, None, ALU.add))
                rt = rtmp[0:B]
                rw = rows[0:B]
                for src, dst in ((0, rt[:, 2, :]), (3, rw[:, 4, :])):
                    g = psum[0:B, 1, src * C:(src + 1) * C]
                    step(V.tensor_copy(rt[:, 3, :], g))
                    step(V.scalar_tensor_tensor(rt[:, 0, :], rt[:, 3, :], -1.0, rt[:, 3, :], ALU.mult, ALU.max))
                    step(V.tensor_scalar(rt[:, 0, :], rt[:, 0, :], 0.25, None, ALU.max))
                    step(V.tensor_scalar(rt[:, 1, :], rt[:, 3, :], 0.0, 2.0, ALU.is_ge, ALU.mult))
                    step(V.scalar_tensor_tensor(dst, rt[:, 1, :], -1.0, rt[:, 0, :], ALU.add, ALU.mult))
                step(V.tensor_tensor(rw[:, 0, :], rt[:, 2, :], gamma_beta[0:B, 0, :], ALU.mult))
                step(V.tensor_tensor(rw[:, 1, :], rt[:, 2, :], gamma_beta[0:B, 1, :], ALU.mult))
                step(V.tensor_scalar(rw[:, 2, :], psum[0:B, 1, 2 * C:3 * C], 1.0, None, ALU.add))
                V.tensor_copy(rw[:, 3, :], psum[0:B, 1, C:2 * C]).then_inc(sem("rows_ready"), 1)
                V.memset(done_flags[:, 3:4], 0.0).then_inc(sem("mod_copied"), 1)
                dve.wait_ge(sem("mod_copied"), 1)
                dve.wait_ge(sem("rows_ready"), 1)

            centre(x1, xc_a, 0, lambda h: dve.wait_ge(sem("x_in"), 64))
            modulation()
            variance(sq, 0)
            for h in range(2):
                divide(xc_a, 0, h).then_inc(sem("xc_ready"), 1)
            dve.wait_ge(sem("filt_in"), 64)
            dve.wait_ge(sem("hp_ready"), B)
            dve.wait_ge(sem("hp_zeroed"), 1)

            def analyse(src, dst, f, n):
                for k in range(TAPS):
                    a = src[:, :, k:k + 2 * n - 1:2]
                    tap = filt[:, f, k:k + 1]
                    if k == 0:
                        step(V.tensor_scalar(dst, a, tap, None, ALU.mult))
                    else:
                        step(V.scalar_tensor_tensor(dst, a, tap, dst, ALU.mult, ALU.add))

            analyse(hp, low1[:, :, 1:1 + S // 2], 0, S // 2)
            analyse(hp, high1[:, :, 1:1 + S // 2], 1, S // 2)
            analyse(low1, low2[:, :, 1:1 + D], 0, D)
            analyse(low1, high2[:, :, 1:1 + D], 1, D)
            lc = low2[:, :, 1:1 + D]
            step(V.tensor_copy(syn_v.rearrange("p (b n) -> p b n", b=B), lc))
            V.tensor_scalar(rden, lc, 0.0, None, ALU.min).then_inc(sem("qmin_ready"), 1)
            dve.wait_ge(sem("qexp_ready"), 1)
            V.scalar_tensor_tensor(qf, lc, 0.0, rden, ALU.max, ALU.add).then_inc(sem("qf_ready"), 1)
            V.memset(done_flags[:, 3:4], 0.0).then_inc(sem("lowc_ready"), 1)
            dve.wait_ge(sem("qf_ready"), 1)
            step(V.tensor_reduce(zsum, qf, AX, ALU.add))
            dve.wait_ge(sem("qv_tok_mm"), 1)
            for h in range(2):
                step(V.tensor_copy(q_tok[:, 4 * h:4 * h + 4, :].rearrange("p a b -> p (a b)"), psum[:, 2 + h, :]))
            dve.wait_ge(sem("v_tok_ready"), 2)
            V.memset(done_flags[:, 3:4], 0.0).then_inc(sem("qv_tok_ready"), 1)
            bd4 = blockdiag.rearrange("p (a c) -> p a c", a=1).broadcast_to([P, 4, P])
            for g in range(4):
                zs = zsum[:, 4 * g:4 * g + 4].rearrange("p (b a) -> p b a", a=1).broadcast_to([P, 4, P])
                step(V.tensor_tensor(zmat[:, 4 * g:4 * g + 4, :], bd4, zs, ALU.mult))
            dve.wait_ge(sem("kv_mm"), 1)
            for g in range(4):
                bank, odd, b0 = [6, 7, 0, 1][g], g // 2, 8 * (g % 2)
                ins = V.tensor_tensor(kvm[:, b0 + odd:b0 + odd + 7:2, :],
                                      psum[:, bank, :].rearrange("p (a c) -> p a c", a=4), bd4, ALU.mult)
            ins.then_inc(sem("kvz_ready"), 1)
            dve.wait_ge(sem("numden_mm"), 1)
            for h in range(2):
                den = psum[:, 4 + h, :].rearrange("p (b n) -> p b n", b=8)
                num = psum[:, 2 + h, :].rearrange("p (b n) -> p b n", b=8)
                rd = rden[:, 8 * h:8 * h + 8, :]
                step(V.tensor_scalar(rd, den, ATTN_EPS, None, ALU.add))
                step(V.reciprocal(rd, rd))
                step(V.tensor_tensor(low2[:, 8 * h:8 * h + 8, 1:1 + D], num, rd, ALU.mult))
            for f in range(2):
                for j, (a, b) in enumerate(((1, 2), (0, 1), (2, 3))):
                    step(V.tensor_tensor(fsum[:, f, j:j + 1], filt[:, 2 + f, a:a + 1], filt[:, 2 + f, b:b + 1],
                                         ALU.add))

            def synthesise(low, high, dst, n, start):
                even, odd = dst[:, :, 0:2 * n - 1:2], dst[:, :, 1:2 * n:2]
                for f, src in enumerate((low, high)):
                    before, at, after = src[:, :, 0:n], src[:, :, 1:n + 1], src[:, :, 2:n + 2]
                    terms = (((before, filt[:, 2 + f, 0:1]), (at, fsum[:, f, 0:1]), (after, filt[:, 2 + f, 3:4])),
                             ((at, fsum[:, f, 1:2]), (after, fsum[:, f, 2:3])))
                    for o, ts in zip((even, odd), terms):
                        for k, (a, tap) in enumerate(ts):
                            if f == 0 and k == 0 and start is None:
                                step(V.tensor_scalar(o, a, tap, None, ALU.mult))
                            elif f == 0 and k == 0:
                                base = start[:, :, 0:2 * n - 1:2] if o is even else start[:, :, 1:2 * n:2]
                                step(V.scalar_tensor_tensor(o, a, tap, base, ALU.mult, ALU.add))
                            else:
                                step(V.scalar_tensor_tensor(o, a, tap, o, ALU.mult, ALU.add))

            synthesise(low2, high2, low1[:, :, 1:1 + S // 2], D, None)
            step(V.memset(low1[:, :, 0:1], 0.0))
            step(V.memset(low1[:, :, 1 + S // 2:4 + S // 2], 0.0))
            synthesise(low1, high1, syn, S // 2, hp[:, :, 1:S + 1])
            V.memset(done_flags[:, 3:4], 0.0).then_inc(sem("syn_ready"), 1)
            rb = row_bc.rearrange("p b (k c) -> p b k c", k=4)

            def by_row(k, h):
                return rb[:, h * B // 2:(h + 1) * B // 2, k:k + 1, :].broadcast_to([P, B // 2, ST, C])

            def seqs(a):
                return a.rearrange("p (b t) c -> p b t c", t=ST)

            def affine(n, k, h):
                xh = seqs(x)[:, h * B // 2:(h + 1) * B // 2]
                step(divide(x, n, h))
                step(V.tensor_tensor(xh, xh, by_row(k, h), ALU.mult))
                step(V.tensor_tensor(xh, xh, by_row(k + 1, h), ALU.add))

            dve.wait_ge(sem("rowbc_copied"), B + 4)
            centre(x, x, 1, lambda h: dve.wait_ge(sem("yt_copied"), (h + 1) * B // 2))
            variance(sq2, 1)
            for h in range(2):
                affine(1, 0, h)
                step(V.tensor_tensor(x1[:, half(h), :], x1[:, half(h), :], x[:, half(h), :], ALU.add))
            centre(x1, x, 2, lambda h: None)
            variance(sq2, 2)
            for h in range(2):
                affine(2, 2, h)
            V.memset(done_flags[:, 2:3], 0.0).then_inc(sem("phase_end"), 1)
            STEPS0 = step.n

            def mean_square(sg):
                dve.wait_ge(sem("xs_ready"), sg + 1)
                for t in range(ST):
                    ins = V.tensor_tensor_reduce(junk[:, t, :], xs[:, t, :], xs[:, t, :], 1.0 / C, EPS, ALU.mult, ALU.add,
                                                 ms[:, t:t + 1])
                ins.then_inc(sem("ms_ready"), 1)

            def scale_rows(sg):
                dve.wait_ge(sem("rstd_ready"), sg + 1)
                for t in range(ST):
                    ins = V.tensor_scalar(z[:, t, :], xs[:, t, :], rstd[:, t:t + 1], None, ALU.mult)
                ins.then_inc(sem("z_ready"), 1)

            def rope(sg, n):
                def turned_half(u):
                    parts = [(slice(0, 512), u // 2, 8)] if u < 4 else [(slice(0, 256), 0, 4), (slice(256, 512), 1, 4)]
                    hf = HD // 2
                    for sl, t, nh in parts:
                        src = qk_raw[:, u, sl].rearrange("p (h d) -> p h d", h=nh)
                        dst = rope_b[:, u % 4, sl].rearrange("p (h d) -> p h d", h=nh)
                        sin = consts[:, K_SIN + t * HD:K_SIN + (t + 1) * HD].rearrange("p (a d) -> p a d", a=1)
                        V.tensor_tensor(dst[:, :, 0:hf], src[:, :, hf:HD], sin[:, :, 0:hf].broadcast_to([P, nh, hf]),
                                        ALU.mult)
                        ins = V.tensor_tensor(dst[:, :, hf:HD], src[:, :, 0:hf],
                                              sin[:, :, hf:HD].broadcast_to([P, nh, hf]), ALU.mult)
                    ins.then_inc(sem("rope_turned"), 1)

                def own_part(u):
                    dve.wait_ge(sem("rope_turned"), 5 * sg + u + 1)
                    parts = [(slice(0, 512), u // 2, 8)] if u < 4 else [(slice(0, 256), 0, 4), (slice(256, 512), 1, 4)]
                    for sl, t, nh in parts:
                        src = qk_raw[:, u, sl].rearrange("p (h d) -> p h d", h=nh)
                        cos = consts[:, K_COS + t * HD:K_COS + (t + 1) * HD].rearrange("p (a d) -> p a d", a=1)
                        ins = V.tensor_tensor(src, src, cos.broadcast_to([P, nh, HD]), ALU.mult)
                    ins.then_inc(sem("s_free"), 1)

                for u in range(5):
                    dve.wait_ge(sem("qk_copied"), 5 * sg + u + 1)
                    dve.wait_ge(sem("rope_done"), 1 + 5 * sg + max(u - 3, 0))
                    turned_half(u)
                    if u >= 1:
                        own_part(u - 1)
                own_part(4)
                dve.wait_ge(sem("s_free"), 1 + n + 5)
                V.tensor_tensor(k_copy(1), as_heads(qk_raw[:, 4, :]), as_heads(rope_b[:, 0, :]), ALU.add) \
                    .then_inc(sem("k_copy_ready"), 1)

            def low_h_rows(sg, n):
                dve.wait_ge(sem("t_free"), 1 + n + 1)
                V.tensor_tensor(h_lo, hT, h_hi.bitcast(F32), ALU.subtract).then_inc(sem("h_lo_ready"), 1)

            def copy_v(n):
                dve.wait_ge(sem("s_full"), n + 1)
                V.tensor_copy(v.rearrange("p t c -> p (t c)"), psum[:, s_bank(S_V), :]).then_inc(sem("s_free"), 1)

            def mask_and_max(sg, q, first, last):
                for i in range(4):
                    k = s_place(S_HEAD[q] + i, last)
                    n = s_index(sg, k, first)
                    dve.wait_ge(sem("s_full"), n + 1)
                    V.memset(done_flags[:, 8 + i:9 + i], 0.0)
                    V.tensor_tensor_reduce(probs[:, q, i, 0:P], psum[:, s_bank(k), 0:P], mask[:, P:2 * P],
                                           SCALE, -3.0e38, ALU.add, ALU.max, rowmax[:, q, 2 * i:2 * i + 1])
                    V.tensor_tensor_reduce(probs[:, q, i, P:3 * P], psum[:, s_bank(k), P:3 * P], mask,
                                           SCALE, -3.0e38, ALU.add, ALU.max,
                                           rowmax[:, q, 2 * i + 1:2 * i + 2]).then_inc(sem("s_free"), 1)
                dve.wait_ge(sem("s_free"), 1 + n + 1)
                V.tensor_scalar(negmax[:, q, :], rowmax[:, q, :], -1.0, None, ALU.mult) \
                    .then_inc(sem("negmax_ready"), 1)

            def invert(qg, q):
                dve.wait_ge(sem("exp_done"), qg + 1)
                V.reciprocal(rinv[:, q, :], rowsum[:, q, :]).then_inc(sem("rinv_ready"), 1)

            def copy_o(qg, q):
                dve.wait_ge(sem("o_full"), qg + 1)
                V.tensor_copy(oT[:, 2 * q:2 * q + 2, :].rearrange("p a b -> p (a b)"), psum[:, O_BANK, :]) \
                    .then_inc(sem("o_free"), 1)

            def update_x(sg, s, k, n):
                dve.wait_ge(sem("s_full"), n + 1)
                xv = x[:, bass.ds(s * ST, ST), :]
                V.tensor_tensor(xv, xv, psum[:, s_bank(k), 0:S].rearrange("p (t c) -> p t c", t=ST), ALU.add) \
                    .then_inc(sem("s_free"), 1)
                dve.wait_ge(sem("s_free"), 1 + n + 1)
                V.tensor_scalar(xv, xv, 100.0, -100.0, ALU.min, ALU.max)

            def copy_k_odd(sg, n, k):
                for u in (4, 5):
                    dve.wait_ge(sem("t_full"), n + u + 1)
                    V.tensor_copy(KT[64:P, 1, 2 * (u - 4):2 * (u - 4) + 2, :].rearrange("p a b -> p (a b)"),
                                  psum[64:P, t_bank(k + u), :]).then_inc(sem("k_odd_copied"), 1)

            def low_weights(sg, s):
                for m in range(3):
                    dve.wait_ge(sem("w_hi_ready"), 3 * sg + m + 1)
                    c = bass.ds(s * W_PIECE, W_PIECE)
                    V.tensor_tensor(w_lo[m][:, c], w_all[m][:, c], w_hi[m][:, c].bitcast(F32), ALU.subtract) \
                        .then_inc(sem("w_lo_ready"), 1)

            def sequence(l, s, first, last):
                sg = l * B + s
                mask_and_max(sg, 0, first, last)
                if not first:
                    invert(4 * sg - 1, 3)
                    copy_o(4 * sg - 2, 2)
                if not last:
                    mean_square(sg + 1)
                mask_and_max(sg, 1, first, last)
                invert(4 * sg, 0)
                if not last:
                    scale_rows(sg + 1)
                if not first:
                    copy_o(4 * sg - 1, 3)
                copy_v(s_index(sg, S_V, first))
                invert(4 * sg + 1, 1)
                if not first:
                    update_x(sg - 1, s - 1, S_OUT, s_index(sg, S_OUT))
                if not last:
                    low_h_rows(sg + 1, t_index(sg, T_H))
                else:
                    prepare(l * NP_, 0, 0)
                mask_and_max(sg, 2, first, last)
                if last:
                    prepare(l * NP_, 1, 0)
                if not last:
                    rope(sg + 1, s_index(sg, S_QK))
                copy_o(4 * sg, 0)
                mask_and_max(sg, 3, first, last)
                invert(4 * sg + 2, 2)
                if not last:
                    copy_k_odd(sg + 1, t_index(sg, T_QK), T_QK)
                low_weights(sg, s)
                copy_o(4 * sg + 1, 1)
                if last:
                    invert(4 * sg + 3, 3)
                    copy_o(4 * sg + 2, 2)
                    prepare(l * NP_, 5, 0)
                    prepare(l * NP_, 2, 0, False)
                    copy_o(4 * sg + 3, 3)
                    k = s_place(S_END, True)
                    update_x(sg, s, k, s_index(sg, k))
                    prepare(l * NP_, 3, 0)

            PREP_STEPS = 15

            def prepare(pg, part, par, running=True):
                st = Steps(STEPS0 + pg * PREP_STEPS)
                if part == 0:
                    dve.wait_ge(sem("xs2_ready"), pg + 1)
                    for t in range(4):
                        ins = V.tensor_tensor_reduce(junk2[:, t, :], xs2[:, t, :], xs2[:, t, :], 1.0 / C, EPS,
                                                     ALU.mult, ALU.add, ms2[:, t:t + 1])
                    ins.then_inc(sem("ms2_ready"), 1)
                    return
                if part == 1:
                    dve.wait_ge(sem("rstd2_ready"), pg + 1)
                    for t in range(4):
                        ins = V.tensor_scalar(z2[:, t, :], xs2[:, t, :], rstd2[:, t:t + 1], None, ALU.mult)
                    ins.then_inc(sem("z2_ready"), 1)
                    return
                if part == 2:
                    dve.wait_ge(sem("logits_mm"), pg + 1)
                    st(V.tensor_copy(logits.rearrange("p a b -> p (a b)"), psum[:, prep_bank(running, 1), 0:4 * NE]))
                    V.memset(done_flags[:, 4:5], 0.0)
                    for t in range(4):
                        ins = V.max(max8[:, t, :], logits[:, t, :])
                    st(ins)
                    V.tensor_tensor(gap.rearrange("p (t a) -> p t a", a=1), max8[:, :, 0:1], max8[:, :, 1:2],
                                    ALU.subtract).then_inc(sem("gap_ready"), 1)
                    for t in range(4):
                        ins = V.max_index(idx8[:, t, :].bitcast(U32), max8[:, t, :], logits[:, t, :])
                    st(ins)
                    st(V.tensor_copy(idxf, idx8[:, :, 0:2].bitcast(U32)))
                    io = iota8.rearrange("p (a e) -> p a e", a=1).broadcast_to([P, 4, NE])
                    for j in range(2):
                        st(V.tensor_tensor(pick[:, j], io, idxf[:, :, j:j + 1].broadcast_to([P, 4, NE]), ALU.is_equal))
                    return
                if part == 5:
                    dve.wait_ge(sem("h2T_ready"), pg + 1)
                    V.tensor_tensor(h2_lo[:, par, :], h2T, h2_hi[:, par, :].bitcast(F32), ALU.subtract) \
                        .then_inc(sem("h2_lo_ready"), 1)
                    return
                if part == 4:
                    dve.wait_ge(sem("combT_mm"), pg + 1)
                    V.tensor_copy(combT[:, :], psum[0:3 * NE, 6, 0:256].bitcast(BF16)).then_inc(sem("combT_ready"), 1)
                    return
                st.n = 6
                dve.wait_ge(sem("tanh_ready"), pg + 1)
                st(V.tensor_scalar(c12[:, 0, :], th, 0.5, 0.5, ALU.mult, ALU.add))
                st(V.tensor_scalar(c12[:, 1, :], th, -0.5, 0.5, ALU.mult, ALU.add))
                for j in range(2):
                    cj = c12[:, j, :].rearrange("p (t a) -> p t a", a=1).broadcast_to([P, 4, NE])
                    st(V.tensor_tensor(pick[:, j], pick[:, j], cj, ALU.mult))
                st(V.tensor_tensor(comb, pick[:, 0], pick[:, 1], ALU.add))
                st(V.tensor_copy(comb_parts[:, :, 0:NE], comb))
                st(V.tensor_tensor(rest, comb, comb_parts[:, :, 0:NE], ALU.subtract))
                st(V.tensor_copy(comb_parts[:, :, NE:2 * NE], rest))
                st(V.tensor_tensor(rest, rest, comb_parts[:, :, NE:2 * NE], ALU.subtract))
                V.tensor_copy(comb_parts[:, :, 2 * NE:3 * NE], rest).then_inc(sem("comb_ready"), 1)
                assert st.n == PREP_STEPS, st.n

            def low_h(pg, n):
                dve.wait_ge(sem("hh_hi_ready"), NU * pg + n + 1)
                V.tensor_tensor(hh_lo[:, n % RING, :], hh[:, n % RING, :], hh_hi[:, n % RING, :].bitcast(F32),
                                ALU.subtract).then_inc(sem("hh_lo_ready"), 1)

            def add_y(pg, p):
                dve.wait_ge(sem("y_tok_mm"), pg + 1)
                xv = x[:, bass.ds(p * 4, 4), :]
                V.tensor_tensor(xv, xv, psum[:, 7, :].rearrange("p (t c) -> p t c", t=4), ALU.add) \
                    .then_inc(sem("y_added"), 1)
                dve.wait_ge(sem("y_added"), 1 + pg + 1)
                V.tensor_scalar(xv, xv, 100.0, -100.0, ALU.min, ALU.max).then_inc(sem("x2_updated"), 1)

            PREP_AT_DVE = {0: 0, 1: 1, 4: 5, 5: 2, 6: 3, 9: 4}

            def experts(pg, p, par, first, last):
                for n in range(NU):
                    dve.wait_ge(sem("silu_ready"), NU * pg + n + 1)
                    dve.wait_ge(sem("up_mm"), NU * pg + n + 1)
                    V.tensor_tensor(gated[:, n % RING, :], silu_g[:, n % 2, :], psum[:, 2 * (n % 2) + 1, :],
                                    ALU.mult).then_inc(sem("gated_ready"), 1)
                    if n >= ROUND_LAG:
                        low_h(pg, n - ROUND_LAG)
                    elif not first:
                        low_h(pg - 1, NU - ROUND_LAG + n)
                    if n == DOWN_LAG + 3 and not first:
                        add_y(pg - 1, p - 1)
                    if not last and n in PREP_AT_DVE:
                        prepare(pg + 1, PREP_AT_DVE[n], 1 - par)
                if last:
                    for n in range(NU - ROUND_LAG, NU):
                        low_h(pg, n)
                    add_y(pg, p)

            with dve.Fori(0, L) as l:
                phase_done(dve, 2 * l)
                s0 = l * B
                mean_square(s0)
                scale_rows(s0)
                dve.wait_ge(sem("wq_hi_ready"), l + 1)
                V.tensor_tensor(wq_lo, wq, wq_hi.bitcast(F32), ALU.subtract).then_inc(sem("wq_lo_ready"), 1)
                low_h_rows(s0, s0 * T_PER)
                V.memset(KT[64:P, 0], 0.0)
                V.memset(KT[0:64, 1], 0.0).then_inc(sem("k_zeroed"), 1)
                rope(s0, s0 * S_PER)
                copy_k_odd(s0, s0 * T_PER + 1, T_FIRST)
                sequence(l, 0, True, False)
                middle_sequences(dve, lambda s: sequence(l, s, False, False))
                sequence(l, B - 1, False, True)
                V.memset(done_flags[:, 2:3], 0.0).then_inc(sem("phase_end"), 1)
                phase_done(dve, 1 + 2 * l)
                prepare(l * NP_, 4, 0)
                all_pairs(dve, l, experts)
                V.memset(done_flags[:, 2:3], 0.0).then_inc(sem("phase_end"), 1)
            dve.wait_ge(sem("x2_updated"), L * NP_)
            NQ = B // 4
            for q in range(4):
                xq = seqs(x)[:, q * NQ:(q + 1) * NQ]
                gq = gb_rows[:, q * NQ:(q + 1) * NQ, :].rearrange("p b (a c) -> p b a c", a=1)
                V.tensor_tensor(xq, xq, gq.broadcast_to([P, NQ, ST, C]), ALU.mult).then_inc(sem("out_gated"), 1)
                dve.wait_ge(sem("out_gated"), q + 1)
                V.tensor_tensor(seqs(x1)[:, q * NQ:(q + 1) * NQ], seqs(x1)[:, q * NQ:(q + 1) * NQ], xq, ALU.add) \
                    .then_inc(sem("out_ready"), 1)


def kernel(**inputs):
    import concourse.bacc as _bacc
    from concourse.bass_utils import run_bass_kernel_spmd as _run

    nc = _bacc.Bacc("TRN2", target_bir_lowering=False, num_devices=1)
    k, sel_seq, sel_exp = shape_constants()
    given = {n: inputs[n] for n in ("L0_attn_x", "L0_wmod", "L0_attn_norm_gamma", "L0_attn_norm_beta", "L0_ffn_wq",
                                    "L0_ffn_wk", "L0_ffn_wv", "L0_ffn_wo", "L0_ffn_wr", "L0_ffn_wg", "L0_ffn_wu",
                                    "L0_ffn_wd")}
    given["cT"] = np.asarray(inputs["L0_c"]).T
    for n in ("h_filter", "g_filter", "h_synth", "g_synth"):
        given[n + "_T"] = np.asarray(inputs["L0_attn_" + n]).T
    given["ln1_T"] = np.asarray(inputs["L0_ffn_ln1_w"]).T
    given["ln2_T"] = np.asarray(inputs["L0_ffn_ln2_w"]).T
    given.update(consts=k, sel_seq=sel_seq, sel_exp=sel_exp)
    arrays, aps = {}, {}
    for n, a in given.items():
        a = np.ascontiguousarray(a)
        arrays["in_" + n] = a
        aps[n] = nc.dram_tensor("in_" + n, a.shape, mybir.dt.from_np(a.dtype), kind="ExternalInput").ap()
    out = nc.dram_tensor("out_0", (B, S, C), F32, kind="ExternalOutput").ap()
    bass_program(nc, aps, out)
    r = _run(nc, [arrays], core_ids=[0])
    return r.results[0]["out_0"]
```
